# Optimizing a Trainium2 kernel written in Bass

```python
import numpy as np
import jax
import jax.numpy as jnp

def _softmax(x, axis=-1):
    return jax.nn.softmax(x, axis=axis)
def _gelu(x):
    return jax.nn.gelu(x, approximate=True)
def _silu(x):
    return jax.nn.silu(x)
def _sigmoid(x):
    return jax.nn.sigmoid(x)
def _layernorm(x, axis=-1, eps=1e-5):
    m = jnp.mean(x, axis=axis, keepdims=True)
    v = jnp.var(x, axis=axis, keepdims=True)
    return (x - m) / jnp.sqrt(v + eps)
def _scatter_add(tgt, idx, src, axis=0):
    return tgt.at[idx].add(src)
def _segment_sum(src, seg, n):
    return jax.ops.segment_sum(src, seg, n)

kernel_name = 'mk_metaformer_d1_conv_nchw1024_568e23'

def setup_inputs(seed: int = 0):
    np.random.seed(seed)
    _w = jnp.asarray
    def _rec_inputs():
        import jax
        import jax.numpy as jnp
        _gk = jax.random.key(seed)
        x = -0.0005963 + 1.001 * jax.random.normal(jax.random.fold_in(_gk, 1), (16, 1024, 12, 16), jnp.float32)
        return x
    x = _rec_inputs()
    def _L0_conv_setup():
        import jax, jax.numpy as jnp
        import numpy as np
        B, N, T, F, K = (16, 1024, 12, 16, 3)
        key = jax.random.key(seed)
        ks = jax.random.split(key, 14)
        u = lambda k, shp: jax.random.uniform(k, shp, dtype=jnp.float32)
        x = jax.random.normal(ks[0], (B, N, T, F), dtype=jnp.float32)
        cheb = jax.random.normal(ks[1], (K, N, N), dtype=jnp.float32) * (1.0 / np.sqrt(N))
        return {'x': x, 't': 0, 'cheb': cheb, 'W1': u(ks[2], (T,)), 'W2': u(ks[3], (F, T)), 'W3': u(ks[4], (F,)), 'bs': u(ks[5], (1, N, N)), 'Vs': u(ks[6], (N, N)), 'U1': u(ks[7], (N,)), 'U2': u(ks[8], (F, N)), 'U3': u(ks[9], (F,)), 'be': u(ks[10], (1, T, T)), 'Ve': u(ks[11], (T, T)), 'Theta': u(ks[12], (K, F, F))}
    _L0_conv_all = _L0_conv_setup()
    _L0_conv_in = {k: v for k, v in _L0_conv_all.items() if k in ('cheb', 'W1', 'W2', 'W3', 'bs', 'Vs', 'U1', 'U2', 'U3', 'be', 'Ve', 'Theta', )}
    del _L0_conv_all

    def _L0_ffn_setup():
        import jax, jax.numpy as jnp
        import numpy as np
        B, S, D, E, R, TOP_K = (4, 4096, 1024, 10, 4, 2)
        SCALING = 1.0 / R
        key = jax.random.key(seed)
        ks = jax.random.split(key, 7)
        return {'x': jax.random.normal(ks[0], (B, S, D), dtype=jnp.float32), 'W_base': jax.random.normal(ks[1], (D, D), dtype=jnp.float32) * D ** (-0.5), 'b_base': jax.random.normal(ks[2], (D,), dtype=jnp.float32) * 0.02, 'gate_W': jax.random.normal(ks[3], (E, D), dtype=jnp.float32) * D ** (-0.5), 'gate_b': jax.random.normal(ks[4], (E,), dtype=jnp.float32) * 0.02, 'lora_down': jax.random.normal(ks[5], (E, R, D), dtype=jnp.float32) * D ** (-0.5), 'lora_up': jax.random.normal(ks[6], (E, D, R), dtype=jnp.float32) * R ** (-0.5)}
    _L0_ffn_all = _L0_ffn_setup()
    _L0_ffn_in = {k: v for k, v in _L0_ffn_all.items() if k in ('W_base', 'b_base', 'gate_W', 'gate_b', 'lora_down', 'lora_up', )}
    del _L0_ffn_all

    return {
        "x": x,
        "L0_conv_cheb": _L0_conv_in["cheb"],
        "L0_conv_W1": _L0_conv_in["W1"],
        "L0_conv_W2": _L0_conv_in["W2"],
        "L0_conv_W3": _L0_conv_in["W3"],
        "L0_conv_bs": _L0_conv_in["bs"],
        "L0_conv_Vs": _L0_conv_in["Vs"],
        "L0_conv_U1": _L0_conv_in["U1"],
        "L0_conv_U2": _L0_conv_in["U2"],
        "L0_conv_U3": _L0_conv_in["U3"],
        "L0_conv_be": _L0_conv_in["be"],
        "L0_conv_Ve": _L0_conv_in["Ve"],
        "L0_conv_Theta": _L0_conv_in["Theta"],
        "L0_ffn_W_base": _L0_ffn_in["W_base"],
        "L0_ffn_b_base": _L0_ffn_in["b_base"],
        "L0_ffn_gate_W": _L0_ffn_in["gate_W"],
        "L0_ffn_gate_b": _L0_ffn_in["gate_b"],
        "L0_ffn_lora_down": _L0_ffn_in["lora_down"],
        "L0_ffn_lora_up": _L0_ffn_in["lora_up"],
    }

def reference(x, L0_conv_cheb, L0_conv_W1, L0_conv_W2, L0_conv_W3, L0_conv_bs, L0_conv_Vs, L0_conv_U1, L0_conv_U2, L0_conv_U3, L0_conv_be, L0_conv_Ve, L0_conv_Theta, L0_ffn_W_base, L0_ffn_b_base, L0_ffn_gate_W, L0_ffn_gate_b, L0_ffn_lora_down, L0_ffn_lora_up):
    import jax
    import jax.numpy as jnp
    def _L0_conv_ref(x, t, cheb, W1, W2, W3, bs, Vs, U1, U2, U3, be, Ve, Theta):
        import jax, jax.numpy as jnp
        import numpy as np
        B, N, T, F, K = (16, 1024, 12, 16, 3)
        xp = jnp.transpose(x, (0, 1, 3, 2))
        lhs_t = jnp.einsum('bnft,n->btf', xp, U1) @ U2
        rhs_t = jnp.einsum('f,bnft->bnt', U3, xp)
        prod_t = jnp.einsum('btn,bnu->btu', lhs_t, rhs_t)
        E = jnp.einsum('tu,buv->btv', Ve, jax.nn.sigmoid(prod_t + be))
        E = jax.nn.softmax(E, axis=1)
        x_tat = jnp.einsum('bnft,btu->bnfu', xp, E)
        lhs_s = jnp.einsum('bnft,t->bnf', x_tat, W1) @ W2
        rhs_s = jnp.einsum('f,bnft->btn', W3, x_tat)
        prod_s = jnp.einsum('bnt,btm->bnm', lhs_s, rhs_s)
        S = jnp.einsum('nm,bmv->bnv', Vs, jax.nn.sigmoid(prod_s + bs))
        S = jax.nn.softmax(S, axis=1)
        rhs_c = jnp.einsum('kij,bij,bift->kbjft', cheb, S, x_tat)
        out = jax.nn.relu(jnp.einsum('kbjft,kfo->bjot', rhs_c, Theta))
        return jnp.transpose(out, (0, 1, 3, 2))

    def _L0_ffn_ref(x, W_base, b_base, gate_W, gate_b, lora_down, lora_up):
        import jax, jax.numpy as jnp
        import numpy as np
        B, S, D, E, R, TOP_K = (4, 4096, 1024, 10, 4, 2)
        SCALING = 1.0 / R
        base_out = jnp.einsum('bsd,od->bso', x, W_base) + b_base
        logits = jnp.einsum('bsd,ed->bse', x, gate_W) + gate_b
        top_vals, top_idx = jax.lax.top_k(logits, TOP_K)
        top_w = jax.nn.softmax(top_vals, axis=-1)
        weights = jnp.sum(top_w[..., None] * jax.nn.one_hot(top_idx, E, dtype=x.dtype), axis=-2)
        h = jnp.einsum('bsd,erd->bser', x, lora_down)
        h = h * weights[..., None]
        lora_out = jnp.einsum('bser,edr->bsd', h, lora_up) * SCALING
        return base_out + lora_out

    def _gn(v, G=32, eps=1e-5):
        B_, C_, H_, W_ = v.shape
        g = v.reshape(B_, G, C_ // G, H_, W_)
        m = jnp.mean(g, axis=(2, 3, 4), keepdims=True)
        s = jnp.var(g, axis=(2, 3, 4), keepdims=True)
        return ((g - m) / jnp.sqrt(s + eps)).reshape(v.shape)

    def _ln_c(v, eps=1e-6):
        m = jnp.mean(v, axis=1, keepdims=True)
        s = jnp.var(v, axis=1, keepdims=True)
        return (v - m) / jnp.sqrt(s + eps)

    def _ln_t(v, eps=1e-5):
        m = jnp.mean(v, axis=-1, keepdims=True)
        s = jnp.var(v, axis=-1, keepdims=True)
        return (v - m) / jnp.sqrt(s + eps)

    def _to_tokens(v):
        B_, C_, H_, W_ = v.shape
        return v.reshape(B_, C_, H_ * W_).transpose(0, 2, 1)
    def _from_tokens(t, like):
        B_, C_, H_, W_ = like.shape
        return t.transpose(0, 2, 1).reshape(B_, C_, H_, W_)

    x = x + _L0_conv_ref(_ln_c(x), 0, L0_conv_cheb, L0_conv_W1, L0_conv_W2, L0_conv_W3, L0_conv_bs, L0_conv_Vs, L0_conv_U1, L0_conv_U2, L0_conv_U3, L0_conv_be, L0_conv_Ve, L0_conv_Theta)
    t = _to_tokens(x)
    t = t + _L0_ffn_ref(_ln_t(t), L0_ffn_W_base, L0_ffn_b_base, L0_ffn_gate_W, L0_ffn_gate_b, L0_ffn_lora_down, L0_ffn_lora_up)
    x = _from_tokens(t, x)
    return x


_drawn_inputs = setup_inputs


def setup_inputs(seed=0):
    import zlib

    import numpy as np

    out = dict(_drawn_inputs(seed))
    spreads = {}
    factors = {'L0_conv_cheb': 2.684,
     'L0_conv_W1': 6.865,
     'L0_conv_W2': 4.019,
     'L0_conv_W3': 3.633,
     'L0_conv_bs': 23.052,
     'L0_conv_U1': 3.38,
     'L0_conv_U2': 3.192,
     'L0_conv_U3': 3.915,
     'L0_conv_be': 64.0,
     'L0_conv_Ve': 2.707,
     'L0_conv_Theta': 4.501,
     'L0_ffn_b_base': 3.974,
     'L0_ffn_gate_b': 4.118}
    for name, (base, spread) in spreads.items():
        noise = np.random.default_rng([zlib.crc32(name.encode()), seed]).standard_normal(out[name].shape)
        drawn = base * np.exp(spread * noise) if base else spread * noise
        out[name] = jnp.asarray(drawn.astype(out[name].dtype))
    for name, factor in factors.items():
        out[name] = (out[name] * factor).astype(out[name].dtype)
    return out
```

```python
import concourse.bass as bass
from concourse import mybir
from contextlib import ExitStack

B, N, T, F, K = 16, 1024, 12, 16, 3
P = 128
NT = N // P
C = T * F
HC = C // 2
HT = T // 2
KC = K * C
EXP, RANK = 10, 4
GC = EXP + EXP * RANK
GP = 64
PAIRS = B // 2
TOK = 2 * C
TG = TOK // HC

X_UP, K_UP = 256.0, 256.0
Y_UP = 32.0
V_UP, SIG_UP = 4096.0, 16384.0
CH_UP = 8192.0
W_UP, Z_UP = 4096.0, 256.0


def metaformer_program(nc, a, out):
    f32, f16, i32, u32 = mybir.dt.float32, mybir.dt.float16, mybir.dt.int32, mybir.dt.uint32
    ALU, ACT, AX = mybir.AluOpType, mybir.ActivationFunctionType, mybir.AxisListType
    ABSMAX = bass.bass_isa.ReduceOp.absmax

    def wait(eng, sem, value):
        if not (isinstance(value, int) and value <= 0):
            eng.wait_ge(sem, value)

    y_d = nc.dram_tensor("y_scratch", (B, P, NT, 2, KC), f16).ap()
    lr_d = nc.dram_tensor("lr_scratch", (B, 48, 2, N), f16).ap()
    x2_d = nc.dram_tensor("x2_scratch", (B, N, C), f32).ap()
    x_b = a["x"].rearrange("b (t p) h w -> b p t (h w)", p=P)
    x2_b = x2_d.rearrange("b (t p) c -> b p t c", p=P)
    out_b = out.rearrange("b (t p) h w -> b p t (h w)", p=P)

    root = ExitStack()
    with root:
        def make(stack):
            def sb(name, shape, dt=f32):
                return stack.enter_context(nc.sbuf_tensor(name, shape, dt))

            def ps(name, shape, dt=f32):
                return stack.enter_context(nc.psum_tensor(name, shape, dt))

            def sem(name):
                return stack.enter_context(nc.semaphore(name))
            return sb, ps, sem

        def newton_rsqrt(dve, var, v, bits, guess, half, chain, base, eps):
            k = [base]

            def link(ins):
                k[0] = k[0] + 1
                ins.then_inc(chain, 1)
                dve.wait_ge(chain, k[0])

            link(nc.vector.tensor_scalar(v, var, eps, None, ALU.add))
            link(nc.vector.tensor_scalar(bits.bitcast(u32), v.bitcast(u32), 1, None, ALU.logical_shift_right))
            link(nc.vector.tensor_scalar(guess.bitcast(i32), bits.bitcast(i32), -1.0, 1597463007.0, ALU.mult, ALU.add))
            for _ in range(3):
                link(nc.vector.scalar_tensor_tensor(half, guess, -0.5, guess, ALU.mult, ALU.mult))
                link(nc.vector.tensor_tensor(half, half, v, ALU.mult))
                link(nc.vector.scalar_tensor_tensor(guess, half, 1.5, guess, ALU.add, ALU.mult))

        NEWTON = 12

        rsb, rps, rsem = make(root)
        ones = rsb("ones_over_n", [P, P])
        ident = rsb("ident", [P, P])
        p2 = rsb("p2", [P, 8])
        rp2 = rsb("rp2", [P, 8])
        fac = rsb("fac", [P, 8])
        s_rootc = rsem("s_rootc")
        VS, CHEB, THETA, W1, W2, W3 = range(6)

        mid = ExitStack()
        with mid:
            msb, mps, msem = make(mid)
            cheb = msb("cheb", [P, K, NT, N])
            vt = msb("vt_split", [P, 2, NT, N], f16)

            with ExitStack() as st:
                sb, ps, sem = make(st)
                vstage = sb("vstage", [P, 1, N])
                amax = sb("amax", [P, 8])
                vmax = sb("vmax", [P, NT + K])
                am_all = sb("am_all", [P, 8])
                ua = sb("ua", [P, NT, 48])
                m48 = sb("m48", [48, C])
                thr = sb("thr", [HC, K, F])
                w2r = sb("w2r", [HC, 48])
                w3r = sb("w3r", [HC, 1])
                iw = sb("iw", [T, 16])
                be = sb("be", [T, T])
                vet = sb("vet", [T, T])
                lrm = sb("lrm", [P, 1])
                xf = sb("xf", [P, NT, C])
                sq = sb("sq", [P, NT, C])
                xn = sb("xn", [P, NT, C])
                sums = sb("sums", [P, C])
                sqs = sb("sqs", [P, C])
                nv = sb("nv", [P, C])
                nb = sb("nb", [P, C])
                ng = sb("ng", [P, C])
                nh = sb("nh", [P, C])
                xt = sb("xt", [HC, 2, 2, N], f16)
                qm = sb("qm", [48, C])
                rr = sb("rr", [48, T])
                gt = sb("gt", [F, 64])
                zt = sb("zt", [T, T])
                tht = sb("tht", [T, T])
                sgt = sb("sgt", [T, 64])
                emx = sb("emx", [T, 1])
                eex = sb("eex", [T, T])
                esm = sb("esm", [T, 1])
                erc = sb("erc", [T, 1])
                et = sb("et", [T, T])
                etr = sb("etr", [T, 2, HT, F])
                er = sb("er", [HC, 2, 16])
                kf = sb("kf", [HC, 2, K, T, F])
                kx = sb("kx", [HC, 2, 2, KC], f16)
                klf = sb("klf", [HC, 2, P])
                kl = sb("kl", [HC, 2, 2, P], f16)
                mh = sb("mh", [P, 512], f16)
                lrt = sb("lrt", [48, 2, N], f16)
                yt = sb("yt", [P, 2, 2, KC], f16)

                p_y = ps("p_y", [P, 2, 2, 512])
                p_t = ps("p_t", [P, 2, 512])
                p_s = ps("p_s", [P, 512])
                p_e = ps("p_e", [P, 512])

                names = ("c vs vmax am allm p2 vlink vh vl vsh pre0 x sum mean xc sq sqs var newt xn q qm rr gt prod zt tanh "
                         "sg el emx eex erc et etr erep er kf k2 klf kh kl klh kll tr xth xtl lr lrh lrl lrst y yh yl yst "
                         "cheb scl").split()
                s = {n: sem("s1_" + n) for n in names}
                s_yst = [sem(f"s1_ystore{i}") for i in range(2)]

                with nc.Block() as block:
                    @block.sync
                    def _(sp):
                        sp.dma_start(ua[:, :, :], a["ua"].rearrange("(t p) c -> p t c", p=P)).then_inc(s["c"], 16)
                        for dst, src in ((ident, "ident"), (lrm, "lrm"), (m48, "m48"), (thr, "thr"), (w2r, "w2r"), (w3r, "w3r"),
                                         (iw, "iw"), (be, "be"), (vet, "vet")):
                            d = dst[:, :, :] if len(dst.shape) == 3 else dst[:, :]
                            sp.dma_start(d, a[src]).then_inc(s["c"], 16)

                        def load_x(i):
                            wait(sp, s["xn"], i)
                            sp.dma_start(xf[:, :, :], x_b[i]).then_inc(s["x"], 16)

                        def store(p):
                            sp.wait_ge(s["lrl"], 4 * p + 4)
                            sp.dma_start(lr_d[p], lrt[:, :, :]).then_inc(s["lrst"], 16)
                            for t in range(NT):
                                sp.wait_ge(s["yh"], 8 * p + t + 1)
                                sp.wait_ge(s["yl"], 8 * p + t + 1)
                                sp.dma_start(y_d[p, :, t], yt[:, t % 2, :, :]).then_inc(s_yst[t % 2], 16)

                        load_x(0)
                        load_x(1)
                        store(0)
                        load_x(2)
                        with sp.Fori(2, B - 1) as i:
                            store(i - 1)
                            load_x(i + 1)
                        for p in (B - 2, B - 1):
                            store(p)
                        sp.wait_ge(s["lrst"], 16 * B)
                        for h in range(2):
                            sp.wait_ge(s_yst[h], 16 * B * NT // 2)

                    @block.gpsimd
                    def _(pool):
                        for k in range(K):
                            pool.dma_start(cheb[:, k], a["cheb"][:, k]).then_inc(s["cheb"], 16)
                        nc.gpsimd.memset(ones[:, :], 1.0 / N).then_inc(s_rootc, 1)
                        nc.gpsimd.memset(amax[:, :], 0.0).then_inc(s_rootc, 1)
                        nc.gpsimd.memset(klf[:, :, :], 0.0).then_inc(s_rootc, 1)
                        nc.gpsimd.memset(gt[:, :], 0.0).then_inc(s_rootc, 1)
                        nc.gpsimd.memset(sgt[:, :], 0.0).then_inc(s_rootc, 1)
                        for t in range(NT):
                            if t:
                                pool.wait_ge(s["vmax"], t)
                            pool.dma_start(vstage[:, 0], a["vst"][t * P:(t + 1) * P, :]).then_inc(s["vs"], 16)
                        pool.wait_ge(s["am"], 6)
                        nc.gpsimd.partition_all_reduce(am_all[:, :], amax[:, :], P, ABSMAX).then_inc(s["allm"], 1)
                        for t in range(NT):
                            pool.wait_ge(s["vmax"], NT)
                            if t:
                                pool.wait_ge(s["vsh"], t)
                            pool.dma_start(vstage[:, 0], a["vst"][t * P:(t + 1) * P, :]).then_inc(s["vs"], 16)

                        def norm(i):
                            pool.wait_ge(s["newt"], NEWTON * i + NEWTON)
                            pool.wait_ge(s["xc"], i + 1)
                            wait(pool, s["q"], i)
                            wait(pool, s["tr"], 4 * i)
                            nc.gpsimd.tensor_tensor(xn[:, :, :], xf[:, :, :],
                                                    ng[:, :].unsqueeze(1).broadcast_to([P, NT, C]), ALU.mult).then_inc(s["xn"], 1)

                        norm(0)
                        with pool.Fori(1, B) as i:
                            norm(i)

                    @block.vector
                    def _(dve):
                        dve.wait_ge(s["c"], 16 * 10)
                        dve.wait_ge(s["cheb"], 16 * K)
                        dve.wait_ge(s_rootc, 5)
                        for t in range(NT):
                            dve.wait_ge(s["vs"], 16 * (t + 1))
                            nc.vector.tensor_reduce(vmax[:, t:t + 1], vstage[:, 0], AX.X, ALU.max,
                                                    apply_absolute_value=True).then_inc(s["vmax"], 1)
                        for k in range(K):
                            nc.vector.tensor_reduce(vmax[:, NT + k:NT + k + 1], cheb[:, k], AX.XY, ALU.max,
                                                    apply_absolute_value=True).then_inc(s["vmax"], 1)
                        dve.wait_ge(s["vmax"], NT + K)
                        nc.vector.tensor_reduce(amax[:, VS:VS + 1], vmax[:, 0:NT], AX.X, ALU.max).then_inc(s["am"], 1)
                        nc.vector.tensor_reduce(amax[:, CHEB:CHEB + 1], vmax[:, NT:NT + K], AX.X, ALU.max).then_inc(s["am"], 1)
                        nc.vector.tensor_reduce(amax[0:HC, THETA:THETA + 1], thr[:, :, :], AX.XY, ALU.max,
                                                apply_absolute_value=True).then_inc(s["am"], 1)
                        nc.vector.tensor_copy(amax[0:T, W1:W1 + 1], iw[:, 12:13]).then_inc(s["am"], 1)
                        nc.vector.tensor_reduce(amax[0:HC, W2:W2 + 1], w2r[:, :], AX.X, ALU.max,
                                                apply_absolute_value=True).then_inc(s["am"], 1)
                        nc.vector.tensor_copy(amax[0:HC, W3:W3 + 1], w3r[:, :]).then_inc(s["am"], 1)
                        links = [0]

                        def link(ins):
                            links[0] += 1
                            ins.then_inc(s["p2"], 1)
                            dve.wait_ge(s["p2"], links[0])

                        dve.wait_ge(s["allm"], 1)
                        link(nc.vector.tensor_scalar(am_all[:, :], am_all[:, :], 1e-30, None, ALU.max))
                        link(nc.vector.tensor_scalar(p2[:, :].bitcast(u32), am_all[:, :].bitcast(u32), 0x7F800000, None,
                                                     ALU.bitwise_and))
                        link(nc.vector.reciprocal(rp2[:, :], p2[:, :]))
                        link(nc.vector.tensor_tensor(fac[:, 5:6], p2[:, W1:W1 + 1], p2[:, W2:W2 + 1], ALU.mult))
                        link(nc.vector.tensor_tensor(fac[:, 0:1], fac[:, 5:6], p2[:, W3:W3 + 1], ALU.mult))
                        link(nc.vector.tensor_scalar(fac[:, 1:2], p2[:, VS:VS + 1], 1.0 / (V_UP * SIG_UP), None, ALU.mult))
                        link(nc.vector.tensor_scalar(fac[:, 2:3], rp2[:, CHEB:CHEB + 1], CH_UP, None, ALU.mult))
                        link(nc.vector.scalar_tensor_tensor(fac[:, 3:4], p2[:, CHEB:CHEB + 1], 1.0 / (CH_UP * Y_UP),
                                                            p2[:, THETA:THETA + 1], ALU.mult, ALU.mult))
                        link(nc.vector.tensor_scalar(fac[:, 4:5], rp2[:, VS:VS + 1], V_UP, None, ALU.mult))
                        link(nc.vector.tensor_scalar(lrm[:, :], lrm[:, :], 1.0 / (X_UP * K_UP), None, ALU.mult))
                        link(nc.vector.tensor_scalar(thr[:, :, :], thr[:, :, :], rp2[0:HC, THETA:THETA + 1], None, ALU.mult))
                        link(nc.vector.tensor_scalar(w2r[:, :], w2r[:, :], rp2[0:HC, W2:W2 + 1], None, ALU.mult))
                        link(nc.vector.tensor_scalar(w3r[:, :], w3r[:, :], rp2[0:HC, W3:W3 + 1], None, ALU.mult))
                        nc.vector.tensor_scalar(iw[:, 12:13], iw[:, 12:13], rp2[0:T, W1:W1 + 1], None,
                                                ALU.mult).then_inc(s["scl"], 1)
                        for t in range(NT):
                            dve.wait_ge(s["vh"], t + 1)
                            nc.vector.scalar_tensor_tensor(vt[:, 1, t], vstage[:, 0], fac[:, 4:5], vt[:, 0, t],
                                                           ALU.mult, ALU.subtract).then_inc(s["vsh"], 1)

                        def lr_low(p, h):
                            dve.wait_ge(s["lrh"], 2 * p + h + 1)
                            wait(dve, s["lrst"], 16 * p)
                            for g in range(2):
                                nc.vector.scalar_tensor_tensor(
                                    lrt[:, g, 512 * h:512 * h + 512], p_t[64 * g:64 * g + 48, h, :], 1.0 / (X_UP * K_UP),
                                    mh[64 * g:64 * g + 48, :], ALU.mult, ALU.subtract).then_inc(s["lrl"], 1)

                        def y_low(p, t):
                            dve.wait_ge(s["yh"], 8 * p + t + 1)
                            nc.vector.scalar_tensor_tensor(
                                yt[:, t % 2, 1, :].rearrange("p (h c) -> p h c", h=2), p_y[:, t % 2, :, 0:KC // 2],
                                Y_UP / (X_UP * K_UP), yt[:, t % 2, 0, :].rearrange("p (h c) -> p h c", h=2),
                                ALU.mult, ALU.subtract).then_inc(s["yl"], 1)

                        def x_low(i, r):
                            dve.wait_ge(s["xth"], 4 * i + r + 1)
                            h, q = r // 2, r % 2
                            nc.vector.scalar_tensor_tensor(
                                xt[:, 1, h, 512 * q:512 * q + 512], p_t[0:HC, r % 2, :], X_UP,
                                xt[:, 0, h, 512 * q:512 * q + 512], ALU.mult, ALU.subtract).then_inc(s["xtl"], 1)

                        def step(i, p):
                            if i is not None:
                                dve.wait_ge(s["x"], 16 * i + 16)
                                wait(dve, s["mean"], i)
                                nc.vector.tensor_reduce(sums[:, :], xf[:, :, :].rearrange("p t c -> p c t"), AX.X,
                                                        ALU.add).then_inc(s["sum"], 1)
                            if p is not None:
                                lr_low(p, 0)
                                lr_low(p, 1)
                            if i is not None:
                                dve.wait_ge(s["mean"], i + 1)
                                dve.wait_ge(s["sum"], i + 1)
                                nc.vector.tensor_tensor(xf[:, :, :], xf[:, :, :],
                                                        p_s[:, 0:C].unsqueeze(1).broadcast_to([P, NT, C]),
                                                        ALU.subtract).then_inc(s["xc"], 1)
                            if p is not None:
                                y_low(p, 0)
                                y_low(p, 1)
                            if i is not None:
                                dve.wait_ge(s["sq"], i + 1)
                                wait(dve, s["var"], i)
                                nc.vector.tensor_reduce(sqs[:, :], sq[:, :, :].rearrange("p t c -> p c t"), AX.X,
                                                        ALU.add).then_inc(s["sqs"], 1)
                            if p is not None:
                                y_low(p, 2)
                                y_low(p, 3)
                            if i is not None:
                                dve.wait_ge(s["var"], i + 1)
                                wait(dve, s["xn"], i)
                                newton_rsqrt(dve, p_s[:, 0:C], nv[:, :], nb[:, :], ng[:, :], nh[:, :], s["newt"],
                                             NEWTON * i, 1e-6)
                            if p is not None:
                                for t in range(4, NT):
                                    y_low(p, t)
                            if i is None:
                                return
                            dve.wait_ge(s["q"], i + 1)
                            nc.vector.tensor_tensor(qm[:, :], p_s[0:48, 0:C], m48[:, :], ALU.mult).then_inc(s["qm"], 1)
                            dve.wait_ge(s["qm"], i + 1)
                            wait(dve, s["prod"], i)
                            nc.vector.tensor_reduce(rr[:, :], qm[:, :].rearrange("p (t f) -> p t f", f=F), AX.X,
                                                    ALU.add).then_inc(s["rr"], 1)
                            dve.wait_ge(s["rr"], i + 1)
                            nc.vector.tensor_copy(gt[:, 0:T], rr[32:48, :]).then_inc(s["gt"], 1)
                            x_low(i, 0)
                            dve.wait_ge(s["prod"], i + 1)
                            wait(dve, s["tanh"], i)
                            nc.vector.tensor_tensor(zt[:, :], p_e[0:T, 0:T], be[:, :], ALU.add).then_inc(s["zt"], 1)
                            x_low(i, 1)
                            dve.wait_ge(s["tanh"], i + 1)
                            wait(dve, s["el"], i)
                            nc.vector.tensor_scalar(sgt[:, 0:T], tht[:, :], 0.5, 0.5, ALU.mult, ALU.add).then_inc(s["sg"], 1)
                            x_low(i, 2)
                            dve.wait_ge(s["el"], i + 1)
                            wait(dve, s["eex"], i)
                            nc.vector.tensor_reduce(emx[:, :], p_e[0:T, 32:32 + T], AX.X, ALU.max,
                                                    negate=True).then_inc(s["emx"], 1)
                            x_low(i, 3)
                            dve.wait_ge(s["eex"], i + 1)
                            nc.vector.reciprocal(erc[:, :], esm[:, :]).then_inc(s["erc"], 1)
                            dve.wait_ge(s["erc"], i + 1)
                            nc.vector.tensor_scalar(et[:, :], eex[:, :], erc[:, 0:1], None, ALU.mult).then_inc(s["et"], 1)
                            dve.wait_ge(s["et"], i + 1)
                            wait(dve, s["erep"], i)
                            nc.vector.tensor_copy(etr[:, :, :, :].rearrange("p h t f -> p (h t) f"),
                                                  et[:, :].unsqueeze(2).broadcast_to([T, T, F])).then_inc(s["etr"], 1)
                            dve.wait_ge(s["erep"], i + 1)
                            nc.vector.tensor_copy(er[:, :, :], p_e[0:HC, 64:96].rearrange("p (h u) -> p h u", h=2)
                                                  ).then_inc(s["er"], 1)
                            dve.wait_ge(s["er"], i + 1)
                            wait(dve, s["kl"], i)
                            wait(dve, s["klh"], i)
                            for h in range(2):
                                nc.vector.tensor_scalar(klf[:, h, 0:48], w2r[:, :], er[:, h, 12:13], None,
                                                        ALU.mult).then_inc(s["klf"], 1)
                            nc.vector.tensor_scalar(klf[:, :, 64:112].rearrange("p h (g u) -> p h g u", g=4),
                                                    er[:, :, 0:12].unsqueeze(2).broadcast_to([HC, 2, 4, T]),
                                                    w3r[:, 0:1], None, ALU.mult).then_inc(s["klf"], 1)
                            for h in range(2):
                                nc.vector.tensor_tensor(kf[:, h], er[:, h, 0:12].unsqueeze(1).unsqueeze(3).broadcast_to([HC, K, T, F]),
                                                        thr[:, :, :].unsqueeze(2).broadcast_to([HC, K, T, F]),
                                                        ALU.mult).then_inc(s["kf"], 1)
                            dve.wait_ge(s["klh"], i + 1)
                            nc.vector.scalar_tensor_tensor(kl[:, 1], klf[:, :, :], K_UP, kl[:, 0], ALU.mult,
                                                           ALU.subtract).then_inc(s["kll"], 1)
                            dve.wait_ge(s["kh"], i + 1)
                            nc.vector.scalar_tensor_tensor(kx[:, 1], kf[:, :, :, :, :].rearrange("p h k u o -> p h (k u o)"), K_UP,
                                                           kx[:, 0], ALU.mult, ALU.subtract).then_inc(s["kl"], 1)

                        step(0, None)
                        step(1, 0)
                        with dve.Fori(2, B) as i:
                            step(i, i - 1)
                        step(None, B - 1)

                    @block.scalar
                    def _(act):
                        act.wait_ge(s["p2"], 9)
                        for t in range(NT):
                            act.wait_ge(s["vs"], 16 * (NT + t + 1))
                            nc.scalar.activation(vt[:, 0, t], vstage[:, 0], ACT.Copy, scale=fac[:, 4:5]).then_inc(s["vh"], 1)

                        def lr_high(p, h):
                            act.wait_ge(s["lr"], 2 * p + h + 1)
                            wait(act, s["lrl"], 4 * p + 2 * h)
                            nc.scalar.activation(mh[:, :], p_t[:, h, :], ACT.Copy, scale=lrm[:, 0:1]).then_inc(s["lrh"], 1)

                        def y_high(p, t):
                            act.wait_ge(s["y"], 8 * p + t + 1)
                            wait(act, s_yst[t % 2], 64 * p + 16 * (t // 2))
                            nc.scalar.activation(yt[:, t % 2, 0, :].rearrange("p (h c) -> p h c", h=2),
                                                 p_y[:, t % 2, :, 0:KC // 2], ACT.Copy,
                                                 scale=Y_UP / (X_UP * K_UP)).then_inc(s["yh"], 1)

                        def x_high(i, r):
                            act.wait_ge(s["tr"], 4 * i + r + 1)
                            wait(act, s["y"], 8 * i)
                            h, q = r // 2, r % 2
                            nc.scalar.activation(xt[:, 0, h, 512 * q:512 * q + 512], p_t[0:HC, r % 2, :], ACT.Copy,
                                                 scale=X_UP).then_inc(s["xth"], 1)

                        def step(i, p):
                            if p is not None:
                                lr_high(p, 0)
                                lr_high(p, 1)
                            if i is not None:
                                act.wait_ge(s["xc"], i + 1)
                                wait(act, s["sqs"], i)
                                nc.scalar.activation(sq[:, :, :], xf[:, :, :], ACT.Square).then_inc(s["sq"], 1)
                            if p is not None:
                                for t in range(NT):
                                    y_high(p, t)
                            if i is None:
                                return
                            x_high(i, 0)
                            x_high(i, 1)
                            act.wait_ge(s["zt"], i + 1)
                            wait(act, s["sg"], i)
                            nc.scalar.activation(tht[:, :], zt[:, :], ACT.Tanh, scale=0.5).then_inc(s["tanh"], 1)
                            x_high(i, 2)
                            x_high(i, 3)
                            act.wait_ge(s["emx"], i + 1)
                            wait(act, s["et"], i)
                            nc.scalar.activation(eex[:, :], p_e[0:T, 32:32 + T], ACT.Exp, bias=emx[:, 0:1],
                                                 accum_out=esm[:, :]).then_inc(s["eex"], 1)
                            act.wait_ge(s["klf"], 3 * i + 3)
                            nc.scalar.activation(kl[:, 0], klf[:, :, :], ACT.Copy, scale=K_UP).then_inc(s["klh"], 1)
                            act.wait_ge(s["kf"], 2 * i + 2)
                            nc.scalar.activation(kx[:, 0], kf[:, :, :, :, :].rearrange("p h k u o -> p h (k u o)"), ACT.Copy,
                                                 scale=K_UP).then_inc(s["kh"], 1)

                        step(0, None)
                        step(1, 0)
                        with act.Fori(2, B) as i:
                            step(i, i - 1)
                        step(None, B - 1)

                    @block.tensor
                    def _(pe):
                        def lr(p, h):
                            n = 0
                            for half in range(2):
                                for w, m in ((0, 0), (0, 1), (1, 0)):
                                    last = nc.tensor.matmul(p_t[:, h, :], kl[:, w, half, :], xt[:, m, half, 512 * h:512 * h + 512],
                                                            start=(n == 0), stop=(n == 5))
                                    n += 1
                            last.then_inc(s["lr"], 1)

                        def y(p, t):
                            wait(pe, s["yl"], 8 * p + t - 1)
                            n = 0
                            for half in range(2):
                                for w, m in ((0, 0), (0, 1), (1, 0)):
                                    for c in range(2):
                                        last = nc.tensor.matmul(p_y[:, t % 2, c, 0:KC // 2], xt[:, w, half, t * P:(t + 1) * P],
                                                                kx[:, m, half, c * (KC // 2):(c + 1) * (KC // 2)],
                                                                start=(n == 0), stop=(n == 5))
                                    n += 1
                            last.then_inc(s["y"], 1)

                        def transposes(i, r):
                            if r >= 2:
                                pe.wait_ge(s["xtl"], 4 * i + r - 1)
                            h, q = r // 2, r % 2
                            for t in range(4):
                                last = nc.tensor.transpose(p_t[0:HC, r % 2, t * P:(t + 1) * P],
                                                           xn[:, 4 * q + t, h * HC:(h + 1) * HC], ident[:, :])
                            last.then_inc(s["tr"], 1)

                        def step(i, p):
                            if i is not None:
                                pe.wait_ge(s["sum"], i + 1)
                                wait(pe, s["qm"], i)
                                nc.tensor.matmul(p_s[:, 0:C], ones[:, :], sums[:, :], start=True, stop=True).then_inc(s["mean"], 1)
                            if p is not None:
                                pe.wait_ge(s["xtl"], 4 * p + 4)
                                pe.wait_ge(s["kll"], p + 1)
                                lr(p, 0)
                                lr(p, 1)
                                pe.wait_ge(s["kl"], p + 1)
                                for t in range(4):
                                    y(p, t)
                            if i is not None:
                                pe.wait_ge(s["sqs"], i + 1)
                                pe.wait_ge(s["xc"], i + 1)
                                nc.tensor.matmul(p_s[:, 0:C], ones[:, :], sqs[:, :], start=True, stop=True).then_inc(s["var"], 1)
                            if p is not None:
                                for t in range(4, NT):
                                    y(p, t)
                            if i is None:
                                return
                            pe.wait_ge(s["xn"], i + 1)
                            pe.wait_ge(s["newt"], NEWTON * i + 1)
                            for t in range(NT):
                                last = nc.tensor.matmul(p_s[0:48, 0:C], ua[:, t, :], xn[:, t, :], start=(t == 0), stop=(t == NT - 1))
                            last.then_inc(s["q"], 1)
                            if p is not None:
                                pe.wait_ge(s["lrl"], 4 * p + 4)
                            transposes(i, 0)
                            transposes(i, 1)
                            pe.wait_ge(s["gt"], i + 1)
                            wait(pe, s["er"], i)
                            nc.tensor.matmul(p_e[0:64, 0:T], gt[:, :], rr[0:F, :], start=True, stop=True).then_inc(s["prod"], 1)
                            transposes(i, 2)
                            transposes(i, 3)
                            pe.wait_ge(s["sg"], i + 1)
                            nc.tensor.matmul(p_e[0:64, 32:32 + T], sgt[:, :], vet[:, :], start=True, stop=True).then_inc(s["el"], 1)
                            pe.wait_ge(s["etr"], i + 1)
                            pe.wait_ge(s["eex"], i + 1)
                            for h in range(2):
                                last = nc.tensor.matmul(p_e[0:HC, 64 + 16 * h:64 + 16 * h + 16],
                                                        etr[:, h].rearrange("p t f -> p (t f)"), iw[:, :], start=True, stop=True)
                            last.then_inc(s["erep"], 1)

                        pe.wait_ge(s_rootc, 5)
                        pe.wait_ge(s["scl"], 1)
                        pe.wait_ge(s["c"], 16 * 10)
                        step(0, None)
                        step(1, 0)
                        with pe.Fori(2, B) as i:
                            step(i, i - 1)
                        step(None, B - 1)

            with ExitStack() as st:
                sb, ps, sem = make(st)
                bst = sb("bs_tile", [P, 2, NT, P])
                lr = sb("lr", [P, 2, N], f16)
                z = sb("z", [P, NT, P])
                sig = sb("sig", [P, 2, 2, NT, P], f16)
                et2 = sb("e_t", [P, N])
                mx = sb("mx", [P, 2])
                nmx = sb("nmx", [P, 2])
                den = sb("den", [P, 2])
                rden = sb("rden", [P, 2])
                oscale = sb("oscale", [P, 2])
                pk = sb("p_k", [P, K, NT, P])
                pkx = sb("p_split", [P, 2, K, NT, P], f16)
                yx = sb("y_split", [P, NT, 2, KC], f16)
                conv = sb("conv", [P, 2, C])
                xres = sb("x_res", [P, 2, C])
                x2t = sb("x2_tile", [P, 2, C])

                p_a = ps("p_a", [P, 2, 512])
                p_b = ps("p_b", [P, 2 * 512])
                p_c = ps("p_c", [P, NT, P])
                p_d = ps("p_d", [P, 2, 512])

                s_prod = sem("s2_prod")
                s_z = sem("s2_z")
                s_tanh = sem("s2_tanh")
                s_sig = sem("s2_sig")
                s_sigh = sem("s2_sigh")
                s_sigl = sem("s2_sigl")
                s_logit = sem("s2_logit")
                s_max = sem("s2_max")
                s_nmax = sem("s2_nmax")
                s_exp = sem("s2_exp")
                s_rden = sem("s2_rden")
                s_osc = sem("s2_osc")
                s_tr = sem("s2_tr")
                s_pk = sem("s2_pk")
                s_pkh = sem("s2_pkh")
                s_pkl = sem("s2_pkl")
                s_conv = sem("s2_conv")
                s_relu = sem("s2_relu")
                s_x2 = sem("s2_x2")
                s_lrpad = sem("s2_lrpad")
                s_lr = sem("s2_lr")
                s_y = [sem(f"s2_y{t}") for t in range(NT)]
                s_bs = [sem(f"s2_bs{i}") for i in range(2)]
                s_xres = [sem(f"s2_xres{i}") for i in range(2)]
                s_st = [sem(f"s2_store{i}") for i in range(2)]

                def batches(eng, slot, first_slot):
                    first_slot()
                    for j in range(NT):
                        slot(0, j, j == 0, False)
                    with eng.Fori(1, B - 1) as b:
                        for j in range(NT):
                            slot(b, j, False, False)
                    for j in range(NT):
                        slot(B - 1, j, False, j == NT - 1)

                with nc.Block() as block:
                    @block.sync
                    def _(sp):
                        def load_lr(b):
                            sp.dma_start(lr[0:48, :, :], lr_d[b]).then_inc(s_lr, 16)

                        def load_bs(j):
                            sp.dma_start(bst[:, j % 2], a["bs"][j % NT]).then_inc(s_bs[j % 2], 16)

                        def store(b, j):
                            wait(sp, s_x2, 8 * b + j + 1)
                            sp.dma_start(x2_b[b, :, j], x2t[:, j % 2]).then_inc(s_st[j % 2], 16)

                        def begin():
                            sp.wait_ge(s_lrpad, 1)
                            load_lr(0)
                            load_bs(0)
                            load_bs(1)

                        def slot(b, j, first, last):
                            if not (first or last) and not (isinstance(b, int) and b == B - 1 and j >= NT - 2):
                                pass
                            more = not (isinstance(b, int) and b == B - 1 and j + 2 >= NT)
                            if more:
                                wait(sp, s_z, 16 * b + 2 * j + 2)
                                load_bs(j + 2)
                            if not (isinstance(b, int) and b == 0 and j < 2):
                                if j >= 2:
                                    store(b, j - 2)
                                else:
                                    store(b - 1, j + 6)
                            sp.dma_start(xres[:, j % 2], x_b[b, :, j]).then_inc(s_xres[j % 2], 16)
                            if j == 1:
                                wait(sp, s_conv, 8 * b)
                                for t in range(NT):
                                    sp.dma_start(yx[:, t], y_d[b, :, t]).then_inc(s_y[t], 16)
                            if j == NT - 2 and not (isinstance(b, int) and b == B - 1):
                                wait(sp, s_prod, 16 * b + 16)
                                load_lr(b + 1)

                        batches(sp, slot, begin)
                        store(B - 1, NT - 2)
                        store(B - 1, NT - 1)
                        for h in range(2):
                            sp.wait_ge(s_st[h], 16 * B * NT // 2)

                    @block.gpsimd
                    def _(pool):
                        nc.gpsimd.memset(lr[:, :, :], 0.0).then_inc(s_lrpad, 1)

                        def sig_low(b, j):
                            wait(pool, s_sigh, 8 * b + j + 1)
                            nc.gpsimd.tensor_tensor(sig[:, j % 2, 1], z[:, :, :], sig[:, j % 2, 0], ALU.subtract).then_inc(s_sigl, 1)

                        def add(b, j):
                            wait(pool, s_relu, 8 * b + j + 1)
                            wait(pool, s_xres[j % 2], 64 * b + 16 * (j // 2) + 16)
                            wait(pool, s_st[j % 2], 64 * b + 16 * (j // 2))
                            nc.gpsimd.tensor_tensor(x2t[:, j % 2], conv[:, j % 2], xres[:, j % 2], ALU.add).then_inc(s_x2, 1)

                        def slot(b, j, first, last):
                            if not last:
                                sig_low(b + (j + 1) // NT, (j + 1) % NT)
                            if not first:
                                add(b - (j == 0), (j - 1) % NT)

                        batches(pool, slot, lambda: sig_low(0, 0))
                        add(B - 1, NT - 1)

                    @block.vector
                    def _(dve):
                        def add_bs(b, j):
                            n = 8 * b + j
                            wait(dve, s_sigl, n)
                            wait(dve, s_bs[j % 2], 64 * b + 16 * (j // 2) + 16)
                            for h in range(2):
                                wait(dve, s_prod, 2 * n + h + 1)
                                nc.vector.scalar_tensor_tensor(
                                    z[:, 4 * h:4 * h + 4, :].rearrange("p t v -> p (t v)"), p_a[:, h, :], fac[:, 0:1],
                                    bst[:, j % 2, 4 * h:4 * h + 4, :].rearrange("p t v -> p (t v)"),
                                    ALU.mult, ALU.add).then_inc(s_z, 1)

                        def mask(b, j):
                            n = 8 * b + j
                            wait(dve, s_tr, n + 1)
                            for k in range(K):
                                wait(dve, s_pkl, 3 * n - 2 + k)
                                nc.vector.scalar_tensor_tensor(pk[:, k], cheb[:, k, :, j * P:(j + 1) * P], fac[:, 2:3],
                                                               p_c[:, :, :], ALU.mult, ALU.mult).then_inc(s_pk, 1)
                                if k:
                                    low(b, j, k - 1)
                            low(b, j, K - 1)

                        def low(b, j, k):
                            n = 8 * b + j
                            wait(dve, s_pkh, 3 * n + k + 1)
                            wait(dve, s_conv, n)
                            nc.vector.tensor_tensor(pkx[:, 1, k], pk[:, k], pkx[:, 0, k], ALU.subtract).then_inc(s_pkl, 1)

                        def row_max(b, j):
                            n = 8 * b + j
                            wait(dve, s_logit, n + 1)
                            wait(dve, s_nmax, n - 1)
                            nc.vector.tensor_reduce(mx[:, j % 2:j % 2 + 1], p_b[:, :], AX.X, ALU.max, negate=True).then_inc(s_max, 1)
                            wait(dve, s_max, n + 1)
                            wait(dve, s_exp, n - 1)
                            nc.vector.tensor_scalar(nmx[:, j % 2:j % 2 + 1], mx[:, j % 2:j % 2 + 1], fac[:, 1:2], None,
                                                    ALU.mult).then_inc(s_nmax, 1)

                        def row_scale(b, j):
                            n = 8 * b + j
                            wait(dve, s_exp, n + 1)
                            nc.vector.reciprocal(rden[:, j % 2:j % 2 + 1], den[:, j % 2:j % 2 + 1]).then_inc(s_rden, 1)
                            wait(dve, s_rden, n + 1)
                            wait(dve, s_relu, n - 1)
                            nc.vector.tensor_scalar(oscale[:, j % 2:j % 2 + 1], rden[:, j % 2:j % 2 + 1], fac[:, 3:4], None,
                                                    ALU.mult).then_inc(s_osc, 1)

                        def slot(b, j, first, last):
                            if not last:
                                add_bs(b + (j + 1) // NT, (j + 1) % NT)
                            if not first:
                                mask(b - (j == 0), (j - 1) % NT)
                            row_max(b, j)
                            row_scale(b, j)

                        batches(dve, slot, lambda: add_bs(0, 0))
                        mask(B - 1, NT - 1)

                    @block.scalar
                    def _(act):
                        def tanh(b, j):
                            n = 8 * b + j
                            wait(act, s_z, 2 * n + 2)
                            nc.scalar.activation(z[:, :, :], z[:, :, :], ACT.Tanh, scale=0.5).then_inc(s_tanh, 1)

                        def sig_high(b, j):
                            n = 8 * b + j
                            wait(act, s_tanh, n + 1)
                            nc.scalar.activation(z[:, :, :], z[:, :, :], ACT.Copy, scale=SIG_UP / 2, bias=SIG_UP / 2).then_inc(s_sig, 1)
                            wait(act, s_sig, n + 1)
                            wait(act, s_logit, n - 1)
                            nc.scalar.activation(sig[:, j % 2, 0], z[:, :, :], ACT.Copy).then_inc(s_sigh, 1)

                        def high(b, j, k):
                            n = 8 * b + j
                            wait(act, s_pk, 3 * n + k + 1)
                            wait(act, s_conv, n)
                            nc.scalar.activation(pkx[:, 0, k], pk[:, k], ACT.Copy).then_inc(s_pkh, 1)

                        def exp(b, j):
                            n = 8 * b + j
                            wait(act, s_nmax, n + 1)
                            wait(act, s_tr, n)
                            wait(act, s_rden, n - 1)
                            nc.scalar.activation(et2[:, :], p_b[:, :], ACT.Exp, bias=nmx[:, j % 2:j % 2 + 1], scale=fac[:, 1:2],
                                                 accum_out=den[:, j % 2:j % 2 + 1]).then_inc(s_exp, 1)

                        def relu(b, j):
                            n = 8 * b + j
                            wait(act, s_conv, n + 1)
                            wait(act, s_osc, n + 1)
                            wait(act, s_x2, n - 1)
                            nc.scalar.activation(conv[:, j % 2], p_d[:, j % 2, 0:C], ACT.Relu,
                                                 scale=oscale[:, j % 2:j % 2 + 1]).then_inc(s_relu, 1)

                        def slot(b, j, first, last):
                            pb, pj = b - (j == 0), (j - 1) % NT
                            if not last:
                                tanh(b + (j + 1) // NT, (j + 1) % NT)
                            if not first:
                                high(pb, pj, 0)
                            if not last:
                                sig_high(b + (j + 1) // NT, (j + 1) % NT)
                            if not first:
                                high(pb, pj, 1)
                                high(pb, pj, 2)
                            exp(b, j)
                            if not first:
                                relu(pb, pj)

                        def begin():
                            tanh(0, 0)
                            sig_high(0, 0)

                        batches(act, slot, begin)
                        for k in range(K):
                            high(B - 1, NT - 1, k)
                        relu(B - 1, NT - 1)

                    @block.tensor
                    def _(pe):
                        def prod(b, j):
                            n = 8 * b + j
                            wait(pe, s_z, 2 * n)
                            if j == 0:
                                wait(pe, s_lr, 16 * b + 16)
                            for h in range(2):
                                for t in range(4):
                                    last = nc.tensor.matmul(p_a[:, h, t * P:(t + 1) * P], lr[:, 0, (4 * h + t) * P:(4 * h + t + 1) * P],
                                                            lr[:, 1, j * P:(j + 1) * P], start=True, stop=True)
                                last.then_inc(s_prod, 1)

                        def logits(b, j):
                            n = 8 * b + j
                            wait(pe, s_sigl, n + 1)
                            wait(pe, s_exp, n)
                            for t in range(NT):
                                for w, m in ((0, 0), (0, 1), (1, 0)):
                                    for c in range(2):
                                        last = nc.tensor.matmul(p_b[:, 512 * c:512 * c + 512], sig[:, j % 2, w, t],
                                                                vt[:, m, t, 512 * c:512 * c + 512],
                                                                start=(t == 0 and w == 0 and m == 0), stop=(t == NT - 1 and w == 1))
                            last.then_inc(s_logit, 1)

                        def transposes(b, j):
                            n = 8 * b + j
                            wait(pe, s_exp, n + 1)
                            wait(pe, s_pk, 3 * n)
                            for t in range(NT):
                                last = nc.tensor.transpose(p_c[:, t, :], et2[:, t * P:(t + 1) * P], ident[:, :])
                            last.then_inc(s_tr, 1)

                        def convolve(b, j):
                            n = 8 * b + j
                            wait(pe, s_pkl, 3 * n + 3)
                            wait(pe, s_relu, n - 1)
                            for t in range(NT):
                                if j == 0:
                                    wait(pe, s_y[t], 16 * b + 16)
                                for k in range(K):
                                    for w, m in ((0, 0), (0, 1), (1, 0)):
                                        last = nc.tensor.matmul(p_d[:, j % 2, 0:C], pkx[:, w, k, t], yx[:, t, m, k * C:(k + 1) * C],
                                                                start=(t == 0 and k == 0 and w == 0 and m == 0),
                                                                stop=(t == NT - 1 and k == K - 1 and w == 1))
                            last.then_inc(s_conv, 1)

                        def slot(b, j, first, last):
                            pb, pj = b - (j == 0), (j - 1) % NT
                            if not last:
                                prod(b + (j + 1) // NT, (j + 1) % NT)
                            if not first:
                                transposes(pb, pj)
                            logits(b, j)
                            if not first:
                                convolve(pb, pj)

                        batches(pe, slot, lambda: prod(0, 0))
                        transposes(B - 1, NT - 1)
                        convolve(B - 1, NT - 1)

        with ExitStack() as st:
            sb, ps, sem = make(st)
            wst = sb("w_stage", [P, NT, N])
            gst = sb("g_stage", [P, NT, GC])
            wx = sb("w_split", [P, 2, NT, N], f16)
            gx = sb("g_split", [P, 2, NT, GC], f16)
            upt = sb("up", [64, N])
            upf = sb("up_factor", [64, 1])
            gb = sb("gate_bias", [HC, EXP])
            iota = sb("iota", [HC, EXP])
            am3 = sb("am3", [P, 2])
            am3_all = sb("am3_all", [P, 2])
            q2 = sb("q2", [P, 2])
            rq2 = sb("rq2", [P, 2])
            fc = sb("fc", [P, 8])
            x3 = sb("x3", [P, 2, NT, TOK])
            zc = sb("zc", [P, NT, TOK])
            sq3 = sb("sq3", [P, NT, TOK])
            zx = sb("z_split", [P, 2, 2, NT, TOK], f16)
            sums3 = sb("sums3", [P, TOK])
            sqs3 = sb("sqs3", [P, TOK])
            nv3 = sb("nv3", [P, TOK])
            nb3 = sb("nb3", [P, TOK])
            ng3 = sb("ng3", [P, TOK])
            nh3 = sb("nh3", [P, TOK])
            gl = sb("gl", [HC, TG, GC])
            top = sb("top", [HC, TG, 8])
            tix = sb("tix", [HC, TG, 8], u32)
            tixf = sb("tixf", [HC, TG, 2])
            dif = sb("dif", [HC, TG])
            ex2 = sb("ex2", [HC, TG])
            den2 = sb("den2", [HC, TG])
            wts = sb("wts", [HC, TG, 2])
            eq = sb("eq", [HC, TG * 2, EXP])
            eqw = sb("eqw", [HC, TG, 2, EXP])
            wgt = sb("wgt", [HC, TG, EXP])
            hw = sb("hw", [HC, TG, P])
            hwt = sb("hwt", [64, 2, TOK])
            ob = sb("ob", [P, 4, TOK])

            p_o = ps("p_o", [P, 4, 512])
            p_m = ps("p_m", [P, 512])
            p_g = ps("p_g", [P, TG, GP])
            p_h = ps("p_h", [P, 512])

            names = ("c w amax allm f wh wl gh gl upl x sum mean xc sq sqs var newt z zh zl gate glog top tix tixf dif ex2 den r w1 w2 "
                     "low eq eqw wgt hw hwtr hwt o oev oadd init").split()
            s = {n: sem("s3_" + n) for n in names}
            s_x3 = [sem(f"s3_x{i}") for i in range(2)]
            s_out = [sem(f"s3_out{i}") for i in range(4)]
            x2_g = x2_d.rearrange("(g q) (t p) c -> g q p t c", q=2, p=P)
            out_g = out.rearrange("(g q) (t p) h w -> g t p q (h w)", q=2, p=P)

            def pairs(eng, step, first):
                first()
                step(0, 0, None)
                step(1, 1, 0)
                with eng.Fori(1, PAIRS // 2) as d:
                    step(2 * d, 0, 2 * d - 1)
                    step(2 * d + 1, 1, 2 * d)
                step(None, PAIRS % 2, PAIRS - 1)

            with nc.Block() as block:
                @block.sync
                def _(sp):
                    def load_x(g, par):
                        for q in range(2):
                            sp.dma_start(x3[:, par, :, q * C:(q + 1) * C], x2_g[g, q]).then_inc(s_x3[par], 16)

                    load_x(0, 0)
                    sp.dma_start(wst[:, :, :], a["wt"].rearrange("(t p) o -> p t o", p=P)).then_inc(s["w"], 16)
                    sp.dma_start(gst[:, :, :], a["gt"].rearrange("(t p) e -> p t e", p=P)).then_inc(s["c"], 16)
                    sp.wait_ge(s["init"], 2)
                    sp.dma_start(upt[0:41, :], a["up"]).then_inc(s["c"], 16)
                    sp.dma_start(upf[:, :], a["upf"]).then_inc(s["c"], 16)
                    sp.dma_start(gb[:, :], a["gb"]).then_inc(s["c"], 16)
                    sp.dma_start(iota[:, :], a["iota"]).then_inc(s["c"], 16)

                    def step(g, par, pg):
                        if pg is not None:
                            for t in range(NT):
                                wait(sp, s["oadd"], 8 * pg + t + 1)
                                sp.dma_start(out_g[pg, t], ob[:, t % 4, :].rearrange("p (q c) -> p q c", q=2)).then_inc(s_out[t % 4], 16)
                        if g is not None and not (isinstance(g, int) and g == PAIRS - 1):
                            load_x(g + 1, 1 - par)

                    step(0, 0, None)
                    step(1, 1, 0)
                    with sp.Fori(1, PAIRS // 2 - 1) as d:
                        step(2 * d, 0, 2 * d - 1)
                        step(2 * d + 1, 1, 2 * d)
                    step(PAIRS - 2, 0, PAIRS - 3)
                    step(PAIRS - 1, 1, PAIRS - 2)
                    step(None, 0, PAIRS - 1)
                    for i in range(4):
                        sp.wait_ge(s_out[i], 16 * PAIRS * NT // 4)

                @block.gpsimd
                def _(pool):
                    nc.gpsimd.memset(upt[:, :], 0.0).then_inc(s["init"], 1)
                    nc.gpsimd.memset(hw[:, :, :], 0.0).then_inc(s["init"], 1)
                    pool.wait_ge(s["init"], 2)
                    nc.gpsimd.memset(hw[:, :, 40:41], 1.0).then_inc(s["init"], 1)
                    pool.wait_ge(s["amax"], 2)
                    nc.gpsimd.partition_all_reduce(am3_all[:, :], am3[:, :], P, ABSMAX).then_inc(s["allm"], 1)

                    def step(g, par, pg):
                        def add(t):
                            wait(pool, s["oev"], 8 * pg + t + 1)
                            nc.gpsimd.tensor_tensor(ob[:, t % 4, :], ob[:, t % 4, :], x3[:, 1 - par, t, :], ALU.add).then_inc(s["oadd"], 1)
                        if pg is not None:
                            for t in range(5):
                                add(t)
                        if g is not None:
                            wait(pool, s["newt"], NEWTON * g + NEWTON)
                            wait(pool, s["xc"], g + 1)
                            wait(pool, s["sq"], g + 1)
                            nc.gpsimd.tensor_tensor(zc[:, :, :], zc[:, :, :], ng3[:, :].unsqueeze(1).broadcast_to([P, NT, TOK]),
                                                    ALU.mult).then_inc(s["z"], 1)
                        if pg is not None:
                            for t in range(5, NT):
                                add(t)

                    pairs(pool, step, lambda: None)

                @block.vector
                def _(dve):
                    def prepare():
                        links = [0]

                        def link(ins):
                            links[0] += 1
                            ins.then_inc(s["f"], 1)
                            dve.wait_ge(s["f"], links[0])

                        dve.wait_ge(s["w"], 16)
                        nc.vector.tensor_reduce(am3[:, 0:1], wst[:, :, :], AX.XY, ALU.max, apply_absolute_value=True).then_inc(s["amax"], 1)
                        dve.wait_ge(s["c"], 16 * 5)
                        nc.vector.tensor_reduce(am3[:, 1:2], gst[:, :, :], AX.XY, ALU.max, apply_absolute_value=True).then_inc(s["amax"], 1)
                        dve.wait_ge(s["allm"], 1)
                        link(nc.vector.tensor_scalar(am3_all[:, :], am3_all[:, :], 1e-30, None, ALU.max))
                        link(nc.vector.tensor_scalar(q2[:, :].bitcast(u32), am3_all[:, :].bitcast(u32), 0x7F800000, None, ALU.bitwise_and))
                        link(nc.vector.reciprocal(rq2[:, :], q2[:, :]))
                        link(nc.vector.tensor_scalar(fc[:, 0:2], rq2[:, :], W_UP, None, ALU.mult))
                        link(nc.vector.tensor_scalar(fc[:, 2:4], q2[:, :], 1.0 / (W_UP * Z_UP), None, ALU.mult))
                        link(nc.vector.tensor_scalar(fc[:, 4:5], rq2[:, 0:1], W_UP * Z_UP, None, ALU.mult))
                        link(nc.vector.tensor_scalar(upf[:, :], upf[:, :], fc[0:64, 4:5], None, ALU.mult))
                        nc.vector.tensor_scalar(upt[:, :], upt[:, :], upf[:, 0:1], None, ALU.mult).then_inc(s["upl"], 1)
                        dve.wait_ge(s["gh"], 1)
                        nc.vector.scalar_tensor_tensor(gx[:, 1], gst[:, :, :], fc[:, 1:2], gx[:, 0], ALU.mult, ALU.subtract).then_inc(s["gl"], 1)
                        for t in range(NT):
                            dve.wait_ge(s["wh"], t + 1)
                            nc.vector.scalar_tensor_tensor(wx[:, 1, t], wst[:, t], fc[:, 0:1], wx[:, 0, t], ALU.mult, ALU.subtract).then_inc(s["wl"], 1)

                    def step(g, par, pg):
                        if g is None:
                            return
                        dve.wait_ge(s_x3[par], 32 * ((g - par) // 2) + 32) if isinstance(g, int) else dve.wait_ge(s_x3[par], 16 * (g - par) + 32)
                        wait(dve, s["mean"], g)
                        nc.vector.tensor_reduce(sums3[:, :], x3[:, par].rearrange("p t c -> p c t"), AX.X, ALU.add).then_inc(s["sum"], 1)
                        dve.wait_ge(s["mean"], g + 1)
                        wait(dve, s["zl"], g)
                        wait(dve, s["zh"], g)
                        nc.vector.tensor_tensor(zc[:, :, :], x3[:, par], p_m[:, 0:TOK].unsqueeze(1).broadcast_to([P, NT, TOK]),
                                                ALU.subtract).then_inc(s["xc"], 1)
                        dve.wait_ge(s["sq"], g + 1)
                        wait(dve, s["var"], g)
                        nc.vector.tensor_reduce(sqs3[:, :], sq3[:, :, :].rearrange("p t c -> p c t"), AX.X, ALU.add).then_inc(s["sqs"], 1)
                        dve.wait_ge(s["var"], g + 1)
                        newton_rsqrt(dve, p_m[:, 0:TOK], nv3[:, :], nb3[:, :], ng3[:, :], nh3[:, :], s["newt"], NEWTON * g, 1e-5)
                        dve.wait_ge(s["zh"], g + 1)
                        nc.vector.scalar_tensor_tensor(zx[:, par, 1], zc[:, :, :], Z_UP, zx[:, par, 0], ALU.mult, ALU.subtract).then_inc(s["zl"], 1)
                        dve.wait_ge(s["gate"], g + 1)
                        nc.vector.scalar_tensor_tensor(gl[:, :, 0:EXP], p_g[0:HC, :, 0:EXP], fc[0:HC, 3:4],
                                                       gb[:, 0:EXP].unsqueeze(1).broadcast_to([HC, TG, EXP]), ALU.mult, ALU.add).then_inc(s["glog"], 1)
                        dve.wait_ge(s["glog"], g + 1)
                        nc.vector.tensor_scalar(gl[:, :, EXP:GC], p_g[0:HC, :, EXP:GC], fc[0:HC, 3:4], None, ALU.mult).then_inc(s["low"], 1)
                        for q in range(TG):
                            nc.vector.max(top[:, q], gl[:, q, 0:EXP]).then_inc(s["top"], 1)
                        wait(dve, s["ex2"], g)
                        dve.wait_ge(s["top"], 4 * g + 4)
                        nc.vector.tensor_tensor(dif[:, :], top[:, :, 1], top[:, :, 0], ALU.subtract).then_inc(s["dif"], 1)
                        for q in range(TG):
                            nc.vector.max_index(tix[:, q], top[:, q], gl[:, q, 0:EXP]).then_inc(s["tix"], 1)
                        dve.wait_ge(s["tix"], 4 * g + 4)
                        nc.vector.tensor_copy(tixf[:, :, :], tix[:, :, 0:2]).then_inc(s["tixf"], 1)
                        dve.wait_ge(s["ex2"], g + 1)
                        nc.vector.tensor_scalar(den2[:, :], ex2[:, :], 1.0, None, ALU.add).then_inc(s["den"], 1)
                        dve.wait_ge(s["den"], g + 1)
                        nc.vector.reciprocal(wts[:, :, 0], den2[:, :]).then_inc(s["r"], 1)
                        dve.wait_ge(s["r"], g + 1)
                        nc.vector.tensor_tensor(wts[:, :, 1], ex2[:, :], wts[:, :, 0], ALU.mult).then_inc(s["w2"], 1)
                        dve.wait_ge(s["tixf"], g + 1)
                        nc.vector.tensor_tensor(eq[:, :, :], iota[:, :].unsqueeze(1).broadcast_to([HC, TG * 2, EXP]),
                                                tixf[:, :, :].rearrange("p q c -> p (q c)").unsqueeze(2).broadcast_to([HC, TG * 2, EXP]),
                                                ALU.is_equal).then_inc(s["eq"], 1)
                        dve.wait_ge(s["eq"], g + 1)
                        dve.wait_ge(s["w2"], g + 1)
                        nc.vector.tensor_tensor(eqw[:, :, :, :].rearrange("p q c e -> p (q c) e"), eq[:, :, :],
                                                wts[:, :, :].rearrange("p q c -> p (q c)").unsqueeze(2).broadcast_to([HC, TG * 2, EXP]),
                                                ALU.mult).then_inc(s["eqw"], 1)
                        dve.wait_ge(s["eqw"], g + 1)
                        nc.vector.tensor_tensor(wgt[:, :, :], eqw[:, :, 0], eqw[:, :, 1], ALU.add).then_inc(s["wgt"], 1)
                        dve.wait_ge(s["low"], g + 1)
                        dve.wait_ge(s["wgt"], g + 1)
                        wait(dve, s["hwtr"], g)
                        nc.vector.tensor_tensor(hw[:, :, 0:40].rearrange("p q (e r) -> p q e r", r=RANK),
                                                gl[:, :, EXP:GC].rearrange("p q (e r) -> p q e r", r=RANK),
                                                wgt[:, :, :].unsqueeze(3).broadcast_to([HC, TG, EXP, RANK]), ALU.mult).then_inc(s["hw"], 1)
                        dve.wait_ge(s["hwtr"], g + 1)
                        wait(dve, s["o"], 8 * (g - 1))
                        nc.vector.tensor_copy(hwt[:, par, :], p_h[0:64, 0:TOK]).then_inc(s["hwt"], 1)

                    pairs(dve, step, prepare)

                @block.scalar
                def _(act):
                    def prepare():
                        act.wait_ge(s["f"], 5)
                        nc.scalar.activation(gx[:, 0], gst[:, :, :], ACT.Copy, scale=fc[:, 1:2]).then_inc(s["gh"], 1)
                        for t in range(NT):
                            nc.scalar.activation(wx[:, 0, t], wst[:, t], ACT.Copy, scale=fc[:, 0:1]).then_inc(s["wh"], 1)

                    def step(g, par, pg):
                        def evac(t):
                            wait(act, s["o"], 8 * pg + t + 1)
                            wait(act, s_out[t % 4], 32 * pg + 16 * (t // 4))
                            nc.scalar.activation(ob[:, t % 4, :], p_o[:, t % 4, 0:TOK], ACT.Copy, scale=fc[:, 2:3]).then_inc(s["oev"], 1)
                        if pg is not None:
                            evac(0)
                            evac(1)
                        if g is not None:
                            act.wait_ge(s["xc"], g + 1)
                            wait(act, s["sqs"], g)
                            nc.scalar.activation(sq3[:, :, :], zc[:, :, :], ACT.Square).then_inc(s["sq"], 1)
                        if pg is not None:
                            for t in range(2, NT):
                                evac(t)
                        if g is None:
                            return
                        act.wait_ge(s["z"], g + 1)
                        wait(act, s["o"], 8 * (g - 1))
                        nc.scalar.activation(zx[:, par, 0], zc[:, :, :], ACT.Copy, scale=Z_UP).then_inc(s["zh"], 1)
                        act.wait_ge(s["dif"], g + 1)
                        wait(act, s["w2"], g)
                        nc.scalar.activation(ex2[:, :], dif[:, :], ACT.Exp).then_inc(s["ex2"], 1)

                    pairs(act, step, prepare)

                @block.tensor
                def _(pe):
                    def prepare():
                        pe.wait_ge(s["init"], 3)
                        pe.wait_ge(s["upl"], 1)
                        pe.wait_ge(s["gl"], 1)
                        pe.wait_ge(s["wl"], NT)

                    def step(g, par, pg):
                        def tile(t):
                            wait(pe, s["oev"], 8 * pg + t - 3)
                            if t == 0:
                                wait(pe, s["hwt"], pg + 1)
                            nc.tensor.matmul(p_o[:, t % 4, 0:TOK], upt[:, t * P:(t + 1) * P], hwt[:, 1 - par, :], start=True, stop=False)
                            for c in range(NT):
                                for w, m in ((0, 0), (0, 1), (1, 0)):
                                    last = nc.tensor.matmul(p_o[:, t % 4, 0:TOK], wx[:, w, c, t * P:(t + 1) * P], zx[:, 1 - par, m, c],
                                                            start=False, stop=(c == NT - 1 and w == 1))
                            last.then_inc(s["o"], 1)

                        if g is not None:
                            pe.wait_ge(s["sum"], g + 1)
                            nc.tensor.matmul(p_m[:, 0:TOK], ones[:, :], sums3[:, :], start=True, stop=True).then_inc(s["mean"], 1)
                        if pg is not None:
                            for t in range(3):
                                tile(t)
                        if g is not None:
                            pe.wait_ge(s["sqs"], g + 1)
                            pe.wait_ge(s["xc"], g + 1)
                            nc.tensor.matmul(p_m[:, 0:TOK], ones[:, :], sqs3[:, :], start=True, stop=True).then_inc(s["var"], 1)
                        if pg is not None:
                            for t in range(3, NT):
                                tile(t)
                        if g is None:
                            return
                        pe.wait_ge(s["zl"], g + 1)
                        for q in range(TG):
                            for c in range(NT):
                                for w, m in ((0, 0), (0, 1), (1, 0)):
                                    last = nc.tensor.matmul(p_g[0:HC, q, 0:GC], zx[:, par, w, c, q * HC:(q + 1) * HC], gx[:, m, c],
                                                            start=(c == 0 and w == 0 and m == 0), stop=(c == NT - 1 and w == 1))
                        last.then_inc(s["gate"], 1)
                        pe.wait_ge(s["hw"], g + 1)
                        wait(pe, s["hwt"], g)
                        for q in range(TG):
                            last = nc.tensor.transpose(p_h[:, q * HC:(q + 1) * HC], hw[:, q, :], ident[0:HC, 0:HC])
                        last.then_inc(s["hwtr"], 1)

                    pe_first = prepare

                    pe.wait_ge(s["init"], 3)
                    pairs(pe, step, pe_first)


def kernel(**inputs):
    import numpy as np
    import concourse.bacc as _bacc
    from concourse import mybir as _mybir
    from concourse.bass_utils import run_bass_kernel_spmd as _run

    g = {k.replace("L0_conv_", "").replace("L0_ffn_", ""): np.asarray(v) for k, v in inputs.items()}
    f4 = g["x"].dtype
    W2t = g["W2"]
    lay = {
        "x": g["x"],
        "cheb": g["cheb"].reshape(K, NT, P, N).transpose(2, 0, 1, 3),
        "bs": g["bs"][0].reshape(NT, P, NT, P).transpose(2, 1, 0, 3),
        "vst": g["Vs"].T,
        "ua": np.concatenate([g["U2"].T, np.zeros((N, 16), f4), np.repeat(g["U1"][:, None], 16, 1)], 1),
        "m48": np.concatenate([np.tile(g["U3"], (16, T)), np.zeros((16, C), f4), np.tile(np.eye(16, dtype=f4), (1, T))], 0),
        "thr": np.tile(g["Theta"].transpose(1, 0, 2), (HT, 1, 1)),
        "w2r": np.tile(W2t, (HT, 4)),
        "w3r": np.tile(g["W3"][:, None], (HT, 1)),
        "iw": np.concatenate([np.eye(T, dtype=f4), g["W1"][:, None], np.zeros((T, 3), f4)], 1),
        "be": g["be"][0],
        "vet": g["Ve"].T,
        "ident": np.eye(P, dtype=f4),
        "lrm": np.array([1.0 if (r < 48 and r // 12 >= 2) or (64 <= r < 112 and (r - 64) // 12 % 2) else 0.0
                         for r in range(P)], f4)[:, None],
        "wt": g["W_base"].T,
        "gt": np.concatenate([g["gate_W"], g["lora_down"].reshape(EXP * RANK, N)], 0).T,
        "up": np.concatenate([g["lora_up"].transpose(0, 2, 1).reshape(EXP * RANK, N), g["b_base"][None]], 0),
        "upf": np.array([1.0 / RANK] * (EXP * RANK) + [1.0] + [0.0] * (63 - EXP * RANK), f4)[:, None],
        "gb": np.tile(g["gate_b"], (HC, 1)),
        "iota": np.tile(np.arange(EXP, dtype=f4), (HC, 1)),
    }
    nc = _bacc.Bacc("TRN2", target_bir_lowering=False, num_devices=1)
    arrays, aps = {}, {}
    for name, v in lay.items():
        v = np.ascontiguousarray(v)
        arrays["in_" + name] = v
        aps[name] = nc.dram_tensor("in_" + name, v.shape, _mybir.dt.from_np(v.dtype), kind="ExternalInput").ap()
    out = nc.dram_tensor("out_0", (B, N, T, F), _mybir.dt.from_np(np.dtype(f4)), kind="ExternalOutput").ap()
    metaformer_program(nc, aps, out)
    r = _run(nc, [arrays], core_ids=[0])
    return r.results[0]["out_0"]
```

```python
import concourse.bass as bass
from concourse import mybir
from contextlib import ExitStack

B, N, T, F, K = 16, 1024, 12, 16, 3
P = 128
NT = N // P
C = T * F
HC = C // 2
HT = T // 2
KC = K * C
EXP, RANK = 10, 4
GC = EXP + EXP * RANK
GP = 64
PAIRS = B // 2
TOK = 2 * C
TG = TOK // HC

X_UP, K_UP = 256.0, 256.0
Y_UP = 32.0
V_UP, SIG_UP = 4096.0, 16384.0
CH_UP = 8192.0
W_UP, Z_UP = 4096.0, 256.0


def metaformer_program(nc, a, out):
    f32, f16, i32, u32 = mybir.dt.float32, mybir.dt.float16, mybir.dt.int32, mybir.dt.uint32
    ALU, ACT, AX = mybir.AluOpType, mybir.ActivationFunctionType, mybir.AxisListType
    ABSMAX = bass.bass_isa.ReduceOp.absmax

    def wait(eng, sem, value):
        if not (isinstance(value, int) and value <= 0):
            eng.wait_ge(sem, value)

    y_d = nc.dram_tensor("y_scratch", (B, P, NT, 2, KC), f16).ap()
    lr_d = nc.dram_tensor("lr_scratch", (B, 48, 2, N), f16).ap()
    x2_d = nc.dram_tensor("x2_scratch", (B, N, C), f32).ap()
    x_b = a["x"].rearrange("b (t p) h w -> b p t (h w)", p=P)
    x2_b = x2_d.rearrange("b (t p) c -> b p t c", p=P)
    out_b = out.rearrange("b (t p) h w -> b p t (h w)", p=P)

    root = ExitStack()
    with root:
        def make(stack):
            def sb(name, shape, dt=f32):
                return stack.enter_context(nc.sbuf_tensor(name, shape, dt))

            def ps(name, shape, dt=f32):
                return stack.enter_context(nc.psum_tensor(name, shape, dt))

            def sem(name):
                return stack.enter_context(nc.semaphore(name))
            return sb, ps, sem

        def newton_rsqrt(dve, var, scale, v, bits, guess, half, chain, base, eps):
            k = [base]

            def link(ins):
                k[0] = k[0] + 1
                ins.then_inc(chain, 1)
                dve.wait_ge(chain, k[0])

            link(nc.vector.tensor_scalar(v, var, scale, eps, ALU.mult, ALU.add))
            link(nc.vector.tensor_scalar(bits.bitcast(u32), v.bitcast(u32), 1, None, ALU.logical_shift_right))
            link(nc.vector.tensor_scalar(guess.bitcast(i32), bits.bitcast(i32), -1.0, 1597463007.0, ALU.mult, ALU.add))
            for _ in range(3):
                link(nc.vector.scalar_tensor_tensor(half, guess, -0.5, guess, ALU.mult, ALU.mult))
                link(nc.vector.tensor_tensor(half, half, v, ALU.mult))
                link(nc.vector.scalar_tensor_tensor(guess, half, 1.5, guess, ALU.add, ALU.mult))

        NEWTON = 12

        rsb, rps, rsem = make(root)
        ones = rsb("ones_over_n", [P, P])
        ident = rsb("ident", [P, P])
        p2 = rsb("p2", [P, 8])
        rp2 = rsb("rp2", [P, 8])
        fac = rsb("fac", [P, 8])
        s_rootc = rsem("s_rootc")
        THETA, W1, W2, W3, VS, CHEB, WB, GD = range(8)

        mid = ExitStack()
        with mid:
            msb, mps, msem = make(mid)
            cheb = msb("cheb", [P, K, NT, N])
            vt = msb("vt_split", [P, 2, NT, N], f16)

            with ExitStack() as st:
                sb, ps, sem = make(st)
                amax = sb("amax", [P, 8])
                am_all = sb("am_all", [P, 8])
                vmax = sb("vmax", [P, NT])
                chmax = sb("chmax", [P, 8])
                wmax = sb("wmax", [P, 8])
                wstage = sb("wstage", [P, N])
                gstage = sb("gstage", [P, NT, GC])
                ua = sb("ua", [P, NT, 18])
                uas = sb("uas", [HC, 18])
                sel_t = sb("sel_t", [HC, 2, T])
                sel_u3 = sb("sel_u3", [HC, 2, T])
                sel_f = sb("sel_f", [HC, F])
                thr = sb("thr", [HC, K, F])
                w2r = sb("w2r", [HC, 48])
                w3r = sb("w3r", [HC, 1])
                iw = sb("iw", [T, 16])
                be = sb("be", [T, T])
                vet = sb("vet", [T, T])
                lrm = sb("lrm", [P, 1])
                xf = sb("xf", [P, 2, NT, C])
                xr = sb("xr", [HC, 2, N])
                junk = sb("junk", [HC, N], f16)
                sm = sb("sm", [HC, 2, 2])
                sm2 = sb("sm2", [HC, 2])
                nmean = sb("nmean", [HC, 2])
                ss = sb("ss", [HC, 2])
                nv = sb("nv", [HC, 2])
                nb = sb("nb", [HC, 2])
                ng = sb("ng", [HC, 2])
                nh = sb("nh", [HC, 2])
                rs = sb("rs", [HC, 2])
                nmr = sb("nmr", [HC, 2])
                qt = sb("qt", [HC, 2, 18])
                qs = sb("qs", [HC, 2, 18])
                dg = sb("dg", [HC, 2, F])
                rg = sb("rg", [F, 80])
                xt = sb("xt", [HC, 2, 2, 2, N], f16)
                zt = sb("zt", [T, T])
                tht = sb("tht", [T, T])
                sgt = sb("sgt", [T, 64])
                emx = sb("emx", [T, 1])
                eex = sb("eex", [T, T])
                esm = sb("esm", [T, 1])
                erc = sb("erc", [T, 1])
                et = sb("et", [T, T])
                etr = sb("etr", [T, 2, HT, F])
                er = sb("er", [HC, 2, 16])
                kf = sb("kf", [HC, 2, K, T, F])
                kx = sb("kx", [HC, 2, 2, 2, KC], f16)
                klf = sb("klf", [HC, 2, P])
                kl = sb("kl", [HC, 2, 2, 2, P], f16)
                mh = sb("mh", [112, 512], f16)
                lrt = sb("lrt", [112, N], f16)
                yt = sb("yt", [P, 2, 2, KC], f16)

                p_y = ps("p_y", [P, 2, 2, 512])
                p_t = ps("p_t", [P, 2, 512])
                p_s = ps("p_s", [P, 512])
                p_e = ps("p_e", [P, 512])

                names = ("c uas uasc aA allA pA vs vmax aB allB pB cheb w chmax wmax aC gd allC pC vh vl cp sm2 nmean sq newt rs nmr v q qt qs dg rg rgs "
                         "prod zt tanh sg el emx eex erc et etr erep er kf klf kh kl klh kll tr xth xtl lr lrh lrl lrst y yh yl").split()
                s = {n: sem("s1_" + n) for n in names}
                s_x = [sem(f"s1_x{i}") for i in range(2)]
                s_yst = [sem(f"s1_ystore{i}") for i in range(2)]

                def batch_steps(eng, step):
                    step(0, 0, None, 0)
                    step(1, 1, 0, 0)
                    with eng.Fori(1, B // 2) as d:
                        step(2 * d, 0, 2 * d - 1, d)
                        step(2 * d + 1, 1, 2 * d, d)
                    step(None, 0, B - 1, None)

                with nc.Block() as block:
                    @block.sync
                    def _(sp):
                        sp.dma_start(xf[:, 0], x_b[0]).then_inc(s_x[0], 16)
                        sp.dma_start(ua[:, :, :], a["ua"].rearrange("(t p) c -> p t c", p=P)).then_inc(s["c"], 16)
                        for dst, src in ((ident, "ident"), (lrm, "lrm"), (sel_t, "sel_t"), (sel_u3, "sel_u3"), (sel_f, "sel_f"),
                                         (thr, "thr"), (w2r, "w2r"), (w3r, "w3r"), (iw, "iw"), (be, "be"), (vet, "vet")):
                            d = dst[:, :, :] if len(dst.shape) == 3 else dst[:, :]
                            sp.dma_start(d, a[src]).then_inc(s["c"], 16)
                        sp.dma_start(xf[:, 1], x_b[1]).then_inc(s_x[1], 16)

                        def step(i, par, p, load):
                            if load:
                                sp.wait_ge(s["tr"], 4 * i)
                                sp.dma_start(xf[:, 1 - par], x_b[i + 1]).then_inc(s_x[1 - par], 16)
                            if p is not None:
                                sp.wait_ge(s["lrl"], 2 * p + 2)
                                for g in range(2):
                                    sp.dma_start(lr_d[p, :, g], lrt[64 * g:64 * g + 48, :]).then_inc(s["lrst"], 16)
                                for t in range(NT):
                                    sp.wait_ge(s["yl"], 8 * p + t + 1)
                                    sp.dma_start(y_d[p, :, t], yt[:, t % 2, :, :]).then_inc(s_yst[t % 2], 16)

                        step(1, 1, 0, True)
                        with sp.Fori(1, B // 2 - 1) as d:
                            step(2 * d, 0, 2 * d - 1, True)
                            step(2 * d + 1, 1, 2 * d, True)
                        step(B - 2, 0, B - 3, True)
                        step(B - 1, 1, B - 2, False)
                        step(None, 0, B - 1, False)
                        sp.wait_ge(s["lrst"], 32 * B)
                        for h in range(2):
                            sp.wait_ge(s_yst[h], 16 * B * NT // 2)

                    @block.gpsimd
                    def _(pool):
                        nc.gpsimd.memset(ones[:, :], 1.0 / N).then_inc(s_rootc, 1)
                        nc.gpsimd.memset(amax[:, :], 0.0).then_inc(s_rootc, 1)
                        nc.gpsimd.memset(klf[:, :, :], 0.0).then_inc(s_rootc, 1)
                        nc.gpsimd.memset(rg[:, :], 0.0).then_inc(s_rootc, 1)
                        nc.gpsimd.memset(sgt[:, :], 0.0).then_inc(s_rootc, 1)
                        pool.dma_start(cheb[:, 1], a["vst"].rearrange("(t p) n -> p t n", p=P)).then_inc(s["vs"], 16)
                        pool.wait_ge(s["aA"], 4)
                        nc.gpsimd.partition_all_reduce(am_all[:, 0:4], amax[:, 0:4], P, ABSMAX).then_inc(s["allA"], 1)
                        for k in (0, 2):
                            pool.dma_start(cheb[:, k], a["cheb"][:, k]).then_inc(s["cheb"], 16)
                        pool.dma_start(gstage[:, :, :], a["gt"].rearrange("(t p) e -> p t e", p=P)).then_inc(s["gd"], 16)
                        pool.wait_ge(s["aB"], 1)
                        nc.gpsimd.partition_all_reduce(am_all[:, VS:VS + 1], amax[:, VS:VS + 1], P, ABSMAX).then_inc(s["allB"], 1)
                        pool.dma_start(wstage[:, :], a["wt"][P:2 * P, :]).then_inc(s["w"], 16)

                        def x_low(i, par):
                            pool.wait_ge(s["xth"], i + 1)
                            nc.gpsimd.tensor_tensor(xt[:, par, 1], xr[:, :, :], xt[:, par, 0], ALU.subtract).then_inc(s["xtl"], 1)

                        x_low(0, 0)
                        x_low(1, 1)
                        pool.wait_ge(s["vl"], 1)
                        pool.dma_start(cheb[:, 1], a["cheb"][:, 1]).then_inc(s["cheb"], 16)
                        with pool.Fori(1, B // 2 - 1) as d:
                            x_low(2 * d, 0)
                            x_low(2 * d + 1, 1)
                            pool.wait_ge(s["wmax"], d)
                            pool.dma_start(wstage[:, :], a["wt"].rearrange("(t p) o -> t p o", p=P)[d + 1]).then_inc(s["w"], 16)
                        x_low(B - 2, 0)
                        x_low(B - 1, 1)
                        pool.wait_ge(s["wmax"], NT - 1)
                        pool.dma_start(wstage[:, :], a["wt"][0:P, :]).then_inc(s["w"], 16)
                        pool.wait_ge(s["aC"], 3)
                        nc.gpsimd.partition_all_reduce(am_all[:, CHEB:8], amax[:, CHEB:8], P, ABSMAX).then_inc(s["allC"], 1)

                    @block.vector
                    def _(dve):
                        def linker(sem_):
                            count = [0]

                            def link(ins):
                                count[0] += 1
                                ins.then_inc(sem_, 1)
                                dve.wait_ge(sem_, count[0])
                            return link

                        def powers(link, lo, hi):
                            link(nc.vector.tensor_scalar(am_all[:, lo:hi], am_all[:, lo:hi], 1e-30, None, ALU.max))
                            link(nc.vector.tensor_scalar(p2[:, lo:hi].bitcast(u32), am_all[:, lo:hi].bitcast(u32), 0x7F800000,
                                                         None, ALU.bitwise_and))
                            link(nc.vector.reciprocal(rp2[:, lo:hi], p2[:, lo:hi]))

                        dve.wait_ge(s["c"], 16 * 12)
                        dve.wait_ge(s_rootc, 5)
                        nc.vector.tensor_reduce(amax[0:HC, THETA:THETA + 1], thr[:, :, :], AX.XY, ALU.max,
                                                apply_absolute_value=True).then_inc(s["aA"], 1)
                        nc.vector.tensor_copy(amax[0:T, W1:W1 + 1], iw[:, 12:13]).then_inc(s["aA"], 1)
                        nc.vector.tensor_reduce(amax[0:HC, W2:W2 + 1], w2r[:, :], AX.X, ALU.max,
                                                apply_absolute_value=True).then_inc(s["aA"], 1)
                        nc.vector.tensor_copy(amax[0:HC, W3:W3 + 1], w3r[:, :]).then_inc(s["aA"], 1)
                        dve.wait_ge(s["uas"], 1)
                        nc.vector.tensor_scalar(uas[:, :], p_s[0:HC, 0:18], float(N), None, ALU.mult).then_inc(s["uasc"], 1)
                        dve.wait_ge(s["allA"], 1)
                        link = linker(s["pA"])
                        powers(link, THETA, W3 + 1)
                        link(nc.vector.tensor_tensor(fac[:, 5:6], p2[:, W1:W1 + 1], p2[:, W2:W2 + 1], ALU.mult))
                        link(nc.vector.tensor_tensor(fac[:, 0:1], fac[:, 5:6], p2[:, W3:W3 + 1], ALU.mult))
                        link(nc.vector.tensor_scalar(lrm[:, :], lrm[:, :], 1.0 / (X_UP * K_UP), None, ALU.mult))
                        link(nc.vector.tensor_scalar(thr[:, :, :], thr[:, :, :], rp2[0:HC, THETA:THETA + 1], None, ALU.mult))
                        link(nc.vector.tensor_scalar(w2r[:, :], w2r[:, :], rp2[0:HC, W2:W2 + 1], None, ALU.mult))
                        link(nc.vector.tensor_scalar(w3r[:, :], w3r[:, :], rp2[0:HC, W3:W3 + 1], None, ALU.mult))
                        link(nc.vector.tensor_scalar(iw[:, 12:13], iw[:, 12:13], rp2[0:T, W1:W1 + 1], None, ALU.mult))

                        def lr_low(p, h):
                            if p is None:
                                return
                            dve.wait_ge(s["lrh"], 2 * p + h + 1)
                            wait(dve, s["lrst"], 32 * p)
                            nc.vector.scalar_tensor_tensor(lrt[:, 512 * h:512 * h + 512], p_t[0:112, h, :], 1.0 / (X_UP * K_UP),
                                                           mh[:, :], ALU.mult, ALU.subtract).then_inc(s["lrl"], 1)

                        def y_low(p, t):
                            if p is None:
                                return
                            dve.wait_ge(s["yh"], 8 * p + t + 1)
                            nc.vector.scalar_tensor_tensor(
                                yt[:, t % 2, 1, :].rearrange("p (h c) -> p h c", h=2), p_y[:, t % 2, :, 0:KC // 2],
                                Y_UP / (X_UP * K_UP), yt[:, t % 2, 0, :].rearrange("p (h c) -> p h c", h=2),
                                ALU.mult, ALU.subtract).then_inc(s["yl"], 1)

                        def tables(part, d):
                            if part == 1:
                                dve.wait_ge(s["cheb"], 16 * K)
                                nc.vector.tensor_reduce(chmax[:, bass.ts(d, 1)], cheb[:, :, :, :].rearrange("p k t j -> p (k t j)")
                                                        [:, bass.ts(d, K * NT * N // 8)], AX.X, ALU.max,
                                                        apply_absolute_value=True).then_inc(s["chmax"], 1)
                            else:
                                dve.wait_ge(s["w"], 16 * NT if isinstance(d, int) else 16 * d)
                                nc.vector.tensor_reduce(wmax[:, bass.ts(d, 1)], wstage[:, :], AX.X, ALU.max,
                                                        apply_absolute_value=True).then_inc(s["wmax"], 1)

                        def step(i, par, p, d):
                            if i is not None:
                                dve.wait_ge(s["cp"], 4 * i + 4)
                                nc.vector.tensor_reduce(sm2[:, :], sm[:, :, :], AX.X, ALU.add).then_inc(s["sm2"], 1)
                                dve.wait_ge(s["sm2"], i + 1)
                                wait(dve, s["sq"], 2 * i)
                                nc.vector.tensor_scalar(nmean[:, :], sm2[:, :], -1.0 / N, None, ALU.mult).then_inc(s["nmean"], 1)
                            if i is None:
                                lr_low(p, 0)
                                y_low(p, 0)
                                lr_low(p, 1)
                                for t in range(1, NT):
                                    y_low(p, t)
                                tables(0, 0)
                                tables(1, 0)
                                return
                            dve.wait_ge(s["sq"], 2 * i + 2)
                            newton_rsqrt(dve, ss[:, :], 1.0 / N, nv[:, :], nb[:, :], ng[:, :], nh[:, :], s["newt"],
                                         NEWTON * i, 1e-6)
                            nc.vector.tensor_scalar(rs[:, :], ng[:, :], X_UP, None, ALU.mult).then_inc(s["rs"], 1)
                            dve.wait_ge(s["rs"], i + 1)
                            nc.vector.tensor_tensor(nmr[:, :], nmean[:, :], rs[:, :], ALU.mult).then_inc(s["nmr"], 1)
                            dve.wait_ge(s["q"], i + 1)
                            for h in range(2):
                                nc.vector.scalar_tensor_tensor(qt[:, h, :], uas[:, :], nmean[:, h:h + 1], p_s[0:HC, 64 * h:64 * h + 18],
                                                               ALU.mult, ALU.add).then_inc(s["qt"], 1)
                            dve.wait_ge(s["qt"], 2 * i + 2)
                            wait(dve, s["rg"], i)
                            nc.vector.tensor_tensor(qs[:, :, :], qt[:, :, :], ng[:, :].unsqueeze(2).broadcast_to([HC, 2, 18]),
                                                    ALU.mult).then_inc(s["qs"], 1)
                            dve.wait_ge(s["qs"], i + 1)
                            nc.vector.tensor_tensor(dg[:, :, :], sel_f[:, :].unsqueeze(1).broadcast_to([HC, 2, F]),
                                                    qs[:, :, 16:17].broadcast_to([HC, 2, F]), ALU.mult).then_inc(s["dg"], 1)
                            lr_low(p, 0)
                            y_low(p, 0)
                            lr_low(p, 1)
                            y_low(p, 1)
                            dve.wait_ge(s["rg"], i + 1)
                            wait(dve, s["prod"], i)
                            nc.vector.tensor_copy(rg[:, 0:32].rearrange("p (a t) -> p a t", a=2)[:, :, 0:T],
                                                  p_e[0:F, 0:32].rearrange("p (a t) -> p a t", a=2)[:, :, 0:T]).then_inc(s["rgs"], 1)
                            dve.wait_ge(s["nmr"], i + 1)
                            for h in range(2):
                                nc.vector.tensor_scalar(xr[:, h, :], xr[:, h, :], rs[:, h:h + 1], nmr[:, h:h + 1],
                                                        ALU.mult, ALU.add).then_inc(s["v"], 1)
                            y_low(p, 2)
                            dve.wait_ge(s["prod"], i + 1)
                            wait(dve, s["tanh"], i)
                            nc.vector.tensor_tensor(zt[:, :], p_e[0:T, 32:32 + T], be[:, :], ALU.add).then_inc(s["zt"], 1)
                            dve.wait_ge(s["tanh"], i + 1)
                            wait(dve, s["el"], i)
                            nc.vector.tensor_scalar(sgt[:, 0:T], tht[:, :], 0.5, 0.5, ALU.mult, ALU.add).then_inc(s["sg"], 1)
                            y_low(p, 3)
                            dve.wait_ge(s["el"], i + 1)
                            wait(dve, s["eex"], i)
                            nc.vector.tensor_reduce(emx[:, :], p_e[0:T, 48:48 + T], AX.X, ALU.max, negate=True).then_inc(s["emx"], 1)
                            y_low(p, 4)
                            dve.wait_ge(s["eex"], i + 1)
                            nc.vector.reciprocal(erc[:, :], esm[:, :]).then_inc(s["erc"], 1)
                            dve.wait_ge(s["erc"], i + 1)
                            nc.vector.tensor_scalar(et[:, :], eex[:, :], erc[:, 0:1], None, ALU.mult).then_inc(s["et"], 1)
                            dve.wait_ge(s["et"], i + 1)
                            wait(dve, s["erep"], i)
                            nc.vector.tensor_copy(etr[:, :, :, :].rearrange("p h t f -> p (h t) f"),
                                                  et[:, :].unsqueeze(2).broadcast_to([T, T, F])).then_inc(s["etr"], 1)
                            y_low(p, 5)
                            dve.wait_ge(s["erep"], i + 1)
                            nc.vector.tensor_copy(er[:, :, :], p_e[0:HC, 64:96].rearrange("p (h u) -> p h u", h=2)).then_inc(s["er"], 1)
                            dve.wait_ge(s["er"], i + 1)
                            wait(dve, s["klh"], i)
                            wait(dve, s["kll"], i)
                            for h in range(2):
                                nc.vector.tensor_scalar(klf[:, h, 0:48], w2r[:, :], er[:, h, 12:13], None, ALU.mult).then_inc(s["klf"], 1)
                            nc.vector.tensor_scalar(klf[:, :, 64:112].rearrange("p h (g u) -> p h g u", g=4),
                                                    er[:, :, 0:12].unsqueeze(2).broadcast_to([HC, 2, 4, T]),
                                                    w3r[:, 0:1], None, ALU.mult).then_inc(s["klf"], 1)
                            wait(dve, s["kh"], i)
                            wait(dve, s["kl"], i)
                            for h in range(2):
                                nc.vector.tensor_tensor(kf[:, h], er[:, h, 0:12].unsqueeze(1).unsqueeze(3).broadcast_to([HC, K, T, F]),
                                                        thr[:, :, :].unsqueeze(2).broadcast_to([HC, K, T, F]), ALU.mult).then_inc(s["kf"], 1)
                            dve.wait_ge(s["klh"], i + 1)
                            nc.vector.scalar_tensor_tensor(kl[:, par, 1], klf[:, :, :], K_UP, kl[:, par, 0], ALU.mult,
                                                           ALU.subtract).then_inc(s["kll"], 1)
                            y_low(p, 6)
                            dve.wait_ge(s["kh"], i + 1)
                            nc.vector.scalar_tensor_tensor(kx[:, par, 1], kf[:, :, :, :, :].rearrange("p h k u o -> p h (k u o)"), K_UP,
                                                           kx[:, par, 0], ALU.mult, ALU.subtract).then_inc(s["kl"], 1)
                            y_low(p, 7)
                            if isinstance(i, int) and i == 0:
                                dve.wait_ge(s["vs"], 16)
                                nc.vector.tensor_reduce(amax[:, VS:VS + 1], cheb[:, 1], AX.XY, ALU.max,
                                                        apply_absolute_value=True).then_inc(s["aB"], 1)
                                dve.wait_ge(s["allB"], 1)
                                link = linker(s["pB"])
                                powers(link, VS, VS + 1)
                                link(nc.vector.tensor_scalar(fac[:, 1:2], p2[:, VS:VS + 1], 1.0 / (V_UP * SIG_UP), None, ALU.mult))
                                link(nc.vector.tensor_scalar(fac[:, 4:5], rp2[:, VS:VS + 1], V_UP, None, ALU.mult))
                            elif isinstance(i, int):
                                dve.wait_ge(s["vh"], 1)
                                nc.vector.scalar_tensor_tensor(vt[:, 1], cheb[:, 1], fac[:, 4:5], vt[:, 0],
                                                               ALU.mult, ALU.subtract).then_inc(s["vl"], 1)
                            else:
                                tables(par, d)

                        batch_steps(dve, step)
                        dve.wait_ge(s["gd"], 16)
                        nc.vector.tensor_reduce(amax[:, GD:GD + 1], gstage[:, :, :], AX.XY, ALU.max, apply_absolute_value=True).then_inc(s["aC"], 1)
                        dve.wait_ge(s["chmax"], 8)
                        nc.vector.tensor_reduce(amax[:, CHEB:CHEB + 1], chmax[:, :], AX.X, ALU.max).then_inc(s["aC"], 1)
                        dve.wait_ge(s["wmax"], 8)
                        nc.vector.tensor_reduce(amax[:, WB:WB + 1], wmax[:, :], AX.X, ALU.max).then_inc(s["aC"], 1)
                        dve.wait_ge(s["allC"], 1)
                        link = linker(s["pC"])
                        powers(link, CHEB, 8)
                        link(nc.vector.tensor_scalar(fac[:, 2:3], rp2[:, CHEB:CHEB + 1], CH_UP, None, ALU.mult))
                        link(nc.vector.scalar_tensor_tensor(fac[:, 3:4], p2[:, CHEB:CHEB + 1], 1.0 / (CH_UP * Y_UP),
                                                            p2[:, THETA:THETA + 1], ALU.mult, ALU.mult))

                    @block.scalar
                    def _(act):
                        def lr_high(p, h):
                            if p is None:
                                return
                            act.wait_ge(s["lr"], 2 * p + h + 1)
                            wait(act, s["lrl"], 2 * p + h)
                            nc.scalar.activation(mh[:, :], p_t[0:112, h, :], ACT.Copy, scale=lrm[0:112, 0:1]).then_inc(s["lrh"], 1)

                        def y_high(p, t):
                            if p is None:
                                return
                            act.wait_ge(s["y"], 8 * p + t + 1)
                            wait(act, s_yst[t % 2], 64 * p + 16 * (t // 2))
                            nc.scalar.activation(yt[:, t % 2, 0, :].rearrange("p (h c) -> p h c", h=2),
                                                 p_y[:, t % 2, :, 0:KC // 2], ACT.Copy,
                                                 scale=Y_UP / (X_UP * K_UP)).then_inc(s["yh"], 1)

                        def step(i, par, p, d):
                            if i is not None:
                                wait(act, s["xtl"], i)
                                for r in range(4):
                                    act.wait_ge(s["tr"], 4 * i + r + 1)
                                    h, q = r // 2, r % 2
                                    nc.scalar.activation(xr[:, h, 512 * q:512 * q + 512], p_t[0:HC, q, :], ACT.Copy,
                                                         accum_out=sm[:, h, q:q + 1]).then_inc(s["cp"], 1)
                            if i is None:
                                lr_high(p, 0)
                                y_high(p, 0)
                                lr_high(p, 1)
                                for t in range(1, NT):
                                    y_high(p, t)
                                return
                            act.wait_ge(s["nmean"], i + 1)
                            for h in range(2):
                                wait(act, s["sq"], 2 * i + h)
                                nc.scalar.activation(junk[:, :], xr[:, h, :], ACT.Square, bias=nmean[:, h:h + 1],
                                                     accum_out=ss[:, h:h + 1]).then_inc(s["sq"], 1)
                            lr_high(p, 0)
                            y_high(p, 0)
                            lr_high(p, 1)
                            y_high(p, 1)
                            y_high(p, 2)
                            act.wait_ge(s["zt"], i + 1)
                            wait(act, s["sg"], i)
                            nc.scalar.activation(tht[:, :], zt[:, :], ACT.Tanh, scale=0.5).then_inc(s["tanh"], 1)
                            y_high(p, 3)
                            act.wait_ge(s["v"], 2 * i + 2)
                            wait(act, s["y"], 8 * (i - 1))
                            nc.scalar.activation(xt[:, par, 0], xr[:, :, :], ACT.Copy).then_inc(s["xth"], 1)
                            act.wait_ge(s["emx"], i + 1)
                            wait(act, s["et"], i)
                            nc.scalar.activation(eex[:, :], p_e[0:T, 48:48 + T], ACT.Exp, bias=emx[:, 0:1],
                                                 accum_out=esm[:, :]).then_inc(s["eex"], 1)
                            y_high(p, 4)
                            y_high(p, 5)
                            act.wait_ge(s["klf"], 3 * i + 3)
                            nc.scalar.activation(kl[:, par, 0], klf[:, :, :], ACT.Copy, scale=K_UP).then_inc(s["klh"], 1)
                            act.wait_ge(s["kf"], 2 * i + 2)
                            nc.scalar.activation(kx[:, par, 0], kf[:, :, :, :, :].rearrange("p h k u o -> p h (k u o)"), ACT.Copy,
                                                 scale=K_UP).then_inc(s["kh"], 1)
                            y_high(p, 6)
                            y_high(p, 7)
                            if isinstance(i, int) and i == 1:
                                act.wait_ge(s["pB"], 5)
                                nc.scalar.activation(vt[:, 0], cheb[:, 1], ACT.Copy, scale=fac[:, 4:5]).then_inc(s["vh"], 1)

                        act.wait_ge(s["pA"], 10)
                        batch_steps(act, step)

                    @block.tensor
                    def _(pe):
                        def lr(p, pp, h):
                            n = 0
                            for half in range(2):
                                for w, m in ((0, 0), (0, 1), (1, 0)):
                                    last = nc.tensor.matmul(p_t[:, h, :], kl[:, pp, w, half, :], xt[:, pp, m, half, 512 * h:512 * h + 512],
                                                            start=(n == 0), stop=(n == 5))
                                    n += 1
                            last.then_inc(s["lr"], 1)

                        def y(p, pp, t):
                            if p is None:
                                return
                            wait(pe, s["yl"], 8 * p + t - 1)
                            n = 0
                            for half in range(2):
                                for w, m in ((0, 0), (0, 1), (1, 0)):
                                    for c in range(2):
                                        last = nc.tensor.matmul(p_y[:, t % 2, c, 0:KC // 2], xt[:, pp, w, half, t * P:(t + 1) * P],
                                                                kx[:, pp, m, half, c * (KC // 2):(c + 1) * (KC // 2)],
                                                                start=(n == 0), stop=(n == 5))
                                    n += 1
                            last.then_inc(s["y"], 1)

                        def transposes(i, par, r):
                            if r >= 2:
                                pe.wait_ge(s["cp"], 4 * i + r - 1)
                            h, q = r // 2, r % 2
                            for t in range(4):
                                last = nc.tensor.transpose(p_t[0:HC, q, t * P:(t + 1) * P],
                                                           xf[:, par, 4 * q + t, h * HC:(h + 1) * HC], ident[:, :])
                            last.then_inc(s["tr"], 1)

                        def step(i, par, p, d):
                            pp = 1 - par
                            if i is not None:
                                if isinstance(i, int):
                                    pe.wait_ge(s_x[par], 16 * (i // 2) + 16)
                                else:
                                    pe.wait_ge(s_x[par], 16 * d + 16)
                                if p is not None:
                                    wait(pe, s["lrl"], 2 * p)
                                transposes(i, par, 0)
                                transposes(i, par, 1)
                                wait(pe, s["qt"], 2 * i)
                                for h in range(2):
                                    for t in range(NT):
                                        last = nc.tensor.matmul(p_s[0:HC, 64 * h:64 * h + 18], xf[:, par, t, h * HC:(h + 1) * HC], ua[:, t, :],
                                                                start=(t == 0), stop=(t == NT - 1))
                                last.then_inc(s["q"], 1)
                                transposes(i, par, 2)
                                transposes(i, par, 3)
                            if p is not None:
                                pe.wait_ge(s["kll"], p + 1)
                                pe.wait_ge(s["xtl"], p + 1)
                                if i is not None:
                                    pe.wait_ge(s["cp"], 4 * i + 3)
                                lr(p, pp, 0)
                                if i is not None:
                                    pe.wait_ge(s["cp"], 4 * i + 4)
                                lr(p, pp, 1)
                                pe.wait_ge(s["kl"], p + 1)
                            y(p, pp, 0)
                            y(p, pp, 1)
                            if i is not None:
                                pe.wait_ge(s["dg"], i + 1)
                                wait(pe, s["er"], i)
                                for h in range(2):
                                    nc.tensor.matmul(p_e[0:F, 0:T], qs[:, h, 0:F], sel_u3[:, h, :], start=(h == 0), stop=(h == 1))
                                for h in range(2):
                                    last = nc.tensor.matmul(p_e[0:F, 16:16 + T], dg[:, h, :], sel_t[:, h, :], start=(h == 0), stop=(h == 1))
                                last.then_inc(s["rg"], 1)
                            y(p, pp, 2)
                            if i is not None:
                                pe.wait_ge(s["rgs"], i + 1)
                                nc.tensor.matmul(p_e[0:64, 32:32 + T], rg[:, 16:80], rg[:, 0:T], start=True, stop=True).then_inc(s["prod"], 1)
                            y(p, pp, 3)
                            if i is not None:
                                pe.wait_ge(s["sg"], i + 1)
                                nc.tensor.matmul(p_e[0:64, 48:48 + T], sgt[:, :], vet[:, :], start=True, stop=True).then_inc(s["el"], 1)
                            y(p, pp, 4)
                            y(p, pp, 5)
                            if i is not None:
                                pe.wait_ge(s["etr"], i + 1)
                                for h in range(2):
                                    last = nc.tensor.matmul(p_e[0:HC, 64 + 16 * h:64 + 16 * h + 16],
                                                            etr[:, h].rearrange("p t f -> p (t f)"), iw[:, :], start=True, stop=True)
                                last.then_inc(s["erep"], 1)
                            y(p, pp, 6)
                            y(p, pp, 7)

                        pe.wait_ge(s_rootc, 5)
                        pe.wait_ge(s["c"], 16 * 12)
                        for t in range(NT):
                            last = nc.tensor.matmul(p_s[0:HC, 0:18], ones[:, 0:HC], ua[:, t, :], start=(t == 0), stop=(t == NT - 1))
                        last.then_inc(s["uas"], 1)
                        pe.wait_ge(s["uasc"], 1)
                        pe.wait_ge(s["pA"], 10)
                        batch_steps(pe, step)


            with ExitStack() as st:
                sb, ps, sem = make(st)
                bst = sb("bs_tile", [P, 2, NT, P])
                lr = sb("lr", [P, 2, N], f16)
                z = sb("z", [P, NT, P])
                sig = sb("sig", [P, 2, 2, NT, P], f16)
                et2 = sb("e_t", [P, N])
                mx = sb("mx", [P, 2])
                nmx = sb("nmx", [P, 2])
                den = sb("den", [P, 2])
                rden = sb("rden", [P, 2])
                oscale = sb("oscale", [P, 2])
                pk = sb("p_k", [P, K, NT, P])
                pkx = sb("p_split", [P, 2, K, NT, P], f16)
                yx = sb("y_split", [P, NT, 2, KC], f16)
                conv = sb("conv", [P, 2, C])
                xres = sb("x_res", [P, 2, C])
                x2t = sb("x2_tile", [P, 2, C])

                p_a = ps("p_a", [P, 2, 512])
                p_b = ps("p_b", [P, 2 * 512])
                p_c = ps("p_c", [P, NT, P])
                p_d = ps("p_d", [P, 2, 512])

                s_prod = sem("s2_prod")
                s_z = sem("s2_z")
                s_tanh = sem("s2_tanh")
                s_sig = sem("s2_sig")
                s_sigh = sem("s2_sigh")
                s_sigl = sem("s2_sigl")
                s_logit = sem("s2_logit")
                s_max = sem("s2_max")
                s_nmax = sem("s2_nmax")
                s_exp = sem("s2_exp")
                s_rden = sem("s2_rden")
                s_osc = sem("s2_osc")
                s_tr = sem("s2_tr")
                s_pk = sem("s2_pk")
                s_pkh = sem("s2_pkh")
                s_pkl = sem("s2_pkl")
                s_conv = sem("s2_conv")
                s_relu = sem("s2_relu")
                s_x2 = sem("s2_x2")
                s_lrpad = sem("s2_lrpad")
                s_lr = sem("s2_lr")
                s_y = [sem(f"s2_y{t}") for t in range(NT)]
                s_bs = [sem(f"s2_bs{i}") for i in range(2)]
                s_xres = [sem(f"s2_xres{i}") for i in range(2)]
                s_st = [sem(f"s2_store{i}") for i in range(2)]

                def batches(eng, slot, first_slot):
                    first_slot()
                    for j in range(NT):
                        slot(0, j, j == 0, False)
                    with eng.Fori(1, B - 1) as b:
                        for j in range(NT):
                            slot(b, j, False, False)
                    for j in range(NT):
                        slot(B - 1, j, False, j == NT - 1)

                with nc.Block() as block:
                    @block.sync
                    def _(sp):
                        def load_lr(b):
                            sp.dma_start(lr[0:48, :, :], lr_d[b]).then_inc(s_lr, 16)

                        def load_bs(j):
                            sp.dma_start(bst[:, j % 2], a["bs"][j % NT]).then_inc(s_bs[j % 2], 16)

                        def store(b, j):
                            wait(sp, s_x2, 8 * b + j + 1)
                            sp.dma_start(x2_b[b, :, j], x2t[:, j % 2]).then_inc(s_st[j % 2], 16)

                        def begin():
                            sp.wait_ge(s_lrpad, 1)
                            load_lr(0)
                            load_bs(0)
                            load_bs(1)

                        def slot(b, j, first, last):
                            if not (first or last) and not (isinstance(b, int) and b == B - 1 and j >= NT - 2):
                                pass
                            more = not (isinstance(b, int) and b == B - 1 and j + 2 >= NT)
                            if more:
                                wait(sp, s_z, 16 * b + 2 * j + 2)
                                load_bs(j + 2)
                            if not (isinstance(b, int) and b == 0 and j < 2):
                                if j >= 2:
                                    store(b, j - 2)
                                else:
                                    store(b - 1, j + 6)
                            sp.dma_start(xres[:, j % 2], x_b[b, :, j]).then_inc(s_xres[j % 2], 16)
                            if j == 1:
                                wait(sp, s_conv, 8 * b)
                                for t in range(NT):
                                    sp.dma_start(yx[:, t], y_d[b, :, t]).then_inc(s_y[t], 16)
                            if j == NT - 2 and not (isinstance(b, int) and b == B - 1):
                                wait(sp, s_prod, 16 * b + 16)
                                load_lr(b + 1)

                        batches(sp, slot, begin)
                        store(B - 1, NT - 2)
                        store(B - 1, NT - 1)
                        for h in range(2):
                            sp.wait_ge(s_st[h], 16 * B * NT // 2)

                    @block.gpsimd
                    def _(pool):
                        nc.gpsimd.memset(lr[:, :, :], 0.0).then_inc(s_lrpad, 1)

                        def sig_low(b, j):
                            wait(pool, s_sigh, 8 * b + j + 1)
                            nc.gpsimd.tensor_tensor(sig[:, j % 2, 1], z[:, :, :], sig[:, j % 2, 0], ALU.subtract).then_inc(s_sigl, 1)

                        def add(b, j):
                            wait(pool, s_relu, 8 * b + j + 1)
                            wait(pool, s_xres[j % 2], 64 * b + 16 * (j // 2) + 16)
                            wait(pool, s_st[j % 2], 64 * b + 16 * (j // 2))
                            nc.gpsimd.tensor_tensor(x2t[:, j % 2], conv[:, j % 2], xres[:, j % 2], ALU.add).then_inc(s_x2, 1)

                        def slot(b, j, first, last):
                            if not last:
                                sig_low(b + (j + 1) // NT, (j + 1) % NT)
                            if not first:
                                add(b - (j == 0), (j - 1) % NT)

                        batches(pool, slot, lambda: sig_low(0, 0))
                        add(B - 1, NT - 1)

                    @block.vector
                    def _(dve):
                        def add_bs(b, j):
                            n = 8 * b + j
                            wait(dve, s_sigl, n)
                            wait(dve, s_bs[j % 2], 64 * b + 16 * (j // 2) + 16)
                            for h in range(2):
                                wait(dve, s_prod, 2 * n + h + 1)
                                nc.vector.scalar_tensor_tensor(
                                    z[:, 4 * h:4 * h + 4, :].rearrange("p t v -> p (t v)"), p_a[:, h, :], fac[:, 0:1],
                                    bst[:, j % 2, 4 * h:4 * h + 4, :].rearrange("p t v -> p (t v)"),
                                    ALU.mult, ALU.add).then_inc(s_z, 1)

                        def mask(b, j):
                            n = 8 * b + j
                            wait(dve, s_tr, n + 1)
                            for k in range(K):
                                wait(dve, s_pkl, 3 * n - 2 + k)
                                nc.vector.scalar_tensor_tensor(pk[:, k], cheb[:, k, :, j * P:(j + 1) * P], fac[:, 2:3],
                                                               p_c[:, :, :], ALU.mult, ALU.mult).then_inc(s_pk, 1)
                                if k:
                                    low(b, j, k - 1)
                            low(b, j, K - 1)

                        def low(b, j, k):
                            n = 8 * b + j
                            wait(dve, s_pkh, 3 * n + k + 1)
                            wait(dve, s_conv, n)
                            nc.vector.tensor_tensor(pkx[:, 1, k], pk[:, k], pkx[:, 0, k], ALU.subtract).then_inc(s_pkl, 1)

                        def row_max(b, j):
                            n = 8 * b + j
                            wait(dve, s_logit, n + 1)
                            wait(dve, s_nmax, n - 1)
                            nc.vector.tensor_reduce(mx[:, j % 2:j % 2 + 1], p_b[:, :], AX.X, ALU.max, negate=True).then_inc(s_max, 1)
                            wait(dve, s_max, n + 1)
                            wait(dve, s_exp, n - 1)
                            nc.vector.tensor_scalar(nmx[:, j % 2:j % 2 + 1], mx[:, j % 2:j % 2 + 1], fac[:, 1:2], None,
                                                    ALU.mult).then_inc(s_nmax, 1)

                        def row_scale(b, j):
                            n = 8 * b + j
                            wait(dve, s_exp, n + 1)
                            nc.vector.reciprocal(rden[:, j % 2:j % 2 + 1], den[:, j % 2:j % 2 + 1]).then_inc(s_rden, 1)
                            wait(dve, s_rden, n + 1)
                            wait(dve, s_relu, n - 1)
                            nc.vector.tensor_scalar(oscale[:, j % 2:j % 2 + 1], rden[:, j % 2:j % 2 + 1], fac[:, 3:4], None,
                                                    ALU.mult).then_inc(s_osc, 1)

                        def slot(b, j, first, last):
                            if not last:
                                add_bs(b + (j + 1) // NT, (j + 1) % NT)
                            if not first:
                                mask(b - (j == 0), (j - 1) % NT)
                            row_max(b, j)
                            row_scale(b, j)

                        batches(dve, slot, lambda: add_bs(0, 0))
                        mask(B - 1, NT - 1)

                    @block.scalar
                    def _(act):
                        def tanh(b, j):
                            n = 8 * b + j
                            wait(act, s_z, 2 * n + 2)
                            nc.scalar.activation(z[:, :, :], z[:, :, :], ACT.Tanh, scale=0.5).then_inc(s_tanh, 1)

                        def sig_high(b, j):
                            n = 8 * b + j
                            wait(act, s_tanh, n + 1)
                            nc.scalar.activation(z[:, :, :], z[:, :, :], ACT.Copy, scale=SIG_UP / 2, bias=SIG_UP / 2).then_inc(s_sig, 1)
                            wait(act, s_sig, n + 1)
                            wait(act, s_logit, n - 1)
                            nc.scalar.activation(sig[:, j % 2, 0], z[:, :, :], ACT.Copy).then_inc(s_sigh, 1)

                        def high(b, j, k):
                            n = 8 * b + j
                            wait(act, s_pk, 3 * n + k + 1)
                            wait(act, s_conv, n)
                            nc.scalar.activation(pkx[:, 0, k], pk[:, k], ACT.Copy).then_inc(s_pkh, 1)

                        def exp(b, j):
                            n = 8 * b + j
                            wait(act, s_nmax, n + 1)
                            wait(act, s_tr, n)
                            wait(act, s_rden, n - 1)
                            nc.scalar.activation(et2[:, :], p_b[:, :], ACT.Exp, bias=nmx[:, j % 2:j % 2 + 1], scale=fac[:, 1:2],
                                                 accum_out=den[:, j % 2:j % 2 + 1]).then_inc(s_exp, 1)

                        def relu(b, j):
                            n = 8 * b + j
                            wait(act, s_conv, n + 1)
                            wait(act, s_osc, n + 1)
                            wait(act, s_x2, n - 1)
                            nc.scalar.activation(conv[:, j % 2], p_d[:, j % 2, 0:C], ACT.Relu,
                                                 scale=oscale[:, j % 2:j % 2 + 1]).then_inc(s_relu, 1)

                        def slot(b, j, first, last):
                            pb, pj = b - (j == 0), (j - 1) % NT
                            if not last:
                                tanh(b + (j + 1) // NT, (j + 1) % NT)
                            if not first:
                                high(pb, pj, 0)
                            if not last:
                                sig_high(b + (j + 1) // NT, (j + 1) % NT)
                            if not first:
                                high(pb, pj, 1)
                                high(pb, pj, 2)
                            exp(b, j)
                            if not first:
                                relu(pb, pj)

                        def begin():
                            tanh(0, 0)
                            sig_high(0, 0)

                        batches(act, slot, begin)
                        for k in range(K):
                            high(B - 1, NT - 1, k)
                        relu(B - 1, NT - 1)

                    @block.tensor
                    def _(pe):
                        def prod(b, j):
                            n = 8 * b + j
                            wait(pe, s_z, 2 * n)
                            if j == 0:
                                wait(pe, s_lr, 16 * b + 16)
                            for h in range(2):
                                for t in range(4):
                                    last = nc.tensor.matmul(p_a[:, h, t * P:(t + 1) * P], lr[:, 0, (4 * h + t) * P:(4 * h + t + 1) * P],
                                                            lr[:, 1, j * P:(j + 1) * P], start=True, stop=True)
                                last.then_inc(s_prod, 1)

                        def logits(b, j):
                            n = 8 * b + j
                            wait(pe, s_sigl, n + 1)
                            wait(pe, s_exp, n)
                            for t in range(NT):
                                for w, m in ((0, 0), (0, 1), (1, 0)):
                                    for c in range(2):
                                        last = nc.tensor.matmul(p_b[:, 512 * c:512 * c + 512], sig[:, j % 2, w, t],
                                                                vt[:, m, t, 512 * c:512 * c + 512],
                                                                start=(t == 0 and w == 0 and m == 0), stop=(t == NT - 1 and w == 1))
                            last.then_inc(s_logit, 1)

                        def transposes(b, j):
                            n = 8 * b + j
                            wait(pe, s_exp, n + 1)
                            wait(pe, s_pk, 3 * n)
                            for t in range(NT):
                                last = nc.tensor.transpose(p_c[:, t, :], et2[:, t * P:(t + 1) * P], ident[:, :])
                            last.then_inc(s_tr, 1)

                        def convolve(b, j):
                            n = 8 * b + j
                            wait(pe, s_pkl, 3 * n + 3)
                            wait(pe, s_relu, n - 1)
                            for t in range(NT):
                                if j == 0:
                                    wait(pe, s_y[t], 16 * b + 16)
                                for k in range(K):
                                    for w, m in ((0, 0), (0, 1), (1, 0)):
                                        last = nc.tensor.matmul(p_d[:, j % 2, 0:C], pkx[:, w, k, t], yx[:, t, m, k * C:(k + 1) * C],
                                                                start=(t == 0 and k == 0 and w == 0 and m == 0),
                                                                stop=(t == NT - 1 and k == K - 1 and w == 1))
                            last.then_inc(s_conv, 1)

                        def slot(b, j, first, last):
                            pb, pj = b - (j == 0), (j - 1) % NT
                            if not last:
                                prod(b + (j + 1) // NT, (j + 1) % NT)
                            if not first:
                                transposes(pb, pj)
                            logits(b, j)
                            if not first:
                                convolve(pb, pj)

                        batches(pe, slot, lambda: prod(0, 0))
                        transposes(B - 1, NT - 1)
                        convolve(B - 1, NT - 1)

        with ExitStack() as st:
            sb, ps, sem = make(st)
            wst = sb("w_stage", [P, NT, N])
            gst = sb("g_stage", [P, NT, GC])
            wx = sb("w_split", [P, 2, NT, N], f16)
            gx = sb("g_split", [P, 2, NT, GC], f16)
            upt = sb("up", [64, N])
            upf = sb("up_factor", [64, 1])
            gb = sb("gate_bias", [HC, EXP])
            iota = sb("iota", [HC, EXP])
            fc = sb("fc", [P, 8])
            x3 = sb("x3", [P, 2, NT, TOK])
            zc = sb("zc", [P, NT, TOK])
            sq3 = sb("sq3", [P, NT, TOK])
            zx = sb("z_split", [P, 2, 2, NT, TOK], f16)
            sums3 = sb("sums3", [P, TOK])
            sqs3 = sb("sqs3", [P, TOK])
            nv3 = sb("nv3", [P, TOK])
            nb3 = sb("nb3", [P, TOK])
            ng3 = sb("ng3", [P, TOK])
            nh3 = sb("nh3", [P, TOK])
            gl = sb("gl", [HC, TG, GC])
            top = sb("top", [HC, TG, 8])
            tix = sb("tix", [HC, TG, 8], u32)
            tixf = sb("tixf", [HC, TG, 2])
            dif = sb("dif", [HC, TG])
            ex2 = sb("ex2", [HC, TG])
            den2 = sb("den2", [HC, TG])
            wts = sb("wts", [HC, TG, 2])
            eq = sb("eq", [HC, TG * 2, EXP])
            eqw = sb("eqw", [HC, TG, 2, EXP])
            wgt = sb("wgt", [HC, TG, EXP])
            hw = sb("hw", [HC, TG, P])
            hwt = sb("hwt", [64, TOK])
            ob = sb("ob", [P, 4, TOK])

            p_o = ps("p_o", [P, 4, 512])
            p_m = ps("p_m", [P, 512])
            p_g = ps("p_g", [P, TG, GP])
            p_h = ps("p_h", [P, 512])

            names = ("c f wh wl gh gl upl x sum mean xc sq sqs var newt z zh zl gate glog top tix tixf dif ex2 den r w1 w2 "
                     "low eq eqw wgt hw hwtr hwt o oev oadd init z0").split()
            s = {n: sem("s3_" + n) for n in names}
            s_w = [sem(f"s3_wload{i}") for i in range(2)]
            s_x3 = [sem(f"s3_x{i}") for i in range(2)]
            s_out = [sem(f"s3_out{i}") for i in range(4)]
            x2_g = x2_d.rearrange("(g q) (t p) c -> g t p q c", q=2, p=P)
            out_g = out.rearrange("(g q) (t p) h w -> g t p q (h w)", q=2, p=P)

            def z_part(g, h):
                n = 2 if isinstance(g, int) and g == 0 else NT // 2
                return n * h, n * h + n

            def pairs(eng, step, first):
                first()
                step(0, 0, None)
                step(1, 1, 0)
                with eng.Fori(1, PAIRS // 2) as d:
                    step(2 * d, 0, 2 * d - 1)
                    step(2 * d + 1, 1, 2 * d)
                step(None, PAIRS % 2, PAIRS - 1)

            with nc.Block() as block:
                @block.sync
                def _(sp):
                    def load_x(g, par, t):
                        sp.dma_start(x3[:, par, t].rearrange("p (q c) -> p q c", q=2), x2_g[g, t]).then_inc(s_x3[par], 16)

                    for t in range(NT):
                        load_x(0, 0, t)
                    sp.dma_start(gst[:, :, :], a["gt"].rearrange("(t p) e -> p t e", p=P)).then_inc(s["c"], 16)
                    for h in range(2):
                        sp.dma_start(wst[:, 4 * h:4 * h + 4], a["wt"].rearrange("(t p) o -> p t o", p=P)[:, 4 * h:4 * h + 4]).then_inc(s_w[h], 16)
                    sp.wait_ge(s["init"], 2)
                    sp.dma_start(upt[0:41, :], a["up"]).then_inc(s["c"], 16)
                    sp.dma_start(upf[:, :], a["upf"]).then_inc(s["c"], 16)
                    sp.dma_start(gb[:, :], a["gb"]).then_inc(s["c"], 16)
                    sp.dma_start(iota[:, :], a["iota"]).then_inc(s["c"], 16)
                    for t in range(NT):
                        load_x(1, 1, t)

                    def step(g, par, pg, load):
                        for t in range(NT):
                            wait(sp, s["oadd"], 8 * pg + t + 1)
                            sp.dma_start(out_g[pg, t], ob[:, t % 4, :].rearrange("p (q c) -> p q c", q=2)).then_inc(s_out[t % 4], 16)
                            if load:
                                load_x(g + 1, 1 - par, t)

                    step(1, 1, 0, True)
                    with sp.Fori(1, PAIRS // 2 - 1) as d:
                        step(2 * d, 0, 2 * d - 1, True)
                        step(2 * d + 1, 1, 2 * d, True)
                    step(PAIRS - 2, 0, PAIRS - 3, True)
                    step(PAIRS - 1, 1, PAIRS - 2, False)
                    step(None, 0, PAIRS - 1, False)
                    for i in range(4):
                        sp.wait_ge(s_out[i], 16 * PAIRS * NT // 4)

                @block.gpsimd
                def _(pool):
                    nc.gpsimd.memset(upt[:, :], 0.0).then_inc(s["init"], 1)
                    nc.gpsimd.memset(hw[:, :, :], 0.0).then_inc(s["init"], 1)
                    pool.wait_ge(s["init"], 2)
                    nc.gpsimd.memset(hw[:, :, 40:41], 1.0).then_inc(s["init"], 1)

                    def step(g, par, pg):
                        def add(t):
                            wait(pool, s["oev"], 8 * pg + t + 1)
                            nc.gpsimd.tensor_tensor(ob[:, t % 4, :], ob[:, t % 4, :], x3[:, 1 - par, t, :], ALU.add).then_inc(s["oadd"], 1)
                        if pg is not None:
                            for t in range(4):
                                add(t)
                        if g is not None:
                            wait(pool, s["newt"], NEWTON * g + NEWTON)
                            wait(pool, s["sq"], g + 1)
                            for h in range(2):
                                lo, hi = z_part(g, h)
                                nc.gpsimd.tensor_tensor(zc[:, lo:hi], zc[:, lo:hi], ng3[:, :].unsqueeze(1).broadcast_to([P, hi - lo, TOK]),
                                                        ALU.mult).then_inc(s["z"], 1)
                        if pg is not None:
                            for t in range(4, NT):
                                add(t)

                    pairs(pool, step, lambda: None)

                @block.vector
                def _(dve):
                    def prepare():
                        links = [0]

                        def link(ins):
                            links[0] += 1
                            ins.then_inc(s["f"], 1)
                            dve.wait_ge(s["f"], links[0])

                        link(nc.vector.tensor_scalar(fc[:, 0:2], rp2[:, WB:GD + 1], W_UP, None, ALU.mult))
                        link(nc.vector.tensor_scalar(fc[:, 2:4], p2[:, WB:GD + 1], 1.0 / (W_UP * Z_UP), None, ALU.mult))
                        link(nc.vector.tensor_scalar(fc[:, 4:5], rp2[:, WB:WB + 1], W_UP * Z_UP, None, ALU.mult))
                        dve.wait_ge(s["c"], 16 * 5)
                        link(nc.vector.tensor_scalar(upf[:, :], upf[:, :], fc[0:64, 4:5], None, ALU.mult))
                        nc.vector.tensor_scalar(upt[:, :], upt[:, :], upf[:, 0:1], None, ALU.mult).then_inc(s["upl"], 1)

                    def w_low(lo, hi):
                        if lo == 0:
                            dve.wait_ge(s["gh"], 1)
                            nc.vector.scalar_tensor_tensor(gx[:, 1], gst[:, :, :], fc[:, 1:2], gx[:, 0], ALU.mult, ALU.subtract).then_inc(s["gl"], 1)
                        for t in range(lo, hi):
                            dve.wait_ge(s["wh"], t + 1)
                            nc.vector.scalar_tensor_tensor(wx[:, 1, t], wst[:, t], fc[:, 0:1], wx[:, 0, t], ALU.mult, ALU.subtract).then_inc(s["wl"], 1)

                    def step(g, par, pg):
                        peeled = isinstance(g, int) and g == 0
                        if g is not None:
                            dve.wait_ge(s_x3[par], 16 * NT * ((g - par) // 2) + 16 * NT if isinstance(g, int) else 8 * NT * (g - par) + 16 * NT)
                            wait(dve, s["mean"], g)
                            nc.vector.tensor_reduce(sums3[:, :], x3[:, par].rearrange("p t c -> p c t"), AX.X, ALU.add).then_inc(s["sum"], 1)
                        if pg is not None:
                            dve.wait_ge(s["gate"], pg + 1)
                            nc.vector.scalar_tensor_tensor(gl[:, :, 0:EXP], p_g[0:HC, :, 0:EXP], fc[0:HC, 3:4],
                                                           gb[:, 0:EXP].unsqueeze(1).broadcast_to([HC, TG, EXP]), ALU.mult, ALU.add).then_inc(s["glog"], 1)
                            dve.wait_ge(s["glog"], pg + 1)
                            nc.vector.tensor_scalar(gl[:, :, EXP:GC], p_g[0:HC, :, EXP:GC], fc[0:HC, 3:4], None, ALU.mult).then_inc(s["low"], 1)
                            for q in range(TG):
                                nc.vector.max(top[:, q], gl[:, q, 0:EXP]).then_inc(s["top"], 1)
                            wait(dve, s["ex2"], pg)
                            dve.wait_ge(s["top"], 4 * pg + 4)
                            nc.vector.tensor_tensor(dif[:, :], top[:, :, 1], top[:, :, 0], ALU.subtract).then_inc(s["dif"], 1)
                            for q in range(TG):
                                nc.vector.max_index(tix[:, q], top[:, q], gl[:, q, 0:EXP]).then_inc(s["tix"], 1)
                            dve.wait_ge(s["tix"], 4 * pg + 4)
                            nc.vector.tensor_copy(tixf[:, :, :], tix[:, :, 0:2]).then_inc(s["tixf"], 1)
                            dve.wait_ge(s["ex2"], pg + 1)
                            nc.vector.tensor_scalar(den2[:, :], ex2[:, :], 1.0, None, ALU.add).then_inc(s["den"], 1)
                            dve.wait_ge(s["den"], pg + 1)
                            nc.vector.reciprocal(wts[:, :, 0], den2[:, :]).then_inc(s["r"], 1)
                            dve.wait_ge(s["r"], pg + 1)
                            nc.vector.tensor_tensor(wts[:, :, 1], ex2[:, :], wts[:, :, 0], ALU.mult).then_inc(s["w2"], 1)
                            dve.wait_ge(s["tixf"], pg + 1)
                            nc.vector.tensor_tensor(eq[:, :, :], iota[:, :].unsqueeze(1).broadcast_to([HC, TG * 2, EXP]),
                                                    tixf[:, :, :].rearrange("p q c -> p (q c)").unsqueeze(2).broadcast_to([HC, TG * 2, EXP]),
                                                    ALU.is_equal).then_inc(s["eq"], 1)
                            dve.wait_ge(s["eq"], pg + 1)
                            dve.wait_ge(s["w2"], pg + 1)
                            nc.vector.tensor_tensor(eqw[:, :, :, :].rearrange("p q c e -> p (q c) e"), eq[:, :, :],
                                                    wts[:, :, :].rearrange("p q c -> p (q c)").unsqueeze(2).broadcast_to([HC, TG * 2, EXP]),
                                                    ALU.mult).then_inc(s["eqw"], 1)
                            dve.wait_ge(s["eqw"], pg + 1)
                            nc.vector.tensor_tensor(wgt[:, :, :], eqw[:, :, 0], eqw[:, :, 1], ALU.add).then_inc(s["wgt"], 1)
                            dve.wait_ge(s["low"], pg + 1)
                            dve.wait_ge(s["wgt"], pg + 1)
                            wait(dve, s["hwtr"], pg)
                            nc.vector.tensor_tensor(hw[:, :, 0:40].rearrange("p q (e r) -> p q e r", r=RANK),
                                                    gl[:, :, EXP:GC].rearrange("p q (e r) -> p q e r", r=RANK),
                                                    wgt[:, :, :].unsqueeze(3).broadcast_to([HC, TG, EXP, RANK]), ALU.mult).then_inc(s["hw"], 1)
                            dve.wait_ge(s["hwtr"], pg + 1)
                            wait(dve, s["o"], 8 * pg)
                            nc.vector.tensor_copy(hwt[:, :], p_h[0:64, 0:TOK]).then_inc(s["hwt"], 1)
                        if g is None:
                            return
                        dve.wait_ge(s["mean"], g + 1)
                        wait(dve, s["zl"], 2 * g)
                        wait(dve, s["zh"], 2 * g)
                        nc.vector.tensor_tensor(zc[:, :, :], x3[:, par], p_m[:, 0:TOK].unsqueeze(1).broadcast_to([P, NT, TOK]),
                                                ALU.subtract).then_inc(s["xc"], 1)
                        if peeled:
                            w_low(0, 3)
                        dve.wait_ge(s["sq"], g + 1)
                        wait(dve, s["var"], g)
                        nc.vector.tensor_reduce(sqs3[:, :], sq3[:, :, :].rearrange("p t c -> p c t"), AX.X, ALU.add).then_inc(s["sqs"], 1)
                        dve.wait_ge(s["var"], g + 1)
                        newton_rsqrt(dve, p_m[:, 0:TOK], 1.0, nv3[:, :], nb3[:, :], ng3[:, :], nh3[:, :], s["newt"], NEWTON * g, 1e-5)
                        if peeled:
                            nc.vector.tensor_tensor(zc[:, 4:NT], zc[:, 4:NT], ng3[:, :].unsqueeze(1).broadcast_to([P, NT - 4, TOK]),
                                                    ALU.mult).then_inc(s["z0"], 1)
                        for h in range(2):
                            dve.wait_ge(s["zh"], 2 * g + h + 1)
                            nc.vector.scalar_tensor_tensor(zx[:, par, 1, 4 * h:4 * h + 4], zc[:, 4 * h:4 * h + 4], Z_UP,
                                                           zx[:, par, 0, 4 * h:4 * h + 4], ALU.mult, ALU.subtract).then_inc(s["zl"], 1)
                        if peeled:
                            w_low(3, NT)

                    pairs(dve, step, prepare)

                @block.scalar
                def _(act):
                    def prepare():
                        act.wait_ge(s["f"], 1)
                        act.wait_ge(s["c"], 16 * 5)
                        nc.scalar.activation(gx[:, 0], gst[:, :, :], ACT.Copy, scale=fc[:, 1:2]).then_inc(s["gh"], 1)

                    def w_high(lo, hi):
                        for t in range(lo, hi):
                            act.wait_ge(s_w[t // 4], 16)
                            nc.scalar.activation(wx[:, 0, t], wst[:, t], ACT.Copy, scale=fc[:, 0:1]).then_inc(s["wh"], 1)

                    def step(g, par, pg):
                        peeled = isinstance(g, int) and g == 0

                        def evac(t):
                            wait(act, s["o"], 8 * pg + t + 1)
                            wait(act, s_out[t % 4], 32 * pg + 16 * (t // 4))
                            nc.scalar.activation(ob[:, t % 4, :], p_o[:, t % 4, 0:TOK], ACT.Copy, scale=fc[:, 2:3]).then_inc(s["oev"], 1)

                        def z_high(h):
                            act.wait_ge(s["z"], 2 * g + h + 1 if not peeled else 2)
                            if peeled:
                                act.wait_ge(s["z0"], 1)
                            wait(act, s["o"], 8 * (g - 1))
                            nc.scalar.activation(zx[:, par, 0, 4 * h:4 * h + 4], zc[:, 4 * h:4 * h + 4], ACT.Copy, scale=Z_UP).then_inc(s["zh"], 1)

                        if pg is not None:
                            act.wait_ge(s["dif"], pg + 1)
                            wait(act, s["w2"], pg)
                            nc.scalar.activation(ex2[:, :], dif[:, :], ACT.Exp).then_inc(s["ex2"], 1)
                        if peeled:
                            w_high(0, 3)
                        if g is not None:
                            act.wait_ge(s["xc"], g + 1)
                            wait(act, s["sqs"], g)
                            nc.scalar.activation(sq3[:, :, :], zc[:, :, :], ACT.Square).then_inc(s["sq"], 1)
                        if peeled:
                            w_high(3, NT)
                        if pg is not None:
                            for t in range(4):
                                evac(t)
                        if g is not None:
                            z_high(0)
                        if pg is not None:
                            evac(4)
                        if g is not None:
                            z_high(1)
                        if pg is not None:
                            for t in range(5, NT):
                                evac(t)

                    pairs(act, step, prepare)

                @block.tensor
                def _(pe):
                    def step(g, par, pg):
                        def gate():
                            pe.wait_ge(s["zl"], 2 * pg + 2)
                            for q in range(TG):
                                for c in range(NT):
                                    for w, m in ((0, 0), (0, 1), (1, 0)):
                                        last = nc.tensor.matmul(p_g[0:HC, q, 0:GC], zx[:, 1 - par, w, c, q * HC:(q + 1) * HC], gx[:, m, c],
                                                                start=(c == 0 and w == 0 and m == 0), stop=(c == NT - 1 and w == 1))
                            last.then_inc(s["gate"], 1)

                        def base(t):
                            wait(pe, s["oev"], 8 * pg + t - 3)
                            for c in range(NT):
                                for w, m in ((0, 0), (0, 1), (1, 0)):
                                    nc.tensor.matmul(p_o[:, t % 4, 0:TOK], wx[:, w, c, t * P:(t + 1) * P], zx[:, 1 - par, m, c],
                                                     start=(c == 0 and w == 0 and m == 0), stop=False)

                        def lora(t):
                            nc.tensor.matmul(p_o[:, t % 4, 0:TOK], upt[:, t * P:(t + 1) * P], hwt[:, :], start=False,
                                             stop=True).then_inc(s["o"], 1)

                        if pg is not None:
                            if isinstance(pg, int) and pg == 0:
                                pe.wait_ge(s["gl"], 1)
                            gate()
                            if isinstance(pg, int) and pg == 0:
                                pe.wait_ge(s["upl"], 1)
                                pe.wait_ge(s["wl"], NT)
                            base(0)
                        if g is not None:
                            pe.wait_ge(s["sum"], g + 1)
                            nc.tensor.matmul(p_m[:, 0:TOK], ones[:, :], sums3[:, :], start=True, stop=True).then_inc(s["mean"], 1)
                        if pg is not None:
                            base(1)
                            pe.wait_ge(s["hw"], pg + 1)
                            wait(pe, s["hwt"], pg)
                            for q in range(TG):
                                last = nc.tensor.transpose(p_h[:, q * HC:(q + 1) * HC], hw[:, q, :], ident[0:HC, 0:HC])
                            last.then_inc(s["hwtr"], 1)
                            base(2)
                            pe.wait_ge(s["hwt"], pg + 1)
                            for t in range(3):
                                lora(t)
                        if g is not None:
                            pe.wait_ge(s["sqs"], g + 1)
                            pe.wait_ge(s["xc"], g + 1)
                            nc.tensor.matmul(p_m[:, 0:TOK], ones[:, :], sqs3[:, :], start=True, stop=True).then_inc(s["var"], 1)
                        if pg is not None:
                            for t in range(3, NT):
                                base(t)
                                lora(t)

                    pe.wait_ge(s["init"], 3)
                    pairs(pe, step, lambda: None)


def kernel(**inputs):
    import numpy as np
    import concourse.bacc as _bacc
    from concourse import mybir as _mybir
    from concourse.bass_utils import run_bass_kernel_spmd as _run

    g = {k.replace("L0_conv_", "").replace("L0_ffn_", ""): np.asarray(v) for k, v in inputs.items()}
    f4 = g["x"].dtype
    W2t = g["W2"]
    sel_u3 = np.zeros((T, F, T), f4)
    for t in range(T):
        sel_u3[t, :, t] = g["U3"]
    lay = {
        "x": g["x"],
        "cheb": g["cheb"].reshape(K, NT, P, N).transpose(2, 0, 1, 3),
        "bs": g["bs"][0].reshape(NT, P, NT, P).transpose(2, 1, 0, 3),
        "vst": g["Vs"].T,
        "ua": np.concatenate([g["U2"].T, g["U1"][:, None], np.zeros((N, 1), f4)], 1),
        "sel_t": np.repeat(np.eye(T, dtype=f4), F, 0).reshape(2, HC, T).transpose(1, 0, 2),
        "sel_u3": sel_u3.reshape(2, HC, T).transpose(1, 0, 2),
        "sel_f": np.tile(np.eye(F, dtype=f4), (HT, 1)),
        "thr": np.tile(g["Theta"].transpose(1, 0, 2), (HT, 1, 1)),
        "w2r": np.tile(W2t, (HT, 4)),
        "w3r": np.tile(g["W3"][:, None], (HT, 1)),
        "iw": np.concatenate([np.eye(T, dtype=f4), g["W1"][:, None], np.zeros((T, 3), f4)], 1),
        "be": g["be"][0],
        "vet": g["Ve"].T,
        "ident": np.eye(P, dtype=f4),
        "lrm": np.array([1.0 if (r < 48 and r // 12 >= 2) or (64 <= r < 112 and (r - 64) // 12 % 2) else 0.0
                         for r in range(P)], f4)[:, None],
        "wt": g["W_base"].T,
        "gt": np.concatenate([g["gate_W"], g["lora_down"].reshape(EXP * RANK, N)], 0).T,
        "up": np.concatenate([g["lora_up"].transpose(0, 2, 1).reshape(EXP * RANK, N), g["b_base"][None]], 0),
        "upf": np.array([1.0 / RANK] * (EXP * RANK) + [1.0] + [0.0] * (63 - EXP * RANK), f4)[:, None],
        "gb": np.tile(g["gate_b"], (HC, 1)),
        "iota": np.tile(np.arange(EXP, dtype=f4), (HC, 1)),
    }
    nc = _bacc.Bacc("TRN2", target_bir_lowering=False, num_devices=1)
    arrays, aps = {}, {}
    for name, v in lay.items():
        v = np.ascontiguousarray(v)
        arrays["in_" + name] = v
        aps[name] = nc.dram_tensor("in_" + name, v.shape, _mybir.dt.from_np(v.dtype), kind="ExternalInput").ap()
    out = nc.dram_tensor("out_0", (B, N, T, F), _mybir.dt.from_np(np.dtype(f4)), kind="ExternalOutput").ap()
    metaformer_program(nc, aps, out)
    r = _run(nc, [arrays], core_ids=[0])
    return r.results[0]["out_0"]
```

```python
import concourse.bass as bass
from concourse import mybir
from contextlib import ExitStack

B, N, T, F, K = 16, 1024, 12, 16, 3
P = 128
NT = N // P
C = T * F
HC = C // 2
HT = T // 2
KC = K * C
EXP, RANK = 10, 4
GC = EXP + EXP * RANK
GP = 64
PAIRS = B // 2
TOK = 2 * C
TG = TOK // HC

X_UP, K_UP = 256.0, 256.0
Y_UP = 32.0
V_UP, SIG_UP = 4096.0, 16384.0
CH_UP = 8192.0
W_UP, Z_UP = 4096.0, 256.0


def metaformer_program(nc, a, out):
    f32, f16, i32, u32 = mybir.dt.float32, mybir.dt.float16, mybir.dt.int32, mybir.dt.uint32
    ALU, ACT, AX = mybir.AluOpType, mybir.ActivationFunctionType, mybir.AxisListType
    ABSMAX = bass.bass_isa.ReduceOp.absmax

    def wait(eng, sem, value):
        if not (isinstance(value, int) and value <= 0):
            eng.wait_ge(sem, value)

    y_d = nc.dram_tensor("y_scratch", (B, P, NT, 2, KC), f16).ap()
    lr_d = nc.dram_tensor("lr_scratch", (B, 48, 2, N), f16).ap()
    x2_d = nc.dram_tensor("x2_scratch", (B, N, C), f32).ap()
    x_b = a["x"].rearrange("b (t p) h w -> b p t (h w)", p=P)
    x2_b = x2_d.rearrange("b (t p) c -> b p t c", p=P)
    out_b = out.rearrange("b (t p) h w -> b p t (h w)", p=P)

    root = ExitStack()
    with root:
        def make(stack):
            def sb(name, shape, dt=f32):
                return stack.enter_context(nc.sbuf_tensor(name, shape, dt))

            def ps(name, shape, dt=f32):
                return stack.enter_context(nc.psum_tensor(name, shape, dt))

            def sem(name):
                return stack.enter_context(nc.semaphore(name))
            return sb, ps, sem

        def newton_rsqrt(dve, var, scale, v, bits, guess, half, chain, base, eps, after=0, work=None):
            k, n = [base], [0]

            def link(ins):
                k[0] = k[0] + 1
                ins.then_inc(chain, 1)
                dve.wait_ge(chain, k[0])
                n[0] = n[0] + 1
                if work and n[0] == after:
                    work()

            link(nc.vector.tensor_scalar(v, var, scale, eps, ALU.mult, ALU.add))
            link(nc.vector.tensor_scalar(bits.bitcast(u32), v.bitcast(u32), 1, None, ALU.logical_shift_right))
            link(nc.vector.tensor_scalar(guess.bitcast(i32), bits.bitcast(i32), -1.0, 1597463007.0, ALU.mult, ALU.add))
            for _ in range(3):
                link(nc.vector.scalar_tensor_tensor(half, guess, -0.5, guess, ALU.mult, ALU.mult))
                link(nc.vector.tensor_tensor(half, half, v, ALU.mult))
                link(nc.vector.scalar_tensor_tensor(guess, half, 1.5, guess, ALU.add, ALU.mult))

        NEWTON = 12

        rsb, rps, rsem = make(root)
        ones = rsb("ones_over_n", [P, P])
        ident = rsb("ident", [P, P])
        p2 = rsb("p2", [P, 8])
        rp2 = rsb("rp2", [P, 8])
        fac = rsb("fac", [P, 8])
        s_rootc = rsem("s_rootc")
        THETA, W1, W2, W3, VS, CHEB, WB, GD = range(8)

        mid = ExitStack()
        with mid:
            msb, mps, msem = make(mid)
            cheb = msb("cheb", [P, K, NT, N])
            vt = msb("vt_split", [P, 2, NT, N], f16)

            with ExitStack() as st:
                sb, ps, sem = make(st)
                amax = sb("amax", [P, 8])
                am_all = sb("am_all", [P, 8])
                vmax = sb("vmax", [P, NT])
                chmax = sb("chmax", [P, K, NT])
                wmax = sb("wmax", [P, 8])
                wstage = sb("wstage", [P, N])
                gstage = sb("gstage", [P, NT, GC])
                ua = sb("ua", [P, NT, 18])
                uas = sb("uas", [HC, 18])
                sel_t = sb("sel_t", [HC, 2, T])
                sel_u3 = sb("sel_u3", [HC, 2, T])
                sel_f = sb("sel_f", [HC, F])
                thr = sb("thr", [HC, K, F])
                w2r = sb("w2r", [HC, 48])
                w3r = sb("w3r", [HC, 1])
                iw = sb("iw", [T, 16])
                be = sb("be", [T, T])
                vet = sb("vet", [T, T])
                lrm = sb("lrm", [P, 1])
                xf = sb("xf", [P, 2, NT, C])
                xr = sb("xr", [HC, 2, N])
                junk = sb("junk", [HC, N], f16)
                turn = sb("turn", [HC, 2])
                nmean = sb("nmean", [HC, 2])
                ss = sb("ss", [HC, 2])
                nv = sb("nv", [HC, 2])
                nb = sb("nb", [HC, 2])
                ng = sb("ng", [HC, 2])
                nh = sb("nh", [HC, 2])
                rs = sb("rs", [HC, 2])
                nmr = sb("nmr", [HC, 2])
                qt = sb("qt", [HC, 2, 18])
                qs = sb("qs", [HC, 2, 18])
                dg = sb("dg", [HC, 2, F])
                rg = sb("rg", [F, 80])
                xt = sb("xt", [HC, 2, 2, 2, N], f16)
                zt = sb("zt", [T, T])
                tht = sb("tht", [T, T])
                sgt = sb("sgt", [T, 64])
                emx = sb("emx", [T, 1])
                eex = sb("eex", [T, T])
                esm = sb("esm", [T, 1])
                erc = sb("erc", [T, 1])
                et = sb("et", [T, T])
                etr = sb("etr", [T, 2, HT, F])
                er = sb("er", [HC, 2, 16])
                kf = sb("kf", [HC, 2, K, T, F])
                kx = sb("kx", [HC, 2, 2, 2, KC], f16)
                klf = sb("klf", [HC, 2, P])
                kl = sb("kl", [HC, 2, 2, 2, P], f16)
                mh = sb("mh", [112, 2, 512], f16)
                lrt = sb("lrt", [112, N], f16)
                yt = sb("yt", [P, 4, 2, KC], f16)

                p_y = ps("p_y", [P, 2, 2, 512])
                p_t = ps("p_t", [P, 2, 512])
                p_s = ps("p_s", [P, 512])
                p_e = ps("p_e", [P, 512])

                names = ("c uas uasc aA allA pA vs vmax aB allB pB cheb cheb1 w chmax wmax aC gd allC pC vh vl cp nmean sq newt rs nmr v q qt qs dg rg rgs "
                         "prod zt tanh sg el emx eex erc et etr erep er kf klf kh kl klh kll tr xth xtl lr lrh lrl lrst y yh yl").split()
                s = {n: sem("s1_" + n) for n in names}
                s_x = [sem(f"s1_x{i}") for i in range(2)]
                s_yst = [sem(f"s1_ystore{i}") for i in range(4)]

                def batch_steps(eng, step):
                    step(0, 0, None, 0)
                    step(1, 1, 0, 0)
                    with eng.Fori(1, B // 2 - 1) as d:
                        step(2 * d, 0, 2 * d - 1, d)
                        step(2 * d + 1, 1, 2 * d, d)
                    step(B - 2, 0, B - 3, B // 2 - 1)
                    step(B - 1, 1, B - 2, B // 2 - 1)
                    step(None, 0, B - 1, None)

                with nc.Block() as block:
                    @block.sync
                    def _(sp):
                        sp.dma_start(xf[:, 0], x_b[0]).then_inc(s_x[0], 16)
                        sp.dma_start(ua[:, :, :], a["ua"].rearrange("(t p) c -> p t c", p=P)).then_inc(s["c"], 16)
                        for dst, src in ((ident, "ident"), (lrm, "lrm"), (sel_t, "sel_t"), (sel_u3, "sel_u3"), (sel_f, "sel_f"),
                                         (thr, "thr"), (w2r, "w2r"), (w3r, "w3r"), (iw, "iw"), (be, "be"), (vet, "vet")):
                            d = dst[:, :, :] if len(dst.shape) == 3 else dst[:, :]
                            sp.dma_start(d, a[src]).then_inc(s["c"], 16)
                        sp.dma_start(xf[:, 1], x_b[1]).then_inc(s_x[1], 16)

                        def step(i, par, p, load):
                            if load:
                                sp.wait_ge(s["tr"], 4 * i + 4)
                                sp.dma_start(xf[:, par], x_b[i + 2]).then_inc(s_x[par], 16)
                            if p is not None:
                                for t in range(NT):
                                    sp.wait_ge(s["yl"], 8 * p + t + 1)
                                    sp.dma_start(y_d[p, :, t], yt[:, t % 4, :, :]).then_inc(s_yst[t % 4], 16)
                                    if t == 6:
                                        sp.wait_ge(s["lrl"], 2 * p + 2)
                                        for g in range(2):
                                            sp.dma_start(lr_d[p, :, g], lrt[64 * g:64 * g + 48, :]).then_inc(s["lrst"], 16)

                        step(0, 0, None, True)
                        step(1, 1, 0, True)
                        with sp.Fori(1, B // 2 - 1) as d:
                            step(2 * d, 0, 2 * d - 1, True)
                            step(2 * d + 1, 1, 2 * d, True)
                        step(B - 2, 0, B - 3, False)
                        step(B - 1, 1, B - 2, False)
                        step(None, 0, B - 1, False)
                        sp.wait_ge(s["lrst"], 32 * B)
                        for h in range(4):
                            sp.wait_ge(s_yst[h], 16 * B * NT // 4)

                    @block.gpsimd
                    def _(pool):
                        nc.gpsimd.memset(ones[:, :], 1.0 / N).then_inc(s_rootc, 1)
                        nc.gpsimd.memset(amax[:, :], 0.0).then_inc(s_rootc, 1)
                        nc.gpsimd.memset(klf[:, :, :], 0.0).then_inc(s_rootc, 1)
                        nc.gpsimd.memset(rg[:, :], 0.0).then_inc(s_rootc, 1)
                        nc.gpsimd.memset(sgt[:, :], 0.0).then_inc(s_rootc, 1)
                        pool.wait_ge(s["aA"], 4)
                        nc.gpsimd.partition_all_reduce(am_all[:, 0:4], amax[:, 0:4], P, ABSMAX).then_inc(s["allA"], 1)
                        pool.dma_start(cheb[:, 1], a["vst"].rearrange("(t p) n -> p t n", p=P)).then_inc(s["vs"], 16)
                        for k in (0, 2):
                            pool.dma_start(cheb[:, k], a["cheb"][:, k]).then_inc(s["cheb"], 16)
                        pool.dma_start(gstage[:, :, :], a["gt"].rearrange("(t p) e -> p t e", p=P)).then_inc(s["gd"], 16)
                        pool.dma_start(wstage[:, :], a["wt"][P:2 * P, :]).then_inc(s["w"], 16)

                        def x_low(i, par):
                            pool.wait_ge(s["xth"], 2 * i + 1)
                            nc.gpsimd.tensor_tensor(turn[:, :], rs[:, :], nmr[:, :], ALU.mult)
                            for h in range(2):
                                nc.gpsimd.tensor_scalar(xr[:, h, :], xr[:, h, :], rs[:, h:h + 1], nmr[:, h:h + 1],
                                                        ALU.mult, ALU.add).then_inc(s["v"], 1)
                                pool.wait_ge(s["v"], 2 * i + h + 1)
                                pool.wait_ge(s["xth"], 2 * i + 2)
                                nc.gpsimd.tensor_tensor(xt[:, par, 1, h], xr[:, h, :], xt[:, par, 0, h], ALU.subtract).then_inc(s["xtl"], 1)

                        x_low(0, 0)
                        pool.wait_ge(s["aB"], 1)
                        nc.gpsimd.partition_all_reduce(am_all[:, VS:VS + 1], amax[:, VS:VS + 1], P, ABSMAX).then_inc(s["allB"], 1)
                        x_low(1, 1)
                        pool.wait_ge(s["vl"], NT)
                        pool.dma_start(cheb[:, 1], a["cheb"][:, 1]).then_inc(s["cheb1"], 16)
                        with pool.Fori(1, B // 2 - 1) as d:
                            x_low(2 * d, 0)
                            x_low(2 * d + 1, 1)
                            pool.wait_ge(s["wmax"], d)
                            pool.dma_start(wstage[:, :], a["wt"].rearrange("(t p) o -> t p o", p=P)[d + 1]).then_inc(s["w"], 16)
                        x_low(B - 2, 0)
                        x_low(B - 1, 1)
                        pool.wait_ge(s["wmax"], NT - 1)
                        pool.dma_start(wstage[:, :], a["wt"][0:P, :]).then_inc(s["w"], 16)
                        pool.wait_ge(s["aC"], 3)
                        nc.gpsimd.partition_all_reduce(am_all[:, CHEB:8], amax[:, CHEB:8], P, ABSMAX).then_inc(s["allC"], 1)

                    @block.vector
                    def _(dve):
                        def linker(sem_):
                            count = [0]

                            def link(ins):
                                count[0] += 1
                                ins.then_inc(sem_, 1)
                                dve.wait_ge(sem_, count[0])
                            return link

                        def powers(link, lo, hi):
                            link(nc.vector.tensor_scalar(am_all[:, lo:hi], am_all[:, lo:hi], 1e-30, None, ALU.max))
                            link(nc.vector.tensor_scalar(p2[:, lo:hi].bitcast(u32), am_all[:, lo:hi].bitcast(u32), 0x7F800000,
                                                         None, ALU.bitwise_and))
                            link(nc.vector.reciprocal(rp2[:, lo:hi], p2[:, lo:hi]))

                        dve.wait_ge(s["c"], 16 * 12)
                        dve.wait_ge(s_rootc, 5)
                        nc.vector.tensor_reduce(amax[0:HC, THETA:THETA + 1], thr[:, :, :], AX.XY, ALU.max,
                                                apply_absolute_value=True).then_inc(s["aA"], 1)
                        nc.vector.tensor_copy(amax[0:T, W1:W1 + 1], iw[:, 12:13]).then_inc(s["aA"], 1)
                        nc.vector.tensor_reduce(amax[0:HC, W2:W2 + 1], w2r[:, :], AX.X, ALU.max,
                                                apply_absolute_value=True).then_inc(s["aA"], 1)
                        nc.vector.tensor_copy(amax[0:HC, W3:W3 + 1], w3r[:, :]).then_inc(s["aA"], 1)
                        dve.wait_ge(s["uas"], 1)
                        nc.vector.tensor_scalar(uas[:, :], p_s[0:HC, 0:18], float(N), None, ALU.mult).then_inc(s["uasc"], 1)
                        dve.wait_ge(s["allA"], 1)
                        link = linker(s["pA"])
                        powers(link, THETA, W3 + 1)
                        link(nc.vector.tensor_tensor(fac[:, 5:6], p2[:, W1:W1 + 1], p2[:, W2:W2 + 1], ALU.mult))
                        link(nc.vector.tensor_tensor(fac[:, 0:1], fac[:, 5:6], p2[:, W3:W3 + 1], ALU.mult))
                        link(nc.vector.tensor_scalar(lrm[:, :], lrm[:, :], 1.0 / (X_UP * K_UP), None, ALU.mult))
                        link(nc.vector.tensor_scalar(thr[:, :, :], thr[:, :, :], rp2[0:HC, THETA:THETA + 1], None, ALU.mult))
                        link(nc.vector.tensor_scalar(w2r[:, :], w2r[:, :], rp2[0:HC, W2:W2 + 1], None, ALU.mult))
                        link(nc.vector.tensor_scalar(w3r[:, :], w3r[:, :], rp2[0:HC, W3:W3 + 1], None, ALU.mult))
                        link(nc.vector.tensor_scalar(iw[:, 12:13], iw[:, 12:13], rp2[0:T, W1:W1 + 1], None, ALU.mult))

                        def lr_low(p, h):
                            if p is None:
                                return
                            dve.wait_ge(s["lrh"], 2 * p + h + 1)
                            wait(dve, s["lrst"], 32 * p)
                            nc.vector.scalar_tensor_tensor(lrt[:, 512 * h:512 * h + 512], p_t[0:112, h, :], 1.0 / (X_UP * K_UP),
                                                           mh[:, h, :], ALU.mult, ALU.subtract).then_inc(s["lrl"], 1)

                        def y_low(p, t):
                            if p is None:
                                return
                            dve.wait_ge(s["yh"], 8 * p + t + 1)
                            nc.vector.scalar_tensor_tensor(
                                yt[:, t % 4, 1, :].rearrange("p (h c) -> p h c", h=2), p_y[:, t % 2, :, 0:KC // 2],
                                Y_UP / (X_UP * K_UP), yt[:, t % 4, 0, :].rearrange("p (h c) -> p h c", h=2),
                                ALU.mult, ALU.subtract).then_inc(s["yl"], 1)

                        def cheb_max(k, d):
                            dve.wait_ge(s["cheb1"] if k == 1 else s["cheb"], 16 if k == 1 else 16 * (K - 1))
                            nc.vector.tensor_reduce(chmax[:, k, bass.ts(d, 1)], cheb[:, k, bass.ts(d, 1), :].rearrange("p a n -> p (a n)"),
                                                    AX.X, ALU.max, apply_absolute_value=True).then_inc(s["chmax"], 1)

                        def w_max(d):
                            dve.wait_ge(s["w"], 16 * NT if isinstance(d, int) and d == 0 else 16 * d)
                            nc.vector.tensor_reduce(wmax[:, bass.ts(d, 1)], wstage[:, :], AX.X, ALU.max,
                                                    apply_absolute_value=True).then_inc(s["wmax"], 1)

                        def vs_max(lo, hi):
                            for t in range(lo, hi):
                                if t == 0:
                                    dve.wait_ge(s["vs"], 16)
                                nc.vector.tensor_reduce(vmax[:, t:t + 1], cheb[:, 1, t, :], AX.X, ALU.max,
                                                        apply_absolute_value=True).then_inc(s["vmax"], 1)

                        def vs_scale():
                            dve.wait_ge(s["vmax"], NT)
                            nc.vector.tensor_reduce(amax[:, VS:VS + 1], vmax[:, :], AX.X, ALU.max).then_inc(s["aB"], 1)
                            dve.wait_ge(s["allB"], 1)
                            link = linker(s["pB"])
                            powers(link, VS, VS + 1)
                            link(nc.vector.tensor_scalar(fac[:, 1:2], p2[:, VS:VS + 1], 1.0 / (V_UP * SIG_UP), None, ALU.mult))
                            link(nc.vector.tensor_scalar(fac[:, 4:5], rp2[:, VS:VS + 1], V_UP, None, ALU.mult))

                        def v_low(t):
                            dve.wait_ge(s["vh"], t + 1)
                            nc.vector.scalar_tensor_tensor(vt[:, 1, t, :], cheb[:, 1, t, :], fac[:, 4:5], vt[:, 0, t, :],
                                                           ALU.mult, ALU.subtract).then_inc(s["vl"], 1)

                        def factors(p, pp, meanwhile):
                            dve.wait_ge(s["erep"], p + 1)
                            nc.vector.tensor_copy(er[:, :, :], p_e[0:HC, 64:96].rearrange("p (h u) -> p h u", h=2)).then_inc(s["er"], 1)
                            dve.wait_ge(s["er"], p + 1)
                            wait(dve, s["klh"], p)
                            wait(dve, s["kll"], p)
                            for h in range(2):
                                nc.vector.tensor_scalar(klf[:, h, 0:48], w2r[:, :], er[:, h, 12:13], None, ALU.mult).then_inc(s["klf"], 1)
                            nc.vector.tensor_scalar(klf[:, :, 64:112].rearrange("p h (g u) -> p h g u", g=4),
                                                    er[:, :, 0:12].unsqueeze(2).broadcast_to([HC, 2, 4, T]),
                                                    w3r[:, 0:1], None, ALU.mult).then_inc(s["klf"], 1)
                            wait(dve, s["kh"], p)
                            wait(dve, s["kl"], p)
                            for h in range(2):
                                nc.vector.tensor_tensor(kf[:, h], er[:, h, 0:12].unsqueeze(1).unsqueeze(3).broadcast_to([HC, K, T, F]),
                                                        thr[:, :, :].unsqueeze(2).broadcast_to([HC, K, T, F]), ALU.mult).then_inc(s["kf"], 1)
                            dve.wait_ge(s["klh"], p + 1)
                            nc.vector.scalar_tensor_tensor(kl[:, pp, 1], klf[:, :, :], K_UP, kl[:, pp, 0], ALU.mult,
                                                           ALU.subtract).then_inc(s["kll"], 1)
                            meanwhile()
                            dve.wait_ge(s["kh"], p + 1)
                            nc.vector.scalar_tensor_tensor(kx[:, pp, 1], kf[:, :, :, :, :].rearrange("p h k u o -> p h (k u o)"), K_UP,
                                                           kx[:, pp, 0], ALU.mult, ALU.subtract).then_inc(s["kl"], 1)

                        def step(i, par, p, d):
                            first = isinstance(i, int) and i == 0
                            second = isinstance(i, int) and i == 1
                            later = not first and not second and i is not None

                            def meanwhile():
                                if i is None or not (isinstance(i, int) and i < 2):
                                    y_low(p - 1, 6)
                                    y_low(p - 1, 7)
                                if i is not None:
                                    dve.wait_ge(s["q"], i + 1)
                                    wait(dve, s["sq"], 2 * i)
                                    nc.vector.tensor_scalar(nmean[:, :], p_s[0:HC, 0:P]
                                                            .rearrange("p (h c) -> p h c", h=2)[:, :, 17], -1.0 / N,
                                                            None, ALU.mult).then_inc(s["nmean"], 1)
                                if later:
                                    cheb_max(2 * par, d)

                            if p is not None:
                                factors(p, 1 - par, meanwhile)
                            else:
                                meanwhile()
                            if i is None:
                                lr_low(p, 0)
                                y_low(p, 0)
                                lr_low(p, 1)
                                y_low(p, 1)
                                w_max(0)
                                cheb_max(0, 0)
                                y_low(p, 2)
                                y_low(p, 3)
                                cheb_max(1, 0)
                                cheb_max(2, 0)
                                for t in range(4, NT):
                                    y_low(p, t)
                                return
                            dve.wait_ge(s["sq"], 2 * i + 2)
                            newton_rsqrt(dve, ss[:, :], 1.0 / N, nv[:, :], nb[:, :], ng[:, :], nh[:, :], s["newt"],
                                         NEWTON * i, 1e-6, 7, lambda: y_low(p, 0))
                            nc.vector.tensor_scalar(rs[:, :], ng[:, :], X_UP, None, ALU.mult).then_inc(s["rs"], 1)
                            dve.wait_ge(s["nmean"], i + 1)
                            for h in range(2):
                                nc.vector.scalar_tensor_tensor(qt[:, h, :], uas[:, :], nmean[:, h:h + 1], p_s[0:HC, 64 * h:64 * h + 18],
                                                               ALU.mult, ALU.add).then_inc(s["qt"], 1)
                            dve.wait_ge(s["rs"], i + 1)
                            nc.vector.tensor_tensor(nmr[:, :], nmean[:, :], rs[:, :], ALU.mult).then_inc(s["nmr"], 1)
                            dve.wait_ge(s["qt"], 2 * i + 2)
                            wait(dve, s["rg"], i)
                            nc.vector.tensor_tensor(qs[:, :, :], qt[:, :, :], ng[:, :].unsqueeze(2).broadcast_to([HC, 2, 18]),
                                                    ALU.mult).then_inc(s["qs"], 1)
                            dve.wait_ge(s["qs"], i + 1)
                            nc.vector.tensor_tensor(dg[:, :, :], sel_f[:, :].unsqueeze(1).broadcast_to([HC, 2, F]),
                                                    qs[:, :, 16:17].broadcast_to([HC, 2, F]), ALU.mult).then_inc(s["dg"], 1)
                            y_low(p, 1)
                            if first:
                                vs_max(0, 4)
                            dve.wait_ge(s["rg"], i + 1)
                            wait(dve, s["prod"], i)
                            nc.vector.tensor_copy(rg[:, 0:32].rearrange("p (a t) -> p a t", a=2)[:, :, 0:T],
                                                  p_e[0:F, 0:32].rearrange("p (a t) -> p a t", a=2)[:, :, 0:T]).then_inc(s["rgs"], 1)
                            y_low(p, 2)
                            if later and par == 0:
                                w_max(d)
                            elif later:
                                cheb_max(1, d)
                            dve.wait_ge(s["prod"], i + 1)
                            wait(dve, s["tanh"], i)
                            nc.vector.tensor_tensor(zt[:, :], p_e[0:T, 32:32 + T], be[:, :], ALU.add).then_inc(s["zt"], 1)
                            y_low(p, 3)
                            if first:
                                vs_max(4, NT)
                            dve.wait_ge(s["tanh"], i + 1)
                            wait(dve, s["el"], i)
                            nc.vector.tensor_scalar(sgt[:, 0:T], tht[:, :], 0.5, 0.5, ALU.mult, ALU.add).then_inc(s["sg"], 1)
                            y_low(p, 4)
                            dve.wait_ge(s["el"], i + 1)
                            wait(dve, s["eex"], i)
                            nc.vector.tensor_reduce(emx[:, :], p_e[0:T, 48:48 + T], AX.X, ALU.max, negate=True).then_inc(s["emx"], 1)
                            if first:
                                vs_scale()
                            dve.wait_ge(s["eex"], i + 1)
                            nc.vector.reciprocal(erc[:, :], esm[:, :]).then_inc(s["erc"], 1)
                            y_low(p, 5)
                            dve.wait_ge(s["erc"], i + 1)
                            nc.vector.tensor_scalar(et[:, :], eex[:, :], erc[:, 0:1], None, ALU.mult).then_inc(s["et"], 1)
                            lr_low(p, 0)
                            dve.wait_ge(s["et"], i + 1)
                            wait(dve, s["erep"], i)
                            nc.vector.tensor_copy(etr[:, :, :, :].rearrange("p h t f -> p (h t) f"),
                                                  et[:, :].unsqueeze(2).broadcast_to([T, T, F])).then_inc(s["etr"], 1)
                            lr_low(p, 1)
                            if second:
                                for t in range(NT):
                                    v_low(t)

                        batch_steps(dve, step)
                        dve.wait_ge(s["gd"], 16)
                        nc.vector.tensor_reduce(amax[:, GD:GD + 1], gstage[:, :, :], AX.XY, ALU.max, apply_absolute_value=True).then_inc(s["aC"], 1)
                        dve.wait_ge(s["chmax"], K * NT)
                        nc.vector.tensor_reduce(amax[:, CHEB:CHEB + 1], chmax[:, :, :], AX.XY, ALU.max).then_inc(s["aC"], 1)
                        dve.wait_ge(s["wmax"], 8)
                        nc.vector.tensor_reduce(amax[:, WB:WB + 1], wmax[:, :], AX.X, ALU.max).then_inc(s["aC"], 1)
                        dve.wait_ge(s["allC"], 1)
                        link = linker(s["pC"])
                        powers(link, CHEB, 8)
                        link(nc.vector.tensor_scalar(fac[:, 2:3], rp2[:, CHEB:CHEB + 1], CH_UP, None, ALU.mult))
                        link(nc.vector.scalar_tensor_tensor(fac[:, 3:4], p2[:, CHEB:CHEB + 1], 1.0 / (CH_UP * Y_UP),
                                                            p2[:, THETA:THETA + 1], ALU.mult, ALU.mult))

                    @block.scalar
                    def _(act):
                        def lr_high(p, h):
                            if p is None:
                                return
                            act.wait_ge(s["lr"], 2 * p + h + 1)
                            wait(act, s["lrl"], 2 * p + h - 1)
                            nc.scalar.activation(mh[:, h, :], p_t[0:112, h, :], ACT.Copy, scale=lrm[0:112, 0:1]).then_inc(s["lrh"], 1)

                        def y_high(p, t):
                            if p is None:
                                return
                            act.wait_ge(s["y"], 8 * p + t + 1)
                            wait(act, s_yst[t % 4], 32 * p + 16 * (t // 4))
                            nc.scalar.activation(yt[:, t % 4, 0, :].rearrange("p (h c) -> p h c", h=2),
                                                 p_y[:, t % 2, :, 0:KC // 2], ACT.Copy,
                                                 scale=Y_UP / (X_UP * K_UP)).then_inc(s["yh"], 1)

                        def x_high(par, h):
                            nc.scalar.activation(xt[:, par, 0, h], xr[:, h, :], ACT.Identity, scale=rs[:, h:h + 1],
                                                 bias=nmr[:, h:h + 1]).then_inc(s["xth"], 1)

                        def x_copy(i, r):
                            act.wait_ge(s["tr"], 4 * i + r + 1)
                            h, q = r // 2, r % 2
                            nc.scalar.activation(xr[:, h, 512 * q:512 * q + 512], p_t[0:HC, q, :],
                                                 ACT.Copy).then_inc(s["cp"], 1)

                        def kl_high(p, pp):
                            act.wait_ge(s["klf"], 3 * p + 3)
                            nc.scalar.activation(kl[:, pp, 0], klf[:, :, :], ACT.Copy, scale=K_UP).then_inc(s["klh"], 1)

                        def kx_high(p, pp):
                            act.wait_ge(s["kf"], 2 * p + 2)
                            nc.scalar.activation(kx[:, pp, 0], kf[:, :, :, :, :].rearrange("p h k u o -> p h (k u o)"), ACT.Copy,
                                                 scale=K_UP).then_inc(s["kh"], 1)

                        def step(i, par, p, d):
                            if i is None:
                                kl_high(p, 1 - par)
                                kx_high(p, 1 - par)
                                lr_high(p, 0)
                                y_high(p, 0)
                                lr_high(p, 1)
                                for t in range(1, NT):
                                    y_high(p, t)
                                return
                            wait(act, s["xtl"], 2 * i - 1)
                            x_copy(i, 0)
                            x_copy(i, 1)
                            if p is not None:
                                kl_high(p, 1 - par)
                            wait(act, s["xtl"], 2 * i)
                            x_copy(i, 2)
                            x_copy(i, 3)
                            if p is not None:
                                kx_high(p, 1 - par)
                            act.wait_ge(s["cp"], 4 * i + 4)
                            act.wait_ge(s["nmean"], i + 1)
                            for h in range(2):
                                wait(act, s["sq"], 2 * i + h)
                                nc.scalar.activation(junk[:, :], xr[:, h, :], ACT.Square, bias=nmean[:, h:h + 1],
                                                     accum_out=ss[:, h:h + 1]).then_inc(s["sq"], 1)
                            y_high(p, 0)
                            y_high(p, 1)
                            act.wait_ge(s["nmr"], i + 1)
                            wait(act, s["y"], 8 * (i - 1))
                            x_high(par, 0)
                            y_high(p, 2)
                            y_high(p, 3)
                            act.wait_ge(s["zt"], i + 1)
                            wait(act, s["sg"], i)
                            nc.scalar.activation(tht[:, :], zt[:, :], ACT.Tanh, scale=0.5).then_inc(s["tanh"], 1)
                            x_high(par, 1)
                            y_high(p, 4)
                            act.wait_ge(s["emx"], i + 1)
                            wait(act, s["et"], i)
                            nc.scalar.activation(eex[:, :], p_e[0:T, 48:48 + T], ACT.Exp, bias=emx[:, 0:1],
                                                 accum_out=esm[:, :]).then_inc(s["eex"], 1)
                            y_high(p, 5)
                            lr_high(p, 0)
                            y_high(p, 6)
                            lr_high(p, 1)
                            y_high(p, 7)
                            if isinstance(i, int) and i == 1:
                                act.wait_ge(s["pB"], 5)
                                for t in range(NT):
                                    nc.scalar.activation(vt[:, 0, t, :], cheb[:, 1, t, :], ACT.Copy, scale=fac[:, 4:5]).then_inc(s["vh"], 1)

                        act.wait_ge(s["pA"], 10)
                        batch_steps(act, step)

                    @block.tensor
                    def _(pe):
                        def lr(p, pp, h):
                            n = 0
                            for half in range(2):
                                for w, m in ((0, 0), (0, 1), (1, 0)):
                                    last = nc.tensor.matmul(p_t[:, h, :], kl[:, pp, w, half, :], xt[:, pp, m, half, 512 * h:512 * h + 512],
                                                            start=(n == 0), stop=(n == 5))
                                    n += 1
                            last.then_inc(s["lr"], 1)

                        def y(p, pp, t):
                            if p is None:
                                return
                            wait(pe, s["yl"], 8 * p + t - 1)
                            n = 0
                            for half in range(2):
                                for w, m in ((0, 0), (0, 1), (1, 0)):
                                    for c in range(2):
                                        last = nc.tensor.matmul(p_y[:, t % 2, c, 0:KC // 2], xt[:, pp, w, half, t * P:(t + 1) * P],
                                                                kx[:, pp, m, half, c * (KC // 2):(c + 1) * (KC // 2)],
                                                                start=(n == 0), stop=(n == 5))
                                    n += 1
                            last.then_inc(s["y"], 1)

                        def transposes(i, par, r):
                            if r >= 2:
                                pe.wait_ge(s["cp"], 4 * i + r - 1)
                            h, q = r // 2, r % 2
                            for t in range(4):
                                last = nc.tensor.transpose(p_t[0:HC, q, t * P:(t + 1) * P],
                                                           xf[:, par, 4 * q + t, h * HC:(h + 1) * HC], ident[:, :])
                            last.then_inc(s["tr"], 1)

                        def replicate(i):
                            pe.wait_ge(s["etr"], i + 1)
                            wait(pe, s["er"], i)
                            for h in range(2):
                                last = nc.tensor.matmul(p_e[0:HC, 64 + 16 * h:64 + 16 * h + 16],
                                                        etr[:, h].rearrange("p t f -> p (t f)"), iw[:, :], start=True, stop=True)
                            last.then_inc(s["erep"], 1)

                        def u_products(n, par, h):
                            if n is None:
                                return
                            for t in range(NT):
                                last = nc.tensor.matmul(p_s[0:HC, 64 * h:64 * h + 18], xf[:, par, t, h * HC:(h + 1) * HC],
                                                        ua[:, t, :], start=(t == 0), stop=(t == NT - 1))
                            if h == 1:
                                last.then_inc(s["q"], 1)

                        def step(i, par, p, d):
                            pp = 1 - par
                            following = None if i is None or (isinstance(i, int) and i == B - 1) else i + 1
                            if i is not None:
                                if p is not None:
                                    wait(pe, s["lrl"], 2 * p)
                                transposes(i, par, 0)
                                transposes(i, par, 1)
                                u_products(i, par, 1)
                                transposes(i, par, 2)
                                transposes(i, par, 3)
                            if p is not None:
                                pe.wait_ge(s["kll"], p + 1)
                                pe.wait_ge(s["xtl"], 2 * p + 2)
                                if i is not None:
                                    pe.wait_ge(s["cp"], 4 * i + 3)
                                lr(p, pp, 0)
                                if i is not None:
                                    pe.wait_ge(s["cp"], 4 * i + 4)
                                lr(p, pp, 1)
                            if p is not None:
                                pe.wait_ge(s["kl"], p + 1)
                            for t in range(3):
                                y(p, pp, t)
                            if i is not None:
                                pe.wait_ge(s["dg"], i + 1)
                                wait(pe, s["er"], i)
                                for h in range(2):
                                    nc.tensor.matmul(p_e[0:F, 0:T], qs[:, h, 0:F], sel_u3[:, h, :], start=(h == 0), stop=(h == 1))
                                for h in range(2):
                                    last = nc.tensor.matmul(p_e[0:F, 16:16 + T], dg[:, h, :], sel_t[:, h, :], start=(h == 0), stop=(h == 1))
                                last.then_inc(s["rg"], 1)
                            y(p, pp, 3)
                            if following is not None:
                                pe.wait_ge(s_x[pp], 16 * (d + par) + 16)
                                pe.wait_ge(s["qt"], 2 * i + 2)
                            u_products(following, pp, 0)
                            if i is not None:
                                pe.wait_ge(s["rgs"], i + 1)
                                nc.tensor.matmul(p_e[0:64, 32:32 + T], rg[:, 16:80], rg[:, 0:T], start=True, stop=True).then_inc(s["prod"], 1)
                            y(p, pp, 4)
                            if i is not None:
                                pe.wait_ge(s["sg"], i + 1)
                                nc.tensor.matmul(p_e[0:64, 48:48 + T], sgt[:, :], vet[:, :], start=True, stop=True).then_inc(s["el"], 1)
                            for t in range(5, NT):
                                y(p, pp, t)
                            if i is not None:
                                replicate(i)

                        pe.wait_ge(s_rootc, 5)
                        pe.wait_ge(s["c"], 16 * 12)
                        for t in range(NT):
                            last = nc.tensor.matmul(p_s[0:HC, 0:18], ones[:, 0:HC], ua[:, t, :], start=(t == 0), stop=(t == NT - 1))
                        last.then_inc(s["uas"], 1)
                        pe.wait_ge(s["uasc"], 1)
                        pe.wait_ge(s["pA"], 10)
                        pe.wait_ge(s_x[0], 16)
                        u_products(0, 0, 0)
                        batch_steps(pe, step)


            with ExitStack() as st:
                sb, ps, sem = make(st)
                bst = sb("bs_tile", [P, 2, NT, P])
                lr = sb("lr", [P, 2, N], f16)
                z = sb("z", [P, NT, P])
                sig = sb("sig", [P, 2, 2, NT, P], f16)
                et2 = sb("e_t", [P, N])
                mx = sb("mx", [P, 2])
                nmx = sb("nmx", [P, 2])
                den = sb("den", [P, 2])
                rden = sb("rden", [P, 2])
                oscale = sb("oscale", [P, 2])
                pk = sb("p_k", [P, K, NT, P])
                pkx = sb("p_split", [P, 2, K, NT, P], f16)
                yx = sb("y_split", [P, NT, 2, KC], f16)
                conv = sb("conv", [P, 2, C])
                xres = sb("x_res", [P, 2, C])
                x2t = sb("x2_tile", [P, 2, C])

                p_a = ps("p_a", [P, 2, 512])
                p_b = ps("p_b", [P, 2 * 512])
                p_c = ps("p_c", [P, NT, P])
                p_d = ps("p_d", [P, 2, 512])

                s_prod = sem("s2_prod")
                s_z = sem("s2_z")
                s_tanh = sem("s2_tanh")
                s_sig = sem("s2_sig")
                s_sigh = sem("s2_sigh")
                s_sigl = sem("s2_sigl")
                s_logit = sem("s2_logit")
                s_max = sem("s2_max")
                s_nmax = sem("s2_nmax")
                s_exp = sem("s2_exp")
                s_rden = sem("s2_rden")
                s_osc = sem("s2_osc")
                s_tr = sem("s2_tr")
                s_pk = sem("s2_pk")
                s_pkh = sem("s2_pkh")
                s_pkl = sem("s2_pkl")
                s_conv = sem("s2_conv")
                s_relu = sem("s2_relu")
                s_x2 = sem("s2_x2")
                s_lrpad = sem("s2_lrpad")
                s_lr = sem("s2_lr")
                s_y = [sem(f"s2_y{t}") for t in range(NT)]
                s_bs = [sem(f"s2_bs{i}") for i in range(2)]
                s_xres = [sem(f"s2_xres{i}") for i in range(2)]
                s_st = [sem(f"s2_store{i}") for i in range(2)]

                def batches(eng, slot, first_slot):
                    first_slot()
                    for j in range(NT):
                        slot(0, j, j == 0, False)
                    with eng.Fori(1, B - 1) as b:
                        for j in range(NT):
                            slot(b, j, False, False)
                    for j in range(NT):
                        slot(B - 1, j, False, j == NT - 1)

                with nc.Block() as block:
                    @block.sync
                    def _(sp):
                        def load_lr(b):
                            sp.dma_start(lr[0:48, :, :], lr_d[b]).then_inc(s_lr, 16)

                        def load_bs(j):
                            sp.dma_start(bst[:, j % 2], a["bs"][j % NT]).then_inc(s_bs[j % 2], 16)

                        def store(b, j):
                            wait(sp, s_x2, 8 * b + j + 1)
                            sp.dma_start(x2_b[b, :, j], x2t[:, j % 2]).then_inc(s_st[j % 2], 16)

                        def begin():
                            load_bs(0)
                            sp.wait_ge(s_lrpad, 1)
                            load_lr(0)
                            load_bs(1)

                        def slot(b, j, first, last):
                            more = not (isinstance(b, int) and b == B - 1 and j + 2 >= NT)
                            if more:
                                wait(sp, s_z, 16 * b + 2 * j + 2)
                                load_bs(j + 2)
                            if not (isinstance(b, int) and b == 0 and j < 2):
                                if j >= 2:
                                    store(b, j - 2)
                                else:
                                    store(b - 1, j + 6)
                            sp.dma_start(xres[:, j % 2], x_b[b, :, j]).then_inc(s_xres[j % 2], 16)
                            if j == 1:
                                wait(sp, s_conv, 8 * b)
                                for t in range(NT):
                                    sp.dma_start(yx[:, t], y_d[b, :, t]).then_inc(s_y[t], 16)
                            if j == NT - 2 and not (isinstance(b, int) and b == B - 1):
                                wait(sp, s_prod, 16 * b + 16)
                                load_lr(b + 1)

                        batches(sp, slot, begin)
                        store(B - 1, NT - 2)
                        store(B - 1, NT - 1)
                        for h in range(2):
                            sp.wait_ge(s_st[h], 16 * B * NT // 2)

                    @block.gpsimd
                    def _(pool):
                        def sig_low(b, j):
                            wait(pool, s_sigh, 8 * b + j + 1)
                            nc.gpsimd.tensor_tensor(sig[:, j % 2, 1], z[:, :, :], sig[:, j % 2, 0], ALU.subtract).then_inc(s_sigl, 1)

                        def add(b, j):
                            wait(pool, s_relu, 8 * b + j + 1)
                            wait(pool, s_xres[j % 2], 64 * b + 16 * (j // 2) + 16)
                            wait(pool, s_st[j % 2], 64 * b + 16 * (j // 2))
                            nc.gpsimd.tensor_tensor(x2t[:, j % 2], conv[:, j % 2], xres[:, j % 2], ALU.add).then_inc(s_x2, 1)

                        def slot(b, j, first, last):
                            if not last:
                                sig_low(b + (j + 1) // NT, (j + 1) % NT)
                            if not first:
                                add(b - (j == 0), (j - 1) % NT)

                        batches(pool, slot, lambda: sig_low(0, 0))
                        add(B - 1, NT - 1)

                    @block.vector
                    def _(dve):
                        def add_bs(b, j):
                            n = 8 * b + j
                            wait(dve, s_sigl, n)
                            wait(dve, s_bs[j % 2], 64 * b + 16 * (j // 2) + 16)
                            for h in range(2):
                                wait(dve, s_prod, 2 * n + h + 1)
                                nc.vector.scalar_tensor_tensor(
                                    z[:, 4 * h:4 * h + 4, :].rearrange("p t v -> p (t v)"), p_a[:, h, :], fac[:, 0:1],
                                    bst[:, j % 2, 4 * h:4 * h + 4, :].rearrange("p t v -> p (t v)"),
                                    ALU.mult, ALU.add).then_inc(s_z, 1)

                        def mask(b, j):
                            n = 8 * b + j
                            wait(dve, s_tr, n + 1)
                            for k in range(K):
                                wait(dve, s_pkl, 3 * n - 2 + k)
                                nc.vector.scalar_tensor_tensor(pk[:, k], cheb[:, k, :, j * P:(j + 1) * P], fac[:, 2:3],
                                                               p_c[:, :, :], ALU.mult, ALU.mult).then_inc(s_pk, 1)
                                if k:
                                    low(b, j, k - 1)
                            low(b, j, K - 1)

                        def low(b, j, k):
                            n = 8 * b + j
                            wait(dve, s_pkh, 3 * n + k + 1)
                            wait(dve, s_conv, n)
                            nc.vector.tensor_tensor(pkx[:, 1, k], pk[:, k], pkx[:, 0, k], ALU.subtract).then_inc(s_pkl, 1)

                        def row_max(b, j):
                            n = 8 * b + j
                            wait(dve, s_logit, n + 1)
                            wait(dve, s_nmax, n - 1)
                            nc.vector.tensor_reduce(mx[:, j % 2:j % 2 + 1], p_b[:, :], AX.X, ALU.max, negate=True).then_inc(s_max, 1)
                            wait(dve, s_max, n + 1)
                            wait(dve, s_exp, n - 1)
                            nc.vector.tensor_scalar(nmx[:, j % 2:j % 2 + 1], mx[:, j % 2:j % 2 + 1], fac[:, 1:2], None,
                                                    ALU.mult).then_inc(s_nmax, 1)

                        def row_scale(b, j):
                            n = 8 * b + j
                            wait(dve, s_exp, n + 1)
                            nc.vector.reciprocal(rden[:, j % 2:j % 2 + 1], den[:, j % 2:j % 2 + 1]).then_inc(s_rden, 1)
                            wait(dve, s_rden, n + 1)
                            wait(dve, s_relu, n - 1)
                            nc.vector.tensor_scalar(oscale[:, j % 2:j % 2 + 1], rden[:, j % 2:j % 2 + 1], fac[:, 3:4], None,
                                                    ALU.mult).then_inc(s_osc, 1)

                        def slot(b, j, first, last):
                            if not last:
                                add_bs(b + (j + 1) // NT, (j + 1) % NT)
                            if not first:
                                mask(b - (j == 0), (j - 1) % NT)
                            row_max(b, j)
                            row_scale(b, j)

                        nc.vector.memset(lr[:, :, :], 0.0).then_inc(s_lrpad, 1)
                        batches(dve, slot, lambda: add_bs(0, 0))
                        mask(B - 1, NT - 1)

                    @block.scalar
                    def _(act):
                        def tanh(b, j):
                            n = 8 * b + j
                            wait(act, s_z, 2 * n + 2)
                            nc.scalar.activation(z[:, :, :], z[:, :, :], ACT.Tanh, scale=0.5).then_inc(s_tanh, 1)

                        def sig_high(b, j):
                            n = 8 * b + j
                            wait(act, s_tanh, n + 1)
                            nc.scalar.activation(z[:, :, :], z[:, :, :], ACT.Copy, scale=SIG_UP / 2, bias=SIG_UP / 2).then_inc(s_sig, 1)
                            wait(act, s_sig, n + 1)
                            wait(act, s_logit, n - 1)
                            nc.scalar.activation(sig[:, j % 2, 0], z[:, :, :], ACT.Copy).then_inc(s_sigh, 1)

                        def high(b, j, k):
                            n = 8 * b + j
                            wait(act, s_pk, 3 * n + k + 1)
                            wait(act, s_conv, n)
                            nc.scalar.activation(pkx[:, 0, k], pk[:, k], ACT.Copy).then_inc(s_pkh, 1)

                        def exp(b, j):
                            n = 8 * b + j
                            wait(act, s_nmax, n + 1)
                            wait(act, s_tr, n)
                            wait(act, s_rden, n - 1)
                            nc.scalar.activation(et2[:, :], p_b[:, :], ACT.Exp, bias=nmx[:, j % 2:j % 2 + 1], scale=fac[:, 1:2],
                                                 accum_out=den[:, j % 2:j % 2 + 1]).then_inc(s_exp, 1)

                        def relu(b, j):
                            n = 8 * b + j
                            wait(act, s_conv, n + 1)
                            wait(act, s_osc, n + 1)
                            wait(act, s_x2, n - 1)
                            nc.scalar.activation(conv[:, j % 2], p_d[:, j % 2, 0:C], ACT.Relu,
                                                 scale=oscale[:, j % 2:j % 2 + 1]).then_inc(s_relu, 1)

                        def slot(b, j, first, last):
                            pb, pj = b - (j == 0), (j - 1) % NT
                            if not last:
                                tanh(b + (j + 1) // NT, (j + 1) % NT)
                            if not first:
                                high(pb, pj, 0)
                            if not last:
                                sig_high(b + (j + 1) // NT, (j + 1) % NT)
                            if not first:
                                high(pb, pj, 1)
                                high(pb, pj, 2)
                            exp(b, j)
                            if not first:
                                relu(pb, pj)

                        def begin():
                            tanh(0, 0)
                            sig_high(0, 0)

                        batches(act, slot, begin)
                        for k in range(K):
                            high(B - 1, NT - 1, k)
                        relu(B - 1, NT - 1)

                    @block.tensor
                    def _(pe):
                        def prod(b, j):
                            n = 8 * b + j
                            wait(pe, s_z, 2 * n)
                            if j == 0:
                                wait(pe, s_lr, 16 * b + 16)
                            for h in range(2):
                                for t in range(4):
                                    last = nc.tensor.matmul(p_a[:, h, t * P:(t + 1) * P], lr[:, 0, (4 * h + t) * P:(4 * h + t + 1) * P],
                                                            lr[:, 1, j * P:(j + 1) * P], start=True, stop=True)
                                last.then_inc(s_prod, 1)

                        def logits(b, j):
                            n = 8 * b + j
                            wait(pe, s_sigl, n + 1)
                            wait(pe, s_exp, n)
                            for t in range(NT):
                                for w, m in ((0, 0), (0, 1), (1, 0)):
                                    for c in range(2):
                                        last = nc.tensor.matmul(p_b[:, 512 * c:512 * c + 512], sig[:, j % 2, w, t],
                                                                vt[:, m, t, 512 * c:512 * c + 512],
                                                                start=(t == 0 and w == 0 and m == 0), stop=(t == NT - 1 and w == 1))
                            last.then_inc(s_logit, 1)

                        def transposes(b, j):
                            n = 8 * b + j
                            wait(pe, s_exp, n + 1)
                            wait(pe, s_pk, 3 * n)
                            for t in range(NT):
                                last = nc.tensor.transpose(p_c[:, t, :], et2[:, t * P:(t + 1) * P], ident[:, :])
                            last.then_inc(s_tr, 1)

                        def convolve(b, j, by_k=False):
                            n = 8 * b + j
                            if not by_k:
                                wait(pe, s_pkl, 3 * n + 3)
                            wait(pe, s_relu, n - 1)
                            order = [(t, k) for k in range(K) for t in range(NT)] if by_k else [(t, k) for t in range(NT) for k in range(K)]
                            for t, k in order:
                                if by_k and t == 0:
                                    wait(pe, s_pkl, 3 * n + k + 1)
                                if j == 0 and k == 0:
                                    wait(pe, s_y[t], 16 * b + 16)
                                for w, m in ((0, 0), (0, 1), (1, 0)):
                                    last = nc.tensor.matmul(p_d[:, j % 2, 0:C], pkx[:, w, k, t], yx[:, t, m, k * C:(k + 1) * C],
                                                            start=(t == 0 and k == 0 and w == 0 and m == 0),
                                                            stop=(t == NT - 1 and k == K - 1 and w == 1))
                            last.then_inc(s_conv, 1)

                        def slot(b, j, first, last):
                            pb, pj = b - (j == 0), (j - 1) % NT
                            if not last:
                                prod(b + (j + 1) // NT, (j + 1) % NT)
                            if not first:
                                transposes(pb, pj)
                            logits(b, j)
                            if not first:
                                convolve(pb, pj)

                        batches(pe, slot, lambda: prod(0, 0))
                        transposes(B - 1, NT - 1)
                        convolve(B - 1, NT - 1, by_k=True)

        with ExitStack() as st:
            sb, ps, sem = make(st)
            wst = sb("w_stage", [P, NT, N])
            gst = sb("g_stage", [P, NT, GC])
            wx = sb("w_split", [P, 2, NT, N], f16)
            gx = sb("g_split", [P, 2, NT, GC], f16)
            upt = sb("up", [64, N])
            upf = sb("up_factor", [64, 1])
            gb = sb("gate_bias", [HC, EXP])
            iota = sb("iota", [HC, EXP])
            fc = sb("fc", [P, 8])
            x3 = sb("x3", [P, 2, NT, TOK])
            zc = sb("zc", [P, NT, TOK])
            sq3 = sb("sq3", [P, NT, TOK])
            zx = sb("z_split", [P, 2, 2, NT, TOK], f16)
            sums3 = sb("sums3", [P, TOK])
            sqs3 = sb("sqs3", [P, TOK])
            nv3 = sb("nv3", [P, TOK])
            nb3 = sb("nb3", [P, TOK])
            ng3 = sb("ng3", [P, TOK])
            nh3 = sb("nh3", [P, TOK])
            gl = sb("gl", [HC, TG, GC])
            top = sb("top", [HC, TG, 8])
            tix = sb("tix", [HC, TG, 8], u32)
            tixf = sb("tixf", [HC, TG, 2])
            dif = sb("dif", [HC, TG])
            ex2 = sb("ex2", [HC, TG])
            den2 = sb("den2", [HC, TG])
            wts = sb("wts", [HC, TG, 2])
            eq = sb("eq", [HC, TG * 2, EXP])
            eqw = sb("eqw", [HC, TG, 2, EXP])
            wgt = sb("wgt", [HC, TG, EXP])
            hw = sb("hw", [HC, TG, P])
            hwt = sb("hwt", [64, TOK])
            ob = sb("ob", [P, 4, TOK])

            p_o = ps("p_o", [P, 4, 512])
            p_m = ps("p_m", [P, 512])
            p_g = ps("p_g", [P, TG, GP])
            p_h = ps("p_h", [P, 512])

            names = ("c f wh wl gh gl upl sum mean xc sq sqs var newt z zh zl gate glog top tix tixf dif ex2 den r w2 "
                     "low eq eqw wgt hw hwtr hwt o oev oadd init z0").split()
            s = {n: sem("s3_" + n) for n in names}
            s_w = [sem(f"s3_wload{i}") for i in range(2)]
            s_x3 = [sem(f"s3_x{i}") for i in range(2)]
            s_out = [sem(f"s3_out{i}") for i in range(4)]
            x2_g = x2_d.rearrange("(g q) (t p) c -> g t p q c", q=2, p=P)
            out_g = out.rearrange("(g q) (t p) h w -> g t p q (h w)", q=2, p=P)

            def z_part(g, h):
                n = 2 if isinstance(g, int) and g == 0 else NT // 2
                return n * h, n * h + n

            def pairs(eng, step):
                step(0, 0, None)
                step(1, 1, 0)
                with eng.Fori(1, PAIRS // 2) as d:
                    step(2 * d, 0, 2 * d - 1)
                    step(2 * d + 1, 1, 2 * d)
                step(None, 0, PAIRS - 1)

            with nc.Block() as block:
                @block.sync
                def _(sp):
                    def load_x(g, par, t):
                        sp.dma_start(x3[:, par, t].rearrange("p (q c) -> p q c", q=2), x2_g[g, t]).then_inc(s_x3[par], 16)

                    for t in range(NT):
                        load_x(0, 0, t)
                    sp.dma_start(gst[:, :, :], a["gt"].rearrange("(t p) e -> p t e", p=P)).then_inc(s["c"], 16)
                    sp.wait_ge(s["init"], 2)
                    sp.dma_start(upt[0:41, :], a["up"]).then_inc(s["c"], 16)
                    sp.dma_start(upf[:, :], a["upf"]).then_inc(s["c"], 16)
                    sp.dma_start(gb[:, :], a["gb"]).then_inc(s["c"], 16)
                    sp.dma_start(iota[:, :], a["iota"]).then_inc(s["c"], 16)
                    for h in range(2):
                        sp.dma_start(wst[:, 4 * h:4 * h + 4], a["wt"].rearrange("(t p) o -> p t o", p=P)[:, 4 * h:4 * h + 4]).then_inc(s_w[h], 16)
                    for t in range(NT):
                        load_x(1, 1, t)

                    def step(g, par, pg, load):
                        for t in range(NT):
                            wait(sp, s["oadd"], 8 * pg + t + 1)
                            sp.dma_start(out_g[pg, t], ob[:, t % 4, :].rearrange("p (q c) -> p q c", q=2)).then_inc(s_out[t % 4], 16)
                            if load:
                                load_x(g + 1, 1 - par, t)

                    step(1, 1, 0, True)
                    with sp.Fori(1, PAIRS // 2 - 1) as d:
                        step(2 * d, 0, 2 * d - 1, True)
                        step(2 * d + 1, 1, 2 * d, True)
                    step(PAIRS - 2, 0, PAIRS - 3, True)
                    step(PAIRS - 1, 1, PAIRS - 2, False)
                    step(None, 0, PAIRS - 1, False)
                    for i in range(4):
                        sp.wait_ge(s_out[i], 16 * PAIRS * NT // 4)

                @block.gpsimd
                def _(pool):
                    nc.gpsimd.memset(upt[:, :], 0.0).then_inc(s["init"], 1)
                    nc.gpsimd.memset(hw[:, :, :], 0.0).then_inc(s["init"], 1)
                    pool.wait_ge(s["init"], 2)
                    nc.gpsimd.memset(hw[:, :, 40:41], 1.0).then_inc(s["init"], 1)

                    def step(g, par, pg):
                        def add(t):
                            wait(pool, s["oev"], 8 * pg + t + 1)
                            nc.gpsimd.tensor_tensor(ob[:, t % 4, :], ob[:, t % 4, :], x3[:, 1 - par, t, :], ALU.add).then_inc(s["oadd"], 1)
                        if pg is not None:
                            for t in range(4):
                                add(t)
                        if g is not None:
                            wait(pool, s["newt"], NEWTON * g + NEWTON)
                            wait(pool, s["sq"], g + 1)
                            for h in range(2):
                                lo, hi = z_part(g, h)
                                nc.gpsimd.tensor_tensor(zc[:, lo:hi], zc[:, lo:hi], ng3[:, :].unsqueeze(1).broadcast_to([P, hi - lo, TOK]),
                                                        ALU.mult).then_inc(s["z"], 1)
                        if pg is not None:
                            for t in range(4, NT):
                                add(t)

                    pairs(pool, step)

                @block.vector
                def _(dve):
                    def prepare():
                        links = [0]

                        def link(ins):
                            links[0] += 1
                            ins.then_inc(s["f"], 1)
                            dve.wait_ge(s["f"], links[0])

                        link(nc.vector.tensor_scalar(fc[:, 0:2], rp2[:, WB:GD + 1], W_UP, None, ALU.mult))
                        link(nc.vector.tensor_scalar(fc[:, 2:4], p2[:, WB:GD + 1], 1.0 / (W_UP * Z_UP), None, ALU.mult))
                        link(nc.vector.tensor_scalar(fc[:, 4:5], rp2[:, WB:WB + 1], W_UP * Z_UP, None, ALU.mult))

                    def w_low(lo, hi):
                        if lo == 0:
                            dve.wait_ge(s["c"], 16 * 5)
                            nc.vector.tensor_scalar(upf[:, :], upf[:, :], fc[0:64, 4:5], None, ALU.mult).then_inc(s["f"], 1)
                            dve.wait_ge(s["f"], 4)
                            nc.vector.tensor_scalar(upt[:, :], upt[:, :], upf[:, 0:1], None, ALU.mult).then_inc(s["upl"], 1)
                            dve.wait_ge(s["gh"], 1)
                            nc.vector.scalar_tensor_tensor(gx[:, 1], gst[:, :, :], fc[:, 1:2], gx[:, 0], ALU.mult, ALU.subtract).then_inc(s["gl"], 1)
                        for t in range(lo, hi):
                            dve.wait_ge(s["wh"], t + 1)
                            nc.vector.scalar_tensor_tensor(wx[:, 1, t], wst[:, t], fc[:, 0:1], wx[:, 0, t], ALU.mult, ALU.subtract).then_inc(s["wl"], 1)

                    def step(g, par, pg):
                        peeled = isinstance(g, int) and g == 0
                        if g is not None:
                            dve.wait_ge(s_x3[par], 16 * NT * ((g - par) // 2) + 16 * NT if isinstance(g, int) else 8 * NT * (g - par) + 16 * NT)
                            wait(dve, s["mean"], g)
                            nc.vector.tensor_reduce(sums3[:, :], x3[:, par].rearrange("p t c -> p c t"), AX.X, ALU.add).then_inc(s["sum"], 1)
                        if pg is not None:
                            dve.wait_ge(s["gate"], pg + 1)
                            nc.vector.scalar_tensor_tensor(gl[:, :, 0:EXP], p_g[0:HC, :, 0:EXP], fc[0:HC, 3:4],
                                                           gb[:, 0:EXP].unsqueeze(1).broadcast_to([HC, TG, EXP]), ALU.mult, ALU.add).then_inc(s["glog"], 1)
                            dve.wait_ge(s["glog"], pg + 1)
                            nc.vector.tensor_scalar(gl[:, :, EXP:GC], p_g[0:HC, :, EXP:GC], fc[0:HC, 3:4], None, ALU.mult).then_inc(s["low"], 1)
                            for q in range(TG):
                                nc.vector.max(top[:, q], gl[:, q, 0:EXP]).then_inc(s["top"], 1)
                            wait(dve, s["ex2"], pg)
                            dve.wait_ge(s["top"], 4 * pg + 4)
                            nc.vector.tensor_tensor(dif[:, :], top[:, :, 1], top[:, :, 0], ALU.subtract).then_inc(s["dif"], 1)
                            for q in range(TG):
                                nc.vector.max_index(tix[:, q], top[:, q], gl[:, q, 0:EXP]).then_inc(s["tix"], 1)
                            dve.wait_ge(s["tix"], 4 * pg + 4)
                            nc.vector.tensor_copy(tixf[:, :, :], tix[:, :, 0:2]).then_inc(s["tixf"], 1)
                            dve.wait_ge(s["ex2"], pg + 1)
                            nc.vector.tensor_scalar(den2[:, :], ex2[:, :], 1.0, None, ALU.add).then_inc(s["den"], 1)
                            dve.wait_ge(s["den"], pg + 1)
                            nc.vector.reciprocal(wts[:, :, 0], den2[:, :]).then_inc(s["r"], 1)
                            dve.wait_ge(s["r"], pg + 1)
                            nc.vector.tensor_tensor(wts[:, :, 1], ex2[:, :], wts[:, :, 0], ALU.mult).then_inc(s["w2"], 1)
                            dve.wait_ge(s["tixf"], pg + 1)
                            nc.vector.tensor_tensor(eq[:, :, :], iota[:, :].unsqueeze(1).broadcast_to([HC, TG * 2, EXP]),
                                                    tixf[:, :, :].rearrange("p q c -> p (q c)").unsqueeze(2).broadcast_to([HC, TG * 2, EXP]),
                                                    ALU.is_equal).then_inc(s["eq"], 1)
                            dve.wait_ge(s["eq"], pg + 1)
                            dve.wait_ge(s["w2"], pg + 1)
                            nc.vector.tensor_tensor(eqw[:, :, :, :].rearrange("p q c e -> p (q c) e"), eq[:, :, :],
                                                    wts[:, :, :].rearrange("p q c -> p (q c)").unsqueeze(2).broadcast_to([HC, TG * 2, EXP]),
                                                    ALU.mult).then_inc(s["eqw"], 1)
                            dve.wait_ge(s["eqw"], pg + 1)
                            nc.vector.tensor_tensor(wgt[:, :, :], eqw[:, :, 0], eqw[:, :, 1], ALU.add).then_inc(s["wgt"], 1)
                            dve.wait_ge(s["low"], pg + 1)
                            dve.wait_ge(s["wgt"], pg + 1)
                            wait(dve, s["hwtr"], pg)
                            nc.vector.tensor_tensor(hw[:, :, 0:40].rearrange("p q (e r) -> p q e r", r=RANK),
                                                    gl[:, :, EXP:GC].rearrange("p q (e r) -> p q e r", r=RANK),
                                                    wgt[:, :, :].unsqueeze(3).broadcast_to([HC, TG, EXP, RANK]), ALU.mult).then_inc(s["hw"], 1)
                            dve.wait_ge(s["hwtr"], pg + 1)
                            wait(dve, s["o"], 8 * pg)
                            nc.vector.tensor_copy(hwt[:, :], p_h[0:64, 0:TOK]).then_inc(s["hwt"], 1)
                        if g is None:
                            return
                        dve.wait_ge(s["mean"], g + 1)
                        wait(dve, s["zl"], 2 * g)
                        wait(dve, s["zh"], 2 * g)
                        nc.vector.tensor_tensor(zc[:, :, :], x3[:, par], p_m[:, 0:TOK].unsqueeze(1).broadcast_to([P, NT, TOK]),
                                                ALU.subtract).then_inc(s["xc"], 1)
                        if peeled:
                            w_low(0, 3)
                        dve.wait_ge(s["sq"], g + 1)
                        wait(dve, s["var"], g)
                        nc.vector.tensor_reduce(sqs3[:, :], sq3[:, :, :].rearrange("p t c -> p c t"), AX.X, ALU.add).then_inc(s["sqs"], 1)
                        dve.wait_ge(s["var"], g + 1)
                        newton_rsqrt(dve, p_m[:, 0:TOK], 1.0, nv3[:, :], nb3[:, :], ng3[:, :], nh3[:, :], s["newt"], NEWTON * g, 1e-5)
                        if peeled:
                            nc.vector.tensor_tensor(zc[:, 4:NT], zc[:, 4:NT], ng3[:, :].unsqueeze(1).broadcast_to([P, NT - 4, TOK]),
                                                    ALU.mult).then_inc(s["z0"], 1)
                        for h in range(2):
                            dve.wait_ge(s["zh"], 2 * g + h + 1)
                            nc.vector.scalar_tensor_tensor(zx[:, par, 1, 4 * h:4 * h + 4], zc[:, 4 * h:4 * h + 4], Z_UP,
                                                           zx[:, par, 0, 4 * h:4 * h + 4], ALU.mult, ALU.subtract).then_inc(s["zl"], 1)
                        if peeled:
                            w_low(3, NT)

                    prepare()
                    pairs(dve, step)

                @block.scalar
                def _(act):
                    def prepare():
                        act.wait_ge(s["f"], 1)
                        act.wait_ge(s["c"], 16 * 5)
                        nc.scalar.activation(gx[:, 0], gst[:, :, :], ACT.Copy, scale=fc[:, 1:2]).then_inc(s["gh"], 1)

                    def w_high(lo, hi):
                        for t in range(lo, hi):
                            act.wait_ge(s_w[t // 4], 16)
                            nc.scalar.activation(wx[:, 0, t], wst[:, t], ACT.Copy, scale=fc[:, 0:1]).then_inc(s["wh"], 1)

                    def step(g, par, pg):
                        peeled = isinstance(g, int) and g == 0

                        def evac(t):
                            wait(act, s["o"], 8 * pg + t + 1)
                            wait(act, s_out[t % 4], 32 * pg + 16 * (t // 4))
                            nc.scalar.activation(ob[:, t % 4, :], p_o[:, t % 4, 0:TOK], ACT.Copy, scale=fc[:, 2:3]).then_inc(s["oev"], 1)

                        def z_high(h):
                            act.wait_ge(s["z"], 2 * g + h + 1 if not peeled else 2)
                            if peeled:
                                act.wait_ge(s["z0"], 1)
                            wait(act, s["o"], 8 * (g - 1))
                            nc.scalar.activation(zx[:, par, 0, 4 * h:4 * h + 4], zc[:, 4 * h:4 * h + 4], ACT.Copy, scale=Z_UP).then_inc(s["zh"], 1)

                        if pg is not None:
                            act.wait_ge(s["dif"], pg + 1)
                            wait(act, s["w2"], pg)
                            nc.scalar.activation(ex2[:, :], dif[:, :], ACT.Exp).then_inc(s["ex2"], 1)
                        if peeled:
                            w_high(0, 3)
                        if g is not None:
                            act.wait_ge(s["xc"], g + 1)
                            wait(act, s["sqs"], g)
                            nc.scalar.activation(sq3[:, :, :], zc[:, :, :], ACT.Square).then_inc(s["sq"], 1)
                        if peeled:
                            w_high(3, NT)
                        if pg is not None:
                            for t in range(4):
                                evac(t)
                        if g is not None:
                            z_high(0)
                        if pg is not None:
                            evac(4)
                        if g is not None:
                            z_high(1)
                        if pg is not None:
                            for t in range(5, NT):
                                evac(t)

                    prepare()
                    pairs(act, step)

                @block.tensor
                def _(pe):
                    def step(g, par, pg):
                        def gate():
                            pe.wait_ge(s["zl"], 2 * pg + 2)
                            for q in range(TG):
                                for c in range(NT):
                                    for w, m in ((0, 0), (0, 1), (1, 0)):
                                        last = nc.tensor.matmul(p_g[0:HC, q, 0:GC], zx[:, 1 - par, w, c, q * HC:(q + 1) * HC], gx[:, m, c],
                                                                start=(c == 0 and w == 0 and m == 0), stop=(c == NT - 1 and w == 1))
                            last.then_inc(s["gate"], 1)

                        def base(t):
                            wait(pe, s["oev"], 8 * pg + t - 3)
                            for c in range(NT):
                                for w, m in ((0, 0), (0, 1), (1, 0)):
                                    nc.tensor.matmul(p_o[:, t % 4, 0:TOK], wx[:, w, c, t * P:(t + 1) * P], zx[:, 1 - par, m, c],
                                                     start=(c == 0 and w == 0 and m == 0), stop=False)

                        def lora(t):
                            nc.tensor.matmul(p_o[:, t % 4, 0:TOK], upt[:, t * P:(t + 1) * P], hwt[:, :], start=False,
                                             stop=True).then_inc(s["o"], 1)

                        if pg is not None:
                            if isinstance(pg, int) and pg == 0:
                                pe.wait_ge(s["gl"], 1)
                            gate()
                            if isinstance(pg, int) and pg == 0:
                                pe.wait_ge(s["upl"], 1)
                                pe.wait_ge(s["wl"], NT)
                            base(0)
                        if g is not None:
                            pe.wait_ge(s["sum"], g + 1)
                            nc.tensor.matmul(p_m[:, 0:TOK], ones[:, :], sums3[:, :], start=True, stop=True).then_inc(s["mean"], 1)
                        if pg is not None:
                            base(1)
                            pe.wait_ge(s["hw"], pg + 1)
                            wait(pe, s["hwt"], pg)
                            for q in range(TG):
                                last = nc.tensor.transpose(p_h[:, q * HC:(q + 1) * HC], hw[:, q, :], ident[0:HC, 0:HC])
                            last.then_inc(s["hwtr"], 1)
                            base(2)
                            pe.wait_ge(s["hwt"], pg + 1)
                            for t in range(3):
                                lora(t)
                            base(3)
                        if g is not None:
                            pe.wait_ge(s["sqs"], g + 1)
                            pe.wait_ge(s["xc"], g + 1)
                            nc.tensor.matmul(p_m[:, 0:TOK], ones[:, :], sqs3[:, :], start=True, stop=True).then_inc(s["var"], 1)
                        if pg is not None:
                            lora(3)
                            for t in range(4, NT):
                                base(t)
                                lora(t)

                    pe.wait_ge(s["init"], 3)
                    pairs(pe, step)


def kernel(**inputs):
    import numpy as np
    import concourse.bacc as _bacc
    from concourse import mybir as _mybir
    from concourse.bass_utils import run_bass_kernel_spmd as _run

    g = {k.replace("L0_conv_", "").replace("L0_ffn_", ""): np.asarray(v) for k, v in inputs.items()}
    f4 = g["x"].dtype
    W2t = g["W2"]
    sel_u3 = np.zeros((T, F, T), f4)
    for t in range(T):
        sel_u3[t, :, t] = g["U3"]
    lay = {
        "x": g["x"],
        "cheb": g["cheb"].reshape(K, NT, P, N).transpose(2, 0, 1, 3),
        "bs": g["bs"][0].reshape(NT, P, NT, P).transpose(2, 1, 0, 3),
        "vst": g["Vs"].T,
        "ua": np.concatenate([g["U2"].T, g["U1"][:, None], np.ones((N, 1), f4)], 1),
        "sel_t": np.repeat(np.eye(T, dtype=f4), F, 0).reshape(2, HC, T).transpose(1, 0, 2),
        "sel_u3": sel_u3.reshape(2, HC, T).transpose(1, 0, 2),
        "sel_f": np.tile(np.eye(F, dtype=f4), (HT, 1)),
        "thr": np.tile(g["Theta"].transpose(1, 0, 2), (HT, 1, 1)),
        "w2r": np.tile(W2t, (HT, 4)),
        "w3r": np.tile(g["W3"][:, None], (HT, 1)),
        "iw": np.concatenate([np.eye(T, dtype=f4), g["W1"][:, None], np.zeros((T, 3), f4)], 1),
        "be": g["be"][0],
        "vet": g["Ve"].T,
        "ident": np.eye(P, dtype=f4),
        "lrm": np.array([1.0 if (r < 48 and r // 12 >= 2) or (64 <= r < 112 and (r - 64) // 12 % 2) else 0.0
                         for r in range(P)], f4)[:, None],
        "wt": g["W_base"].T,
        "gt": np.concatenate([g["gate_W"], g["lora_down"].reshape(EXP * RANK, N)], 0).T,
        "up": np.concatenate([g["lora_up"].transpose(0, 2, 1).reshape(EXP * RANK, N), g["b_base"][None]], 0),
        "upf": np.array([1.0 / RANK] * (EXP * RANK) + [1.0] + [0.0] * (63 - EXP * RANK), f4)[:, None],
        "gb": np.tile(g["gate_b"], (HC, 1)),
        "iota": np.tile(np.arange(EXP, dtype=f4), (HC, 1)),
    }
    nc = _bacc.Bacc("TRN2", target_bir_lowering=False, num_devices=1)
    arrays, aps = {}, {}
    for name, v in lay.items():
        v = np.ascontiguousarray(v)
        arrays["in_" + name] = v
        aps[name] = nc.dram_tensor("in_" + name, v.shape, _mybir.dt.from_np(v.dtype), kind="ExternalInput").ap()
    out = nc.dram_tensor("out_0", (B, N, T, F), _mybir.dt.from_np(np.dtype(f4)), kind="ExternalOutput").ap()
    metaformer_program(nc, aps, out)
    r = _run(nc, [arrays], core_ids=[0])
    return r.results[0]["out_0"]
```
